# Optimizing a Trainium2 kernel written in Bass

```python
import numpy as np
import jax
import jax.numpy as jnp

def _softmax(x, axis=-1):
    return jax.nn.softmax(x, axis=axis)

def _gelu(x):
    return jax.nn.gelu(x, approximate=True)

def _silu(x):
    return jax.nn.silu(x)

def _sigmoid(x):
    return jax.nn.sigmoid(x)

def _layernorm(x, axis=-1, eps=1e-05):
    m = jnp.mean(x, axis=axis, keepdims=True)
    v = jnp.var(x, axis=axis, keepdims=True)
    return (x - m) / jnp.sqrt(v + eps)

def _scatter_add(tgt, idx, src, axis=0):
    return tgt.at[idx].add(src)

def _segment_sum(src, seg, n):
    return jax.ops.segment_sum(src, seg, n)
kernel_name = 'mk_sandwich_d1_jaxref_r4_0585ee'

def setup_inputs(seed: int=0):
    np.random.seed(seed)
    _w = jnp.asarray

    def _L0_attn_setup():
        import jax, jax.numpy as jnp
        import numpy as np
        B, S, D, H = (4, 512, 256, 1024)
        EPS = 1e-12

        def _linear(x, W, b):
            return x @ W.T + b
        key = jax.random.key(seed)
        ks = jax.random.split(key, 14)
        s = lambda d: 1.0 / np.sqrt(d)
        return {'x': jax.random.normal(ks[0], (B, S, D), dtype=jnp.float32), 'Wq': jax.random.normal(ks[1], (D, D), dtype=jnp.float32) * s(D), 'bq': jax.random.normal(ks[2], (D,), dtype=jnp.float32) * 0.01, 'Wk': jax.random.normal(ks[3], (D, D), dtype=jnp.float32) * s(D), 'bk': jax.random.normal(ks[4], (D,), dtype=jnp.float32) * 0.01, 'Wv': jax.random.normal(ks[5], (D, D), dtype=jnp.float32) * s(D), 'bv': jax.random.normal(ks[6], (D,), dtype=jnp.float32) * 0.01, 'W1': jax.random.normal(ks[7], (D, D), dtype=jnp.float32) * s(D), 'b1': jax.random.normal(ks[8], (D,), dtype=jnp.float32) * 0.01, 'W2': jax.random.normal(ks[9], (H, D), dtype=jnp.float32) * s(D), 'b2': jax.random.normal(ks[10], (H,), dtype=jnp.float32) * 0.01, 'W3': jax.random.normal(ks[11], (D, H), dtype=jnp.float32) * s(H), 'b3': jax.random.normal(ks[12], (D,), dtype=jnp.float32) * 0.01}
    _L0_attn_in = _L0_attn_setup()

    def _L0_ffn_setup():
        import jax, jax.numpy as jnp
        import numpy as np
        D_MODEL = 256
        N_HEADS = 16
        N_EXPERTS = 8
        TOP_K = 2
        EXPERT_HIDDEN = D_MODEL * 4 // N_EXPERTS

        def layer_norm(x, g, b, eps=1e-05):
            mu = jnp.mean(x, axis=-1, keepdims=True)
            var = jnp.var(x, axis=-1, keepdims=True)
            return (x - mu) * jax.lax.rsqrt(var + eps) * g + b
        key = jax.random.key(seed)
        ks = jax.random.split(key, 12)
        s = 1.0 / np.sqrt(D_MODEL)
        return {'x': jax.random.normal(ks[0], (2, 512, D_MODEL), dtype=jnp.float32), 'Wq': jax.random.normal(ks[1], (D_MODEL, D_MODEL), dtype=jnp.float32) * s, 'Wk': jax.random.normal(ks[2], (D_MODEL, D_MODEL), dtype=jnp.float32) * s, 'Wv': jax.random.normal(ks[3], (D_MODEL, D_MODEL), dtype=jnp.float32) * s, 'Wo': jax.random.normal(ks[4], (D_MODEL, D_MODEL), dtype=jnp.float32) * s, 'g1': jnp.ones((D_MODEL,), jnp.float32), 'b1': jnp.zeros((D_MODEL,), jnp.float32), 'g2': jnp.ones((D_MODEL,), jnp.float32), 'b2': jnp.zeros((D_MODEL,), jnp.float32), 'Wg': jax.random.normal(ks[5], (D_MODEL, N_EXPERTS), dtype=jnp.float32) * s, 'W1': jax.random.normal(ks[6], (N_EXPERTS, D_MODEL, EXPERT_HIDDEN), dtype=jnp.float32) * s, 'W2': jax.random.normal(ks[7], (N_EXPERTS, EXPERT_HIDDEN, D_MODEL), dtype=jnp.float32) * (1.0 / np.sqrt(EXPERT_HIDDEN))}
    _L0_ffn_in = _L0_ffn_setup()
    _d = {'L0_attn_x': _L0_attn_in['x'], 'L0_attn_Wq': _L0_attn_in['Wq'], 'L0_attn_bq': _L0_attn_in['bq'], 'L0_attn_Wk': _L0_attn_in['Wk'], 'L0_attn_bk': _L0_attn_in['bk'], 'L0_attn_Wv': _L0_attn_in['Wv'], 'L0_attn_bv': _L0_attn_in['bv'], 'L0_attn_W1': _L0_attn_in['W1'], 'L0_attn_b1': _L0_attn_in['b1'], 'L0_attn_W2': _L0_attn_in['W2'], 'L0_attn_b2': _L0_attn_in['b2'], 'L0_attn_W3': _L0_attn_in['W3'], 'L0_attn_b3': _L0_attn_in['b3'], 'L0_ffn_Wq': _L0_ffn_in['Wq'], 'L0_ffn_Wk': _L0_ffn_in['Wk'], 'L0_ffn_Wv': _L0_ffn_in['Wv'], 'L0_ffn_Wo': _L0_ffn_in['Wo'], 'L0_ffn_g1': _L0_ffn_in['g1'], 'L0_ffn_b1': _L0_ffn_in['b1'], 'L0_ffn_g2': _L0_ffn_in['g2'], 'L0_ffn_b2': _L0_ffn_in['b2'], 'L0_ffn_Wg': _L0_ffn_in['Wg'], 'L0_ffn_W1': _L0_ffn_in['W1'], 'L0_ffn_W2': _L0_ffn_in['W2']}
    _x0 = _d['L0_attn_x']
    _d['L0_attn_x'] = jax.random.normal(jax.random.fold_in(jax.random.key(seed), 1), (4, 1024, 256), dtype=_x0.dtype)
    del _x0
    return _d

def reference(L0_attn_x, L0_attn_Wq, L0_attn_bq, L0_attn_Wk, L0_attn_bk, L0_attn_Wv, L0_attn_bv, L0_attn_W1, L0_attn_b1, L0_attn_W2, L0_attn_b2, L0_attn_W3, L0_attn_b3, L0_ffn_Wq, L0_ffn_Wk, L0_ffn_Wv, L0_ffn_Wo, L0_ffn_g1, L0_ffn_b1, L0_ffn_g2, L0_ffn_b2, L0_ffn_Wg, L0_ffn_W1, L0_ffn_W2):

    def _L0_attn_ref(x, Wq, bq, Wk, bk, Wv, bv, W1, b1, W2, b2, W3, b3):
        import jax, jax.numpy as jnp
        import numpy as np
        B, S, D, H = (4, 512, 256, 1024)
        EPS = 1e-12

        def _linear(x, W, b):
            return x @ W.T + b
        Q = _linear(x, Wq, bq)
        K = _linear(x, Wk, bk)
        V = _linear(x, Wv, bv)
        Q = Q / jnp.maximum(jnp.linalg.norm(Q, axis=2, keepdims=True), EPS)
        K = K / jnp.maximum(jnp.linalg.norm(K, axis=2, keepdims=True), EPS)
        sim = jnp.einsum('bqd,bkd->bqk', Q, K)
        attn = jax.nn.softmax(sim, axis=2)
        out = jnp.einsum('bqk,bkd->bqd', attn, V)
        h = jax.nn.relu(_linear(out, W1, b1))
        h = jax.nn.relu(_linear(h, W2, b2))
        return _linear(h, W3, b3)

    def _L0_ffn_ref(x, Wq, Wk, Wv, Wo, g1, b1, g2, b2, Wg, W1, W2):
        import jax, jax.numpy as jnp
        import numpy as np
        D_MODEL = 256
        N_HEADS = 16
        N_EXPERTS = 8
        TOP_K = 2
        EXPERT_HIDDEN = D_MODEL * 4 // N_EXPERTS

        def layer_norm(x, g, b, eps=1e-05):
            mu = jnp.mean(x, axis=-1, keepdims=True)
            var = jnp.var(x, axis=-1, keepdims=True)
            return (x - mu) * jax.lax.rsqrt(var + eps) * g + b
        B, S, D = x.shape
        H, dk = (N_HEADS, D // N_HEADS)
        xn = layer_norm(x, g1, b1)
        q = (xn @ Wq).reshape(B, S, H, dk).transpose(0, 2, 1, 3)
        k = (xn @ Wk).reshape(B, S, H, dk).transpose(0, 2, 1, 3)
        v = (xn @ Wv).reshape(B, S, H, dk).transpose(0, 2, 1, 3)
        scores = jnp.einsum('bhqd,bhkd->bhqk', q, k) / np.sqrt(dk)
        attn = jax.nn.softmax(scores, axis=-1)
        o = jnp.einsum('bhqk,bhkd->bhqd', attn, v)
        o = o.transpose(0, 2, 1, 3).reshape(B, S, D) @ Wo
        x = x + o
        xn2 = layer_norm(x, g2, b2)
        xf = xn2.reshape(B * S, D)
        gate = xf @ Wg
        topv, topi = jax.lax.top_k(gate, TOP_K)
        probs = jax.nn.softmax(topv, axis=-1)
        cw = jnp.sum(jax.nn.one_hot(topi, N_EXPERTS, dtype=xf.dtype) * probs[..., None], axis=1)
        h = jax.nn.relu(jnp.einsum('td,edh->teh', xf, W1))
        y = jnp.einsum('teh,ehd->ted', h, W2)
        moe = jnp.einsum('ted,te->td', y, cw).reshape(B, S, D)
        return x + moe
    x = L0_attn_x
    x = x + _layernorm(_L0_attn_ref(_layernorm(x, axis=-1), L0_attn_Wq, L0_attn_bq, L0_attn_Wk, L0_attn_bk, L0_attn_Wv, L0_attn_bv, L0_attn_W1, L0_attn_b1, L0_attn_W2, L0_attn_b2, L0_attn_W3, L0_attn_b3), axis=-1)
    x = x + _layernorm(_L0_ffn_ref(_layernorm(x, axis=-1), L0_ffn_Wq, L0_ffn_Wk, L0_ffn_Wv, L0_ffn_Wo, L0_ffn_g1, L0_ffn_b1, L0_ffn_g2, L0_ffn_b2, L0_ffn_Wg, L0_ffn_W1, L0_ffn_W2), axis=-1)
    return x

_drawn_inputs = setup_inputs


def setup_inputs(seed=0):
    import zlib

    import numpy as np

    out = dict(_drawn_inputs(seed))
    spreads = {'L0_ffn_g1': (1.0, 0.2),
     'L0_ffn_b1': (0.0, 0.1),
     'L0_ffn_g2': (1.0, 0.2),
     'L0_ffn_b2': (0.0, 0.1)}
    factors = {'L0_attn_bq': 31.812, 'L0_attn_bk': 64.0}
    for name, (base, spread) in spreads.items():
        noise = np.random.default_rng([zlib.crc32(name.encode()), seed]).standard_normal(out[name].shape)
        drawn = base * np.exp(spread * noise) if base else spread * noise
        out[name] = jnp.asarray(drawn.astype(out[name].dtype))
    for name, factor in factors.items():
        out[name] = (out[name] * factor).astype(out[name].dtype)
    return out
```

```python
from contextlib import ExitStack

import concourse.bass as bass
from concourse import mybir

ACT = mybir.ActivationFunctionType
ALU = mybir.AluOpType
AX = mybir.AxisListType
F32 = mybir.dt.float32
F32R = mybir.dt.float32r
BF16 = mybir.dt.bfloat16
U32 = mybir.dt.uint32

P = 128
B, S, D = 4, 1024, 256
HID = 1024
NH, DK = 16, 16
NE, EH = 8, 128
T = S // P
K = D // P
HALF = 512
C = S // HALF
TH = T // C
M2 = HID // P
LN_EPS = 1e-5
NORM_FLOOR = 1e-24
PARTS = 3
NPOS = 6
STACK = NPOS * DK
SHIFT_ROWS = 2
QUARTER = S // 4
HPI = 4
VW = 32
LAST_M = 9


class Signal:

    def __init__(self, ctx, nc, name, per, credit=0):
        self.sem, self.per, self.credit = nc.alloc_semaphore(name), per, credit

    def at(self, b, n, more=0):
        n += self.credit
        assert n > 0
        return b * self.per + more + n


def split_weights(nc, ident, mhalf, sources):
    with ExitStack() as ctx:
        stages = [ctx.enter_context(nc.sbuf_tensor(f"stage_{hi.name}", list(dram.shape), F32))
                  for dram, hi, lo in sources]
        loaded = [nc.alloc_semaphore(f"loaded_{hi.name}") for _, hi, _ in sources]
        hi_done = nc.alloc_semaphore(f"hi_done_from_{sources[0][1].name}")
        zeroed = nc.alloc_semaphore(f"ident_zeroed_{sources[0][1].name}")
        block = ctx.enter_context(nc.Block())

        @block.sync
        def _(sp):
            for (dram, hi, lo), stage, sem in zip(sources, stages, loaded):
                sp.dma_start(stage[:], dram).then_inc(sem, 16)

        @block.gpsimd
        def _(pool):
            if ident is not None:
                pool.memset(mhalf[:, :], -0.5)
                pool.memset(ident[:, :], 0.0).then_inc(zeroed, 1)
                pool.wait_ge(zeroed, 1)
                pool.affine_select(out=ident[:, :], in_=ident[:, :], compare_op=ALU.not_equal, fill=1.0,
                                   base=0, pattern=[[-1, P]], channel_multiplier=1)

        @block.scalar
        def _(act):
            for (dram, hi, lo), stage, sem in zip(sources, stages, loaded):
                act.wait_ge(sem, 16)
                act.activation(hi[:], stage[:], ACT.Copy).then_inc(hi_done, 1)

        @block.vector
        def _(dve):
            for n, ((dram, hi, lo), stage) in enumerate(zip(sources, stages)):
                dve.wait_ge(hi_done, n + 1)
                dve.tensor_tensor(lo[:], stage[:], hi[:].bitcast(F32), ALU.subtract)


class LayerNorm:

    def __init__(self, ctx, nc, name, mhalf):
        self.stats = ctx.enter_context(nc.sbuf_tensor(f"{name}_stats", [P, T, 6], F32))
        self.mean_var = ctx.enter_context(nc.sbuf_tensor(f"{name}_mean_var", [P, T, 2], F32))
        self.var_eps = ctx.enter_context(nc.sbuf_tensor(f"{name}_var_eps", [P, T], F32))
        self.rstd = ctx.enter_context(nc.sbuf_tensor(f"{name}_rstd", [P, T], F32))
        self.mhalf = mhalf
        self.stats_done = Signal(ctx, nc, f"{name}_stats_done", T)
        self.stats_seen = nc.alloc_semaphore(f"{name}_stats_seen")
        self.moments_done = Signal(ctx, nc, f"{name}_moments_done", T)
        self.eps_added = Signal(ctx, nc, f"{name}_eps_added", C)
        self.rstd_ready = Signal(ctx, nc, f"{name}_rstd_ready", C)

    def tile_stats(self, dve, b, t, src):
        dve.bn_stats(self.stats[:, t, :], src).then_inc(self.stats_done.sem, 1)

    def half_moments(self, dve, b, c):
        dve.wait_ge(self.stats_done.sem, self.stats_done.at(b, TH * c + TH))
        dve.sem_inc(self.stats_seen, 1)
        for t in range(TH * c, TH * c + TH):
            dve.bn_aggr(self.mean_var[:, t, :], self.stats[:, t, :]).then_inc(self.moments_done.sem, 1)
        dve.wait_ge(self.moments_done.sem, self.moments_done.at(b, TH * c + TH))
        dve.tensor_scalar(self.var_eps[:, TH * c:TH * c + TH], self.mean_var[:, TH * c:TH * c + TH, 1],
                          LN_EPS, None, ALU.add).then_inc(self.eps_added.sem, 1)

    def half_rstd(self, pool, b, c):
        pool.wait_ge(self.eps_added.sem, self.eps_added.at(b, c + 1))
        half = slice(TH * c, TH * c + TH)
        pool.tensor_tensor(self.rstd[:, half], self.var_eps[:, half], self.mhalf[:, 0:TH],
                           ALU.pow).then_inc(self.rstd_ready.sem, 1)

    def wait_rstd(self, eng, b, c):
        eng.wait_ge(self.rstd_ready.sem, self.rstd_ready.at(b, c + 1))

    def normalise(self, dve, t, dst, src):
        return dve.tensor_scalar(dst, src, self.mean_var[:, t, 0:1], self.rstd[:, t:t + 1],
                                 ALU.subtract, ALU.mult)


def three_products(pe, out, w, m, first, last):
    pe.matmul(out, w[0], m[0], start=first, stop=False)
    pe.matmul(out, w[0], m[1], start=False, stop=False)
    return pe.matmul(out, w[1], m[0], start=False, stop=last)


def cosine_block(nc, outer, ident, mhalf, x, x1, weights, b_qk, b_v, b_1, b_2, b_3):
    wqk, wv, w1, w2, w3 = weights
    with ExitStack() as ctx:
        def sb(name, shape, dt=F32):
            return ctx.enter_context(nc.sbuf_tensor(name, shape, dt))

        def signal(name, per, credit=0):
            return Signal(ctx, nc, name, per, credit)

        def pair(name, shape):
            return sb(f"{name}_hi", shape, F32R), sb(f"{name}_lo", shape, F32R)

        x_in = sb("x_in", [P, T, D])
        tok = sb("tok", [P, T, D])
        qk = sb("qk", [P, T, 2 * D])
        x_res = qk[:, 0:T // 2, :].rearrange("p t (u d) -> p (t u) d", u=2)
        xn = qk[:, T // 2:T, :].rearrange("p t (u d) -> p (t u) d", u=2)
        xT = pair("xT", [P, K, S])
        qT = pair("qT", [P, K, S])
        kT = pair("kT", [P, K, S])
        v = pair("v", [P, T, D + 2])
        wide = pair("wide", [P, M2, HALF])
        oT = pair("oT", [P, K, HALF])
        h1T = pair("h1T", [P, K, HALF])
        f32 = sb("f32", [P, 2, HALF])
        v32 = f32[:, :, :].rearrange("p n (u d) -> p n u d", u=2)
        bqk_row = sb("bqk_row", [P, 2 * D])
        bv_row = sb("bv_row", [P, 2, D])
        b3_row = sb("b3_row", [P, D])
        b1_col = sb("b1_col", [P, K])
        b2_col = sb("b2_col", [P, M2])
        squares = sb("squares", [P, 2, D])
        ssq = sb("ssq", [P, T, 2])
        ssq_floor = sb("ssq_floor", [P, T, 2])
        rnorm = sb("rnorm", [P, T, 2])
        rden = sb("rden", [P, T])
        banks = ctx.enter_context(nc.psum_tensor("banks", [P, 8, HALF], F32))
        X, Y = 0, 4

        ln_in = LayerNorm(ctx, nc, "ln_in", mhalf)
        ln_out = LayerNorm(ctx, nc, "ln_out", mhalf)
        consts = nc.alloc_semaphore("consts_loaded")
        ones_set = nc.alloc_semaphore("v_ones_set")
        x_loaded = [signal(f"x_loaded{c}", 16) for c in range(C)]
        xres_loaded = signal("xres_loaded", 16)
        x1_stored = [signal(f"x1_stored{c}", 16, 16) for c in range(C)]
        x_normed = signal("x_normed", T)
        xT_ready = signal("xT_ready", 2 * K)
        xT_hi = signal("xT_hi", 2 * K)
        xT_lo = signal("xT_lo", 2 * K)
        qk_ready = signal("qk_ready", T)
        qk_biased = signal("qk_biased", T)
        squared = signal("squared", 2 * T, 2)
        floored = signal("floored", C)
        rnorm_ready = signal("rnorm_ready", C)
        q_scaled = signal("q_scaled", T)
        v_ready = signal("v_ready", T // 2)
        v_biased = signal("v_biased", T // 2)
        v_hi = signal("v_hi", T // 2)
        v_lo = signal("v_lo", T // 2)
        qkT_ready = signal("qkT_ready", 4 * K)
        qkT_hi = signal("qkT_hi", 4 * K)
        qkT_lo = signal("qkT_lo", 4 * K)
        NF = 2 * (T + K + M2)
        tile_ready = signal("tile_ready", NF)
        f32_done = signal("f32_done", NF, NF)
        hi_done = signal("hi_done", NF)
        lo_done = signal("lo_done", NF, 2)
        o_ready = signal("o_ready", T)
        den_inverted = signal("den_inverted", T)
        o_done = signal("o_done", T)
        oT_ready = signal("oT_ready", 2 * K)
        oT_hi = signal("oT_hi", 2 * K)
        oT_lo = signal("oT_lo", 2 * K)
        h3_ready = signal("h3_ready", T)
        h3_biased = signal("h3_biased", T, T)
        h3_normed = signal("h3_normed", T)
        x1_done = signal("x1_done", T)
        CUT_P = [0, T]
        CUT_H1 = [2 * T, 2 * T + K + M2]
        CUT_H2 = [2 * T + K, 2 * T + 2 * K + M2]

        def bank_of(n):
            if n < 2 * T:
                return X + n % 4
            for c in range(C):
                if CUT_H1[c] <= n < CUT_H1[c] + K:
                    return Y + K + n - CUT_H1[c]
            return Y + (n - CUT_H2[0]) % 4 if n < CUT_H1[1] else X + (n - CUT_H2[1]) % 4

        xb = x.rearrange("b (t p) d -> b p t d", p=P)
        x1b = x1.rearrange("b (t p) d -> b p t d", p=P)
        block = ctx.enter_context(nc.Block())

        @block.sync
        def _(sp):
            for dst, src in ((bqk_row[:, 0:D], b_qk[0]), (bqk_row[:, D:2 * D], b_qk[1]), (bv_row[:, 0, :], b_v),
                             (bv_row[:, 1, :], b_v), (b3_row[:, :], b_3)):
                sp.dma_start(dst, src.to_broadcast([P, D])).then_inc(consts, 16)
            sp.dma_start(b1_col[:, :], b_1).then_inc(consts, 16)
            sp.dma_start(b2_col[:, :], b_2).then_inc(consts, 16)

            def load_x(b):
                for c in range(C):
                    sp.dma_start(x_in[:, TH * c:TH * c + TH, :], xb[b, :, TH * c:TH * c + TH, :])\
                        .then_inc(x_loaded[c].sem, 16)

            def batch(b, last):
                if not last:
                    sp.wait_ge(x_normed.sem, x_normed.at(b, T))
                    load_x(b + 1)
                sp.wait_ge(qkT_ready.sem, qkT_ready.at(b, 4 * K))
                sp.dma_start(x_res, xb[b]).then_inc(xres_loaded.sem, 16)
                for c in range(C):
                    sp.wait_ge(x1_done.sem, x1_done.at(b, TH * c + TH))
                    sp.dma_start(x1b[b, :, TH * c:TH * c + TH, :], tok[:, TH * c:TH * c + TH, :])\
                        .then_inc(x1_stored[c].sem, 16)

            load_x(0)
            with sp.Fori(0, B - 1) as b:
                batch(b, False)
            batch(B - 1, True)
            for c in range(C):
                sp.wait_ge(x1_stored[c].sem, x1_stored[c].at(B - 1, 16))

        @block.gpsimd
        def _(pool):
            for part, value in zip(v, (1.0, 0.0)):
                pool.memset(part[:, :, D:D + 2].bitcast(F32), value).then_inc(ones_set, 1)

            def batch(b, last):
                for c in range(C):
                    pool.wait_ge(floored.sem, floored.at(b, c + 1))
                    half = slice(TH * c, TH * c + TH)
                    pool.tensor_tensor(rnorm[:, half, :], ssq_floor[:, half, :],
                                       mhalf[:, 0:2 * TH].rearrange("p (t u) -> p t u", u=2),
                                       ALU.pow).then_inc(rnorm_ready.sem, 1)
                if not last:
                    for c in range(C):
                        ln_in.half_rstd(pool, b + 1, c)
                for c in range(C):
                    ln_out.half_rstd(pool, b, c)

            for c in range(C):
                ln_in.half_rstd(pool, 0, c)
            with pool.Fori(0, B - 1) as b:
                batch(b, False)
            batch(B - 1, True)

        @block.scalar
        def _(act):
            for sig in (squared,):
                act.sem_inc(sig.sem, sig.credit)
            act.sem_inc(f32_done.sem, f32_done.credit)
            act.wait_ge(consts, 16 * 7)

            def cut_hi(b, n, hi):
                act.wait_ge(f32_done.sem, f32_done.at(b, n + 1))
                act.activation(hi, f32[:, n % 2, :], ACT.Copy).then_inc(hi_done.sem, 1)

            def make(b, n, func, **kw):
                act.wait_ge(tile_ready.sem, tile_ready.at(b, n + 1))
                act.wait_ge(lo_done.sem, lo_done.at(b, n - 1))
                act.activation(f32[:, n % 2, :], banks[:, bank_of(n), :], func, **kw).then_inc(f32_done.sem, 1)

            def o_transposed_hi(b, c):
                for k in range(K):
                    act.wait_ge(oT_ready.sem, oT_ready.at(b, K * c + k + 1))
                    act.activation(oT[0][:, k, :], banks[:, Y + k, :], ACT.Copy).then_inc(oT_hi.sem, 1)

            def hidden_1(b, c):
                for m in range(K):
                    n = CUT_H1[c] + m
                    make(b, n, ACT.Relu, bias=b1_col[:, m:m + 1])
                    cut_hi(b, n, h1T[0][:, m, :])

            def hidden_2(b, c):
                for m in range(M2):
                    n = CUT_H2[c] + m
                    make(b, n, ACT.Relu, bias=b2_col[:, m:m + 1])
                    cut_hi(b, n, wide[0][:, m, :])

            def probabilities(b, c):
                for kt in range(T):
                    n = CUT_P[c] + kt
                    make(b, n, ACT.Exp, scale=rnorm[:, kt, 1:2])
                    cut_hi(b, n, wide[0][:, kt, :])

            with act.Fori(0, B) as b:
                for n in range(2 * K):
                    c, k = divmod(n, K)
                    act.wait_ge(xT_ready.sem, xT_ready.at(b, n + 1))
                    act.activation(xT[0][:, k, HALF * c:HALF * c + HALF], banks[:, X + n, :], ACT.Copy)\
                        .then_inc(xT_hi.sem, 1)
                for t in range(T):
                    act.wait_ge(qk_biased.sem, qk_biased.at(b, t + 1))
                    for u in range(2):
                        act.wait_ge(squared.sem, squared.at(b, 2 * t + u - 1))
                        act.activation(squares[:, u, :], qk[:, t, D * u:D * u + D], ACT.Square,
                                       accum_out=ssq[:, t, u:u + 1]).then_inc(squared.sem, 1)
                for n in range(T // 2):
                    act.wait_ge(v_biased.sem, v_biased.at(b, n + 1))
                    act.activation(v[0][:, 2 * n:2 * n + 2, 0:D], v32[:, n % 2, :, :], ACT.Copy)\
                        .then_inc(v_hi.sem, 1)
                for n in range(4 * K):
                    c, which, k = n // (2 * K), n // K % 2, n % K
                    act.wait_ge(qkT_ready.sem, qkT_ready.at(b, n + 1))
                    dst = (qT, kT)[which][0]
                    act.activation(dst[:, k, HALF * c:HALF * c + HALF], banks[:, Y + n % 4, :], ACT.Copy)\
                        .then_inc(qkT_hi.sem, 1)
                act.wait_ge(rnorm_ready.sem, rnorm_ready.at(b, C))
                act.wait_ge(v_lo.sem, v_lo.at(b, T // 2))
                probabilities(b, 0)
                probabilities(b, 1)
                o_transposed_hi(b, 0)
                hidden_1(b, 0)
                hidden_2(b, 0)
                o_transposed_hi(b, 1)
                hidden_1(b, 1)
                hidden_2(b, 1)

        @block.vector
        def _(dve):
            for sig in (lo_done, h3_biased):
                dve.sem_inc(sig.sem, sig.credit)
            for sig in x1_stored:
                dve.sem_inc(sig.sem, sig.credit)
            dve.wait_ge(consts, 16 * 7)

            def cut_lo(b, n, hi, lo):
                dve.wait_ge(hi_done.sem, hi_done.at(b, n + 1))
                dve.tensor_tensor(lo, f32[:, n % 2, :], hi.bitcast(F32), ALU.subtract).then_inc(lo_done.sem, 1)

            def attention_rows(b, c):
                for t in range(TH * c, TH * c + TH):
                    bank = banks[:, (Y, X)[c] + t % 4, :]
                    dve.wait_ge(o_ready.sem, o_ready.at(b, t + 1))
                    dve.reciprocal(rden[:, t:t + 1], bank[:, D:D + 1]).then_inc(den_inverted.sem, 1)
                    dve.wait_ge(den_inverted.sem, den_inverted.at(b, t + 1))
                    dve.tensor_scalar(tok[:, t, :], bank[:, 0:D], rden[:, t:t + 1], None, ALU.mult)\
                        .then_inc(o_done.sem, 1)

            def o_transposed_lo(b, c):
                for k in range(K):
                    dve.wait_ge(oT_hi.sem, oT_hi.at(b, K * c + k + 1))
                    dve.tensor_tensor(oT[1][:, k, :], banks[:, Y + k, :], oT[0][:, k, :].bitcast(F32),
                                      ALU.subtract).then_inc(oT_lo.sem, 1)

            def cut_many(b, first, many, dst):
                for m in range(many):
                    cut_lo(b, first + m, dst[0][:, m, :], dst[1][:, m, :])

            def mlp_rows(b, c):
                for t in range(TH * c, TH * c + TH):
                    dve.wait_ge(h3_ready.sem, h3_ready.at(b, t + 1))
                    dve.tensor_tensor(tok[:, t, :], banks[:, (X, Y)[c] + t % 4, 0:D], b3_row[:, :], ALU.add)\
                        .then_inc(h3_biased.sem, 1)
                    dve.wait_ge(h3_biased.sem, h3_biased.at(b, t + 1))
                    ln_out.tile_stats(dve, b, t, tok[:, t, :])
                ln_out.half_moments(dve, b, c)

            def block_output(b, c):
                ln_out.wait_rstd(dve, b, c)
                if c == 0:
                    dve.wait_ge(xres_loaded.sem, xres_loaded.at(b, 16))
                for t in range(TH * c, TH * c + TH):
                    ln_out.normalise(dve, t, tok[:, t, :], tok[:, t, :]).then_inc(h3_normed.sem, 1)
                for t in range(TH * c, TH * c + TH):
                    dve.wait_ge(h3_normed.sem, h3_normed.at(b, t + 1))
                    dve.tensor_tensor(tok[:, t, :], tok[:, t, :], x_res[:, t, :], ALU.add)\
                        .then_inc(x1_done.sem, 1)

            def input_rows(b):
                for c in range(C):
                    dve.wait_ge(x_loaded[c].sem, x_loaded[c].at(b, 16))
                    for t in range(TH * c, TH * c + TH):
                        ln_in.tile_stats(dve, b, t, x_in[:, t, :])
                    ln_in.half_moments(dve, b, c)
                for c in range(C):
                    ln_in.wait_rstd(dve, b, c)
                    for t in range(TH * c, TH * c + TH):
                        ln_in.normalise(dve, t, xn[:, t, :], x_in[:, t, :]).then_inc(x_normed.sem, 1)

            def batch(b, last):
                for n in range(2 * K):
                    c, k = divmod(n, K)
                    half = slice(HALF * c, HALF * c + HALF)
                    dve.wait_ge(xT_hi.sem, xT_hi.at(b, n + 1))
                    dve.tensor_tensor(xT[1][:, k, half], banks[:, X + n, :], xT[0][:, k, half].bitcast(F32),
                                      ALU.subtract).then_inc(xT_lo.sem, 1)
                for t in range(T):
                    dve.wait_ge(qk_ready.sem, qk_ready.at(b, t + 1))
                    dve.tensor_tensor(qk[:, t, :], banks[:, Y + t % 4, :], bqk_row[:, :], ALU.add)\
                        .then_inc(qk_biased.sem, 1)
                for n in range(T // 2):
                    dve.wait_ge(v_ready.sem, v_ready.at(b, n + 1))
                    dve.tensor_tensor(v32[:, n % 2, :, :],
                                      banks[:, X + n, :].rearrange("p (u d) -> p u d", u=2), bv_row[:, :, :],
                                      ALU.add).then_inc(v_biased.sem, 1)
                    dve.wait_ge(v_hi.sem, v_hi.at(b, n + 1))
                    dve.tensor_tensor(v[1][:, 2 * n:2 * n + 2, 0:D], v32[:, n % 2, :, :],
                                      v[0][:, 2 * n:2 * n + 2, 0:D].bitcast(F32), ALU.subtract)\
                        .then_inc(v_lo.sem, 1)
                    if n < C:
                        c, half = n, slice(TH * n, TH * n + TH)
                        dve.wait_ge(squared.sem, squared.at(b, 2 * TH * (c + 1)))
                        dve.tensor_scalar(ssq_floor[:, half, :], ssq[:, half, :], NORM_FLOOR, None, ALU.max)\
                            .then_inc(floored.sem, 1)
                for c in range(C):
                    dve.wait_ge(rnorm_ready.sem, rnorm_ready.at(b, c + 1))
                    for t in range(TH * c, TH * c + TH):
                        dve.tensor_scalar(qk[:, t, 0:D], qk[:, t, 0:D], rnorm[:, t, 0:1], None, ALU.mult)\
                            .then_inc(q_scaled.sem, 1)
                for n in range(4 * K):
                    c, which, k = n // (2 * K), n // K % 2, n % K
                    half = slice(HALF * c, HALF * c + HALF)
                    dst = (qT, kT)[which]
                    dve.wait_ge(qkT_hi.sem, qkT_hi.at(b, n + 1))
                    dve.tensor_tensor(dst[1][:, k, half], banks[:, Y + n % 4, :], dst[0][:, k, half].bitcast(F32),
                                      ALU.subtract).then_inc(qkT_lo.sem, 1)
                cut_many(b, CUT_P[0], T, wide)
                for c in range(C):
                    dve.wait_ge(x1_stored[c].sem, x1_stored[c].at(b, 0))
                attention_rows(b, 0)
                cut_many(b, CUT_P[1], T, wide)
                if not last:
                    input_rows(b + 1)
                o_transposed_lo(b, 0)
                cut_many(b, CUT_H1[0], K, h1T)
                attention_rows(b, 1)
                cut_many(b, CUT_H2[0], M2, wide)
                mlp_rows(b, 0)
                o_transposed_lo(b, 1)
                cut_many(b, CUT_H1[1], K, h1T)
                cut_many(b, CUT_H2[1], M2, wide)
                block_output(b, 0)
                mlp_rows(b, 1)
                block_output(b, 1)

            input_rows(0)
            with dve.Fori(0, B - 1) as b:
                batch(b, False)
            batch(B - 1, True)

        @block.tensor
        def _(pe):
            pe.wait_ge(ones_set, 2)

            def scores(b, c):
                for kt in range(T):
                    n = CUT_P[c] + kt
                    bank = banks[:, bank_of(n), :]
                    if n >= 4:
                        pe.wait_ge(f32_done.sem, f32_done.at(b, n - 3))
                    if n == 0:
                        pe.wait_ge(v_biased.sem, v_biased.at(b, T // 2))
                        pe.wait_ge(qkT_lo.sem, qkT_lo.at(b, 4 * K))
                    for k in range(K):
                        mm = three_products(pe, bank, [w[:, k, P * kt:P * kt + P] for w in kT],
                                            [m[:, k, HALF * c:HALF * c + HALF] for m in qT], k == 0, k == K - 1)
                    mm.then_inc(tile_ready.sem, 1)

            def attend(b, c):
                for t in range(TH * c, TH * c + TH):
                    bank = banks[:, (Y, X)[c] + t % 4, 0:D + 2]
                    if t == 0:
                        pe.wait_ge(v_lo.sem, v_lo.at(b, T // 2))
                    if t == TH:
                        pe.wait_ge(f32_done.sem, f32_done.at(b, 2 * T))
                    for kt in range(T):
                        if t % TH == 0:
                            pe.wait_ge(lo_done.sem, lo_done.at(b, CUT_P[c] + kt + 1))
                        q = t % TH
                        mm = three_products(pe, bank, [w[:, kt, P * q:P * q + P] for w in wide],
                                            [m[:, kt, :] for m in v], kt == 0, kt == T - 1)
                    mm.then_inc(o_ready.sem, 1)

            def transpose_o(b, c):
                for k in range(K):
                    if c == 0:
                        pe.wait_ge(o_done.sem, o_done.at(b, TH))
                    else:
                        pe.wait_ge(o_done.sem, o_done.at(b, T))
                        pe.wait_ge(f32_done.sem, f32_done.at(b, CUT_H2[0] + M2))
                    for q in range(TH):
                        mm = pe.transpose(banks[:, Y + k, P * q:P * q + P],
                                          tok[:, TH * c + q, P * k:P * k + P], ident[:, :])
                    mm.then_inc(oT_ready.sem, 1)

            def hidden_1(b, c):
                for m in range(K):
                    for k in range(K):
                        pe.wait_ge(oT_lo.sem, oT_lo.at(b, K * c + k + 1))
                        mm = three_products(pe, banks[:, bank_of(CUT_H1[c] + m), :],
                                            [w[:, k, P * m:P * m + P] for w in w1], [o[:, k, :] for o in oT],
                                            k == 0, k == K - 1)
                    mm.then_inc(tile_ready.sem, 1)

            def hidden_2(b, c):
                for m in range(M2):
                    n = CUT_H2[c] + m
                    if m == 0 and c == 0:
                        pe.wait_ge(oT_lo.sem, oT_lo.at(b, K))
                        pe.wait_ge(f32_done.sem, f32_done.at(b, CUT_H1[0] + K))
                    if m == 0 and c == 1:
                        pe.wait_ge(h3_biased.sem, h3_biased.at(b, TH))
                    if m >= 4:
                        pe.wait_ge(f32_done.sem, f32_done.at(b, n - 3))
                    for k in range(K):
                        pe.wait_ge(lo_done.sem, lo_done.at(b, CUT_H1[c] + k + 1))
                        mm = three_products(pe, banks[:, bank_of(n), :], [w[:, k, P * m:P * m + P] for w in w2],
                                            [h[:, k, :] for h in h1T], k == 0, k == K - 1)
                    mm.then_inc(tile_ready.sem, 1)

            def mlp_out(b, c):
                for t in range(TH * c, TH * c + TH):
                    bank, q = banks[:, (X, Y)[c] + t % 4, 0:D], t % TH
                    if t == 0:
                        pe.wait_ge(o_done.sem, o_done.at(b, T))
                    if t == TH:
                        pe.wait_ge(oT_lo.sem, oT_lo.at(b, 2 * K))
                        pe.wait_ge(f32_done.sem, f32_done.at(b, CUT_H1[1] + K))
                    for m in range(M2):
                        if q == 0:
                            pe.wait_ge(lo_done.sem, lo_done.at(b, CUT_H2[c] + m + 1))
                        mm = three_products(pe, bank, [h[:, m, P * q:P * q + P] for h in wide],
                                            [w[:, m, :] for w in w3], m == 0, m == M2 - 1)
                    mm.then_inc(h3_ready.sem, 1)

            with pe.Fori(0, B) as b:
                for n in range(2 * K):
                    c, k = divmod(n, K)
                    if n == 0:
                        pe.wait_ge(f32_done.sem, f32_done.at(b, 0))
                    pe.wait_ge(x_normed.sem, x_normed.at(b, TH * c + TH))
                    for q in range(TH):
                        mm = pe.transpose(banks[:, X + n, P * q:P * q + P],
                                          xn[:, TH * c + q, P * k:P * k + P], ident[:, :])
                    mm.then_inc(xT_ready.sem, 1)
                for t in range(T):
                    if t == 0:
                        pe.wait_ge(h3_biased.sem, h3_biased.at(b, 0))
                    if t % TH == 0:
                        pe.wait_ge(xT_lo.sem, xT_lo.at(b, K * (t // TH + 1)))
                    if t >= 4:
                        pe.wait_ge(qk_biased.sem, qk_biased.at(b, t - 3))
                    for k in range(K):
                        mm = three_products(pe, banks[:, Y + t % 4, :], [w[:, k, P * t:P * t + P] for w in xT],
                                            [m[:, k, :] for m in wqk], k == 0, k == K - 1)
                    mm.then_inc(qk_ready.sem, 1)
                for n in range(T // 2):
                    for u in range(2):
                        t = 2 * n + u
                        for k in range(K):
                            mm = three_products(pe, banks[:, X + n, D * u:D * u + D],
                                                [w[:, k, P * t:P * t + P] for w in xT],
                                                [m[:, k, :] for m in wv], k == 0, k == K - 1)
                    mm.then_inc(v_ready.sem, 1)
                for n in range(4 * K):
                    c, which, k = n // (2 * K), n // K % 2, n % K
                    if n == 0:
                        pe.wait_ge(qk_biased.sem, qk_biased.at(b, T))
                    pe.wait_ge(q_scaled.sem, q_scaled.at(b, TH * (c + 1)))
                    if n >= 4:
                        pe.wait_ge(qkT_lo.sem, qkT_lo.at(b, n - 3))
                    for q in range(TH):
                        mm = pe.transpose(banks[:, Y + n % 4, P * q:P * q + P],
                                          qk[:, TH * c + q, D * which + P * k:D * which + P * k + P], ident[:, :])
                    mm.then_inc(qkT_ready.sem, 1)
                scores(b, 0)
                attend(b, 0)
                scores(b, 1)
                transpose_o(b, 0)
                hidden_1(b, 0)
                attend(b, 1)
                hidden_2(b, 0)
                mlp_out(b, 0)
                transpose_o(b, 1)
                hidden_1(b, 1)
                hidden_2(b, 1)
                mlp_out(b, 1)


def expert_block(nc, ident, mhalf, x1, out, weights, wg_in, cols):
    wqk, wv, wo, w1, w2 = weights
    with ExitStack() as ctx:
        def sb(name, shape, dt=F32):
            return ctx.enter_context(nc.sbuf_tensor(name, shape, dt))

        def signal(name, per, credit=0):
            return Signal(ctx, nc, name, per, credit)

        def pair(name, shape):
            return sb(f"{name}_hi", shape, F32R), sb(f"{name}_lo", shape, F32R)

        z = sb("z", [P, T, D])
        z_next = sb("z_next", [P, T, D])
        xn = sb("xn", [P, T, D])
        cut = pair("cut", [P, NE * HALF])
        xT = [m[:, 0:K * S].rearrange("p (k s) -> p k s", k=K) for m in cut]
        oT = [m[:, K * S:2 * K * S].rearrange("p (k s) -> p k s", k=K) for m in cut]
        hidden = [m[:, :].rearrange("p (e s) -> p e s", e=NE) for m in cut]
        v = sb("v_rows", [P, T, D])
        vh = sb("v_head", [P, 2, T, VW])
        f32 = sb("f32_b", [P, 2, HALF])
        q_stack = sb("q_stack", [P, HPI, S], BF16)
        k_stack = sb("k_stack", [P, HPI, S], BF16)
        probs = sb("probs", [P, 2 * T, HALF])
        parts = probs[:, 0:2 * K * PARTS, :].bitcast(BF16).rearrange("p (n a) s -> p n a s", a=PARTS)
        cw_all = probs[:, 0:8, :].rearrange("p n s -> p (n s)")
        cw_row = probs[:, 8:16, :].rearrange("p n s -> p (n s)")
        o_out = sb("o_out", [P, 2, QUARTER])
        inv_out = sb("inv_out", [P, 2, QUARTER])
        o_num = sb("o_num", [P, K, S])
        o_inv = sb("o_inv", [P, K, S])
        xf32 = o_num[:, 0, :].rearrange("p (k s) -> p k s", k=K)
        x_res = o_inv[:, :, :].rearrange("p k (t d) -> p (k t) d", d=D)
        xfT = pair("xfT", [P, K, HALF])
        maxima = sb("maxima", [P, 2, T])
        neg = sb("neg", [T, 2, P])
        neg_hi = sb("neg_hi", [T, 2, P], BF16)
        neg_lo = sb("neg_lo", [T, 2, P], BF16)
        wg = sb("wg", [P, K, NE])
        col = {n: sb(f"norm_{n}", [P, K]) for n in cols}
        lane = sb("lane", [P, TH, NE])
        gate = sb("gate", [P, T, NE])
        top = sb("top", [P, T, 8])
        top_at = sb("top_at", [P, T, 8], U32)
        top_lane = sb("top_lane", [P, T, 2])
        gap = sb("gap", [P, T])
        gap_exp = sb("gap_exp", [P, T])
        gap_sum = sb("gap_sum", [P, T])
        share = sb("share", [P, T, 2])
        picked = sb("picked", [P, 2, TH, NE])
        weighted = sb("weighted", [P, 2, TH, NE])
        cw = sb("cw", [P, T, NE])
        cwT = sb("cwT", [TH * NE, C, P])
        banks = ctx.enter_context(nc.psum_tensor("banks_b", [P, 8, HALF], F32))
        X, Y = 0, 4
        ST, PV = 4, 6

        q_dram = nc.dram_tensor("q_parts", [B, D, NPOS, S], BF16).ap()
        k_dram = nc.dram_tensor("k_parts", [B, D, NPOS, S], BF16).ap()
        o_dram = nc.dram_tensor("o_rows", [B, NH, VW, S], F32).ap()
        inv_dram = nc.dram_tensor("inv_rows", [B, NH, S], F32).ap()

        ln_z = LayerNorm(ctx, nc, "ln_z", mhalf)
        ln_a = LayerNorm(ctx, nc, "ln_a", mhalf)
        ln_m = LayerNorm(ctx, nc, "ln_m", mhalf)
        ln_o = LayerNorm(ctx, nc, "ln_o", mhalf)
        STEPS, STEP_GAP = 19, 6
        NST, NM, NMT = 2 * T, T + 1, NH * (T + 1)
        consts = nc.alloc_semaphore("b_consts_loaded")
        prepared = nc.alloc_semaphore("b_buffers_prepared")
        taken = {eng: nc.alloc_semaphore(f"wait_taken_{eng}") for eng in ("sp", "pool", "dve", "pe")}
        x1_loaded = [signal(f"b_x1_loaded{c}", 16) for c in range(C)]
        z_done = signal("z_done", T)
        a_normed = signal("a_normed", T)
        xT_ready = signal("b_xT_ready", 2 * K)
        f_done = signal("f_done", 2 * K)
        f_hi = signal("f_hi", 2 * K)
        f_lo = signal("f_lo", 2 * K, 2)
        NQ = 2 * K * C
        qk_ready = signal("b_qk_ready", NQ)
        part1_done = signal("part1_done", NQ)
        rest_done = signal("rest_done", NQ)
        part2_done = signal("part2_done", NQ)
        part3_done = signal("part3_done", NQ)
        parts_stored = signal("parts_stored", 16 * 3 * 2 * K)
        z_copied = signal("z_copied", 1)
        v_ready = signal("b_v_ready", T // 2)
        v_copied = signal("v_copied", T // 2)
        vh_ready = signal("vh_ready", NH)
        stack_loaded = [signal(f"stack_loaded{n}", 2 * 16 * NH // HPI) for n in range(HPI)]
        shift_loaded = [signal(f"shift_loaded{n}", 2 * 16 * NH // HPI, 32 * (n >= HPI - 2)) for n in range(HPI)]
        max_ready = signal("max_ready", NMT)
        max_read = signal("max_read", NMT, 2)
        neg_hi_done = signal("neg_hi_done", NH, 2)
        neg_lo_done = signal("neg_lo_done", NH, 2)
        st_ready = signal("st_ready", NH * NST)
        exp_done = signal("exp_done", NH * NST, 2)
        pv_done = signal("pv_done", 4 * NH, 8)
        o_copied = signal("o_copied", NH, 2)
        inverted = signal("inverted", NH)
        o_stored = [signal(f"o_stored{n}", 32 * NH // 2, 32) for n in range(2)]
        o_loaded = signal("o_loaded", 16 * 2 * K)
        o_normed = [signal(f"o_normed{k}", C) for k in range(K)]
        oT_hi = signal("b_oT_hi", K * C)
        oT_lo = signal("b_oT_lo", K * C)
        wo_ready = signal("wo_ready", T)
        x2_done = signal("x2_done", T)
        m_normed = signal("m_normed", T)
        xfT_ready = signal("xfT_ready", 2 * K)
        xf_done = signal("xf_done", 2 * K)
        xf_hi = signal("xf_hi", 2 * K)
        xf_lo = signal("xf_lo", 2 * K)
        gT_ready = signal("gT_ready", C)
        gT_copied = signal("gT_copied", C)
        gate_ready = signal("gate_ready", C)
        choose = signal("choose", STEPS * C)
        gap_exp_done = signal("gap_exp_done", C)
        cwT_ready = signal("cwT_ready", C)
        cwT_copied = signal("cwT_copied", C)
        cw_row_loaded = signal("cw_row_loaded", 16 * C)
        cw_spread = signal("cw_spread", C)
        up_ready = signal("up_ready", C * NE)
        up_done = signal("up_done", C * NE, C * NE)
        up_hi = signal("up_hi", C * NE)
        up_lo = signal("up_lo", C * NE)
        down_ready = signal("down_ready", T)
        y_done = signal("y_done", T, T)
        y_normed = signal("y_normed", T)
        out_done = signal("out_done", T)
        res_loaded = signal("res_loaded", 16)
        out_stored = [signal(f"out_stored{c}", 16, 16) for c in range(C)]

        x1b = x1.rearrange("b (t p) d -> b p t d", p=P)
        outb = out.rearrange("b (t p) d -> b p t d", p=P)

        def m_index(q):
            return q if q < 2 else q + 1

        RING_0 = 2 * T + 1
        block = ctx.enter_context(nc.Block())

        @block.sync
        def _(sp):
            for n in cols:
                sp.dma_start(col[n][:, :], cols[n]).then_inc(consts, 16)
            sp.dma_start(wg[:, :, :], wg_in.rearrange("(k p) e -> p k e", p=P)).then_inc(consts, 16)

            def load_x1(b):
                for c in range(C):
                    sp.dma_start(z_next[:, TH * c:TH * c + TH, :], x1b[b, :, TH * c:TH * c + TH, :])\
                        .then_inc(x1_loaded[c].sem, 16)

            def store_parts(b, m, which):
                own = parts[:, 2 * m + which, :, :]
                sources = ((own, own[:, 0:2, :], own[:, 0:1, :]) if which else
                           (own[:, 0:1, :].to_broadcast([P, 3, S]), own[:, 1:2, :].to_broadcast([P, 2, S]),
                            own[:, 2:3, :]))
                sp.wait_ge(part3_done.sem, part3_done.at(b, (2 * m + which + 1) * C))
                for first, many, src in zip((0, 3, 5), (3, 2, 1), sources):
                    sp.dma_start((q_dram, k_dram)[which][b, P * m:P * m + P, first:first + many, :], src)\
                        .then_inc(parts_stored.sem, 16)

            def load_stack(b, slot, row):
                for stack, rows in ((q_stack, q_dram), (k_stack, k_dram)):
                    sp.dma_start(stack[0:STACK, slot, :], rows[b, bass.ds(row, DK), :, :]
                                 .rearrange("r a s -> (r a) s")).then_inc(stack_loaded[slot].sem, 16)

            def heads(b, i, last):
                for j in range(HPI):
                    if not last:
                        sp.wait_ge(st_ready.sem, st_ready.at(b, NST * (j + 1), i * HPI * NST))
                        sp.sem_inc(taken["sp"], 1)
                        load_stack(b, j, i * HPI * DK + (HPI + j) * DK)
                    sp.wait_ge(o_copied.sem, o_copied.at(b, j + 1, i * HPI))
                    sp.sem_inc(taken["sp"], 1)
                    sp.dma_start(o_dram[b, i * HPI + j].rearrange("d (u s) -> u d s", u=4), o_out[:, j % 2, :])\
                        .then_inc(o_stored[j % 2].sem, 16)
                    sp.wait_ge(inverted.sem, inverted.at(b, j + 1, i * HPI))
                    sp.sem_inc(taken["sp"], 1)
                    sp.dma_start(inv_dram[b, i * HPI + j].rearrange("(u s) -> u s", u=4),
                                 inv_out[DK:P:VW, j % 2, :]).then_inc(o_stored[j % 2].sem, 16)

            def load_o(b, k):
                for u in range(2):
                    sp.wait_ge(o_stored[u].sem, o_stored[u].at(b, 32 * NH // 2 * (k + 1) // K))
                sp.sem_inc(taken["sp"], 1)
                some = slice(NH // K * k, NH // K * (k + 1))
                sp.dma_start(o_num[:, k, :], o_dram[b, some, 0:DK, :]).then_inc(o_loaded.sem, 16)
                sp.dma_start(o_inv[:, k, :], inv_dram[b, some, :].rearrange("h (o s) -> h o s", o=1)
                             .to_broadcast([NH // K, DK, S]))\
                    .then_inc(o_loaded.sem, 16)

            def batch(b, last):
                for m in range(K):
                    for which in range(2):
                        store_parts(b, m, which)
                    if m == 0:
                        sp.wait_ge(parts_stored.sem, parts_stored.at(b, 16 * 3 * 2))
                        sp.sem_inc(taken["sp"], 1)
                        for slot in range(HPI):
                            load_stack(b, slot, slot * DK)
                sp.wait_ge(parts_stored.sem, parts_stored.at(b, 16 * 3 * 2 * K))
                sp.sem_inc(taken["sp"], 1)
                if not last:
                    sp.wait_ge(z_copied.sem, z_copied.at(b, 1))
                    sp.sem_inc(taken["sp"], 1)
                    load_x1(b + 1)
                with sp.Fori(0, NH // HPI - 1) as i:
                    heads(b, i, False)
                load_o(b, 0)
                heads(b, NH // HPI - 1, True)
                load_o(b, 1)
                for k in range(K):
                    sp.wait_ge(o_normed[k].sem, o_normed[k].at(b, C))
                sp.dma_start(x_res, x1b[b]).then_inc(res_loaded.sem, 16)
                for c in range(C):
                    sp.wait_ge(cwT_copied.sem, cwT_copied.at(b, c + 1))
                    if c > 0:
                        sp.wait_ge(cw_spread.sem, cw_spread.at(b, c))
                    sp.dma_start(cw_row[0:1, :].rearrange("o (r p) -> o r p", p=P), cwT[:, c, :])\
                        .then_inc(cw_row_loaded.sem, 16)
                for c in range(C):
                    sp.wait_ge(out_done.sem, out_done.at(b, TH * c + TH))
                    sp.dma_start(outb[b, :, TH * c:TH * c + TH, :], xn[:, TH * c:TH * c + TH, :])\
                        .then_inc(out_stored[c].sem, 16)

            load_x1(0)
            with sp.Fori(0, B - 1) as b:
                batch(b, False)
            batch(B - 1, True)
            for c in range(C):
                sp.wait_ge(out_stored[c].sem, out_stored[c].at(B - 1, 16))

        @block.gpsimd
        def _(pool):
            for sig in (neg_hi_done, neg_lo_done):
                pool.sem_inc(sig.sem, sig.credit)
            pool.memset(q_stack[96:P, :, :], 0.0).then_inc(prepared, 1)
            pool.memset(k_stack[96:P, :, :], 1.0).then_inc(prepared, 1)
            pool.wait_ge(prepared, 2)
            pool.memset(vh[:, :, :, :], 1.0).then_inc(prepared, 1)
            pool.iota(lane[:, :, :], [[0, TH], [1, NE]], base=0, channel_multiplier=0,
                      allow_small_or_imprecise_dtypes=True).then_inc(prepared, 1)
            pool.memset(neg_hi[:, :, :], 0.0).then_inc(prepared, 1)
            pool.wait_ge(prepared, 5)
            for slot in range(HPI - 2, HPI):
                for row in (STACK, STACK + 1):
                    pool.dma_start(q_stack[row:row + 1, slot, :].rearrange("o (t p) -> o t p", p=P),
                                   neg_hi[:, slot % 2, :]).then_inc(shift_loaded[slot].sem, 16)

            def negate_max(b, i, j, ring):
                slot = j % HPI
                pool.wait_ge(max_read.sem, max_read.at(b, ring, i * HPI * NM))
                before, turn = (slot + 2) % HPI, (j - 2) // HPI + 1
                pool.wait_ge(shift_loaded[before].sem, shift_loaded[before].at(b, 32 * turn, i * 32))
                pool.sem_inc(taken["pool"], 1)
                pool.tensor_copy(neg_hi[:, j % 2, :], neg[:, j % 2, :]).then_inc(neg_hi_done.sem, 1)
                pool.wait_ge(neg_hi_done.sem, neg_hi_done.at(b, j + 1, i * HPI))
                pool.tensor_tensor(neg_lo[:, j % 2, :], neg[:, j % 2, :], neg_hi[:, j % 2, :],
                                   ALU.subtract).then_inc(neg_lo_done.sem, 1)
                pool.wait_ge(neg_lo_done.sem, neg_lo_done.at(b, j + 1, i * HPI))
                pool.sem_inc(taken["pool"], 1)
                for row, src in ((STACK, neg_hi), (STACK + 1, neg_lo)):
                    pool.dma_start(q_stack[row:row + 1, slot, :].rearrange("o (t p) -> o t p", p=P),
                                   src[:, j % 2, :]).then_inc(shift_loaded[slot].sem, 16)

            def head_values(b, i, j):
                pool.wait_ge(pv_done.sem, pv_done.at(b, 4 * (j - 1), i * HPI * 4))
                pool.sem_inc(taken["pool"], 1)
                first = i * HPI * DK + j * DK
                pool.tensor_copy(vh[:, j % 2, :, 0:DK], v[:, :, bass.ds(first, DK)]).then_inc(vh_ready.sem, 1)

            def heads(b, i, last):
                for j in range(HPI):
                    if not (last and j == HPI - 1):
                        done = RING_0 + NM * j + (3 if not (last and j == HPI - 2) else 1)
                        negate_max(b, i, j + 1, done)
                        head_values(b, i, j + 1)

            def normalise_o(b, k, c):
                half = slice(HALF * c, HALF * c + HALF)
                pool.wait_ge(o_loaded.sem, o_loaded.at(b, 16 * 2 * (k + 1)))
                pool.tensor_tensor(o_num[:, k, half], o_num[:, k, half], o_inv[:, k, half], ALU.mult)\
                    .then_inc(o_normed[k].sem, 1)

            def input_rows(b):
                for ln in (ln_z, ln_a):
                    for c in range(C):
                        ln.half_rstd(pool, b, c)

            def batch(b, last):
                negate_max(b, 0, 0, T + 1)
                pool.wait_ge(v_copied.sem, v_copied.at(b, T // 2))
                head_values(b, 0, 0)
                with pool.Fori(0, NH // HPI - 1) as i:
                    heads(b, i, False)
                heads(b, NH // HPI - 1, True)
                for c in range(C):
                    normalise_o(b, 0, c)
                if not last:
                    input_rows(b + 1)
                for c in range(C):
                    ln_m.half_rstd(pool, b, c)
                for c in range(C):
                    pool.wait_ge(cw_row_loaded.sem, cw_row_loaded.at(b, 16 * (c + 1)))
                    if c > 0:
                        pool.wait_ge(up_done.sem, up_done.at(b, NE * c))
                    pool.sem_inc(taken["pool"], 1)
                    pool.partition_broadcast(cw_all, cw_row[0:1, :], channels=P).then_inc(cw_spread.sem, 1)
                for c in range(C):
                    ln_o.half_rstd(pool, b, c)

            input_rows(0)
            with pool.Fori(0, B - 1) as b:
                batch(b, False)
            batch(B - 1, True)

        @block.scalar
        def _(act):
            for sig in (exp_done, o_copied, *o_stored):
                act.sem_inc(sig.sem, sig.credit)
            act.wait_ge(consts, 16 * (len(cols) + 1))

            def exponential(b, i, j, n):
                act.wait_ge(st_ready.sem, st_ready.at(b, NST * j + n + 1, i * HPI * NST))
                if n % 4 == 0:
                    act.wait_ge(pv_done.sem, pv_done.at(b, 4 * j + n // 4 - 3, i * HPI * 4))
                act.activation(probs[:, n, :], banks[:, ST + n % 2, :], ACT.Exp).then_inc(exp_done.sem, 1)

            def copy_o(b, i, j):
                act.wait_ge(pv_done.sem, pv_done.at(b, 4 * (j + 1), i * HPI * 4))
                act.wait_ge(o_stored[j % 2].sem, o_stored[j % 2].at(b, 32 * (j // 2), i * 32 * HPI // 2))
                act.activation(o_out[:, j % 2, :], banks[:, PV + j % 2, 0:QUARTER], ACT.Copy).then_inc(o_copied.sem, 1)

            def attention_hi(b, k):
                for c in range(C):
                    half = slice(HALF * c, HALF * c + HALF)
                    act.wait_ge(o_normed[k].sem, o_normed[k].at(b, c + 1))
                    act.activation(oT[0][:, k, half], o_num[:, k, half], ACT.Copy).then_inc(oT_hi.sem, 1)

            def heads(b, i, last):
                for j in range(HPI):
                    for n in range(NST):
                        exponential(b, i, j, n)
                        if n == 4 and j > 0:
                            copy_o(b, i, j - 1)
                        if last and j == HPI - 1 and n == 7:
                            attention_hi(b, 0)
                copy_o(b, i, HPI - 1)

            with act.Fori(0, B) as b:
                for n in range(2 * K):
                    c, k = divmod(n, K)
                    act.wait_ge(xT_ready.sem, xT_ready.at(b, n + 1))
                    act.wait_ge(f_lo.sem, f_lo.at(b, n - 1))
                    act.activation(f32[:, n % 2, :], banks[:, X + n, :], ACT.Identity, bias=col["b1"][:, k:k + 1],
                                   scale=col["g1"][:, k:k + 1]).then_inc(f_done.sem, 1)
                    act.wait_ge(f_done.sem, f_done.at(b, n + 1))
                    act.activation(xT[0][:, k, HALF * c:HALF * c + HALF], f32[:, n % 2, :], ACT.Copy)\
                        .then_inc(f_hi.sem, 1)
                for n in range(NQ):
                    scale = DK ** -0.5 if n // C % 2 == 0 else 1.0
                    act.wait_ge(qk_ready.sem, qk_ready.at(b, n + 1))
                    half = slice(HALF * (n % C), HALF * (n % C) + HALF)
                    act.activation(parts[:, n // C, 0, half], banks[:, Y + n % 4, :], ACT.Copy, scale=scale)\
                        .then_inc(part1_done.sem, 1)
                    act.wait_ge(rest_done.sem, rest_done.at(b, n + 1))
                    act.activation(parts[:, n // C, 1, half], f32[:, n % 2, :], ACT.Copy).then_inc(part2_done.sem, 1)
                for n in range(T // 2):
                    act.wait_ge(v_ready.sem, v_ready.at(b, n + 1))
                    act.activation(v[:, 2 * n:2 * n + 2, :], banks[:, Y + n, :].rearrange("p (u d) -> p u d", u=2),
                                   ACT.Copy).then_inc(v_copied.sem, 1)
                act.wait_ge(y_done.sem, y_done.at(b, 0))
                act.activation(z[:, :, :], z_next[:, :, :], ACT.Copy).then_inc(z_copied.sem, 1)
                act.wait_ge(parts_stored.sem, parts_stored.at(b, 16 * 3 * 2 * K))
                with act.Fori(0, NH // HPI - 1) as i:
                    heads(b, i, False)
                heads(b, NH // HPI - 1, True)
                attention_hi(b, 1)
                for c in range(C):
                    for k in range(K):
                        n = K * c + k
                        act.wait_ge(xfT_ready.sem, xfT_ready.at(b, n + 1))
                        act.activation(xf32[:, k, :], banks[:, (X, Y)[c] + k, :], ACT.Identity,
                                       bias=col["b2"][:, k:k + 1], scale=col["g2"][:, k:k + 1]).then_inc(xf_done.sem, 1)
                        act.wait_ge(xf_done.sem, xf_done.at(b, n + 1))
                        act.activation(xfT[0][:, k, :], xf32[:, k, :], ACT.Copy).then_inc(xf_hi.sem, 1)
                    act.wait_ge(gT_ready.sem, gT_ready.at(b, c + 1))
                    if c > 0:
                        act.wait_ge(up_lo.sem, up_lo.at(b, NE * c))
                    act.activation(f32[0:NE, c, :], banks[0:NE, (X, Y)[c] + 2, :], ACT.Copy).then_inc(gT_copied.sem, 1)
                    act.wait_ge(choose.sem, choose.at(b, STEPS * c + STEP_GAP))
                    act.activation(gap_exp[:, TH * c:TH * c + TH], gap[:, TH * c:TH * c + TH], ACT.Exp)\
                        .then_inc(gap_exp_done.sem, 1)
                    for n in range(NE * c, NE * c + NE):
                        act.wait_ge(up_done.sem, up_done.at(b, n + 1))
                        act.activation(hidden[0][:, n % NE, :], f32[:, n % 2, :], ACT.Copy).then_inc(up_hi.sem, 1)

        @block.vector
        def _(dve):
            for sig in (f_lo, max_read, up_done, y_done):
                dve.sem_inc(sig.sem, sig.credit)
            dve.wait_ge(consts, 16 * (len(cols) + 1))
            dve.wait_ge(prepared, 5)

            def negated_maxima(b, i, head, done):
                step = done - 1
                dve.wait_ge(max_ready.sem, max_ready.at(b, done, i * HPI * NM))
                dve.wait_ge(neg_lo_done.sem, neg_lo_done.at(b, head - 1, i * HPI))
                dve.tensor_scalar(neg[:, head % 2, :], banks[0:T, 2 * (step % 2), 0:P], -1.0, None, ALU.mult)\
                    .then_inc(max_read.sem, 1)

            def tile_maximum(b, i, head, q, done):
                step = done - 1
                dve.wait_ge(max_ready.sem, max_ready.at(b, done, i * HPI * NM))
                dve.tensor_reduce(maxima[:, head % 2, q:q + 1], banks[:, 2 * (step % 2):2 * (step % 2) + 2, :],
                                  AX.XY, ALU.max).then_inc(max_read.sem, 1)

            def invert(b, i, j):
                dve.wait_ge(o_copied.sem, o_copied.at(b, j + 1, i * HPI))
                dve.wait_ge(o_stored[j % 2].sem, o_stored[j % 2].at(b, 32 * (j // 2), i * 32 * HPI // 2))
                dve.reciprocal(inv_out[:, j % 2, :], o_out[:, j % 2, :]).then_inc(inverted.sem, 1)

            def heads(b, i, last):
                for j in range(HPI):
                    base, more = RING_0 + NM * j, not (last and j >= HPI - 2)
                    for q in range(T):
                        if more:
                            tile_maximum(b, i, j + 2, q, base + m_index(q) + 1)
                        if q == 4 and j > 0 and not (last and j == HPI - 1):
                            invert(b, i, j - 1)
                        if q == 1 and not (last and j == HPI - 1):
                            negated_maxima(b, i, j + 1, base + (3 if more else 1))
                if not last:
                    invert(b, i, HPI - 1)

            def normalise_o(b, k, c):
                half = slice(HALF * c, HALF * c + HALF)
                dve.wait_ge(o_loaded.sem, o_loaded.at(b, 16 * 2 * (k + 1)))
                dve.tensor_tensor(o_num[:, k, half], o_num[:, k, half], o_inv[:, k, half], ALU.mult)\
                    .then_inc(o_normed[k].sem, 1)

            def attention_lo(b, k, c):
                half = slice(HALF * c, HALF * c + HALF)
                dve.wait_ge(oT_hi.sem, oT_hi.at(b, C * k + c + 1))
                dve.tensor_tensor(oT[1][:, k, half], o_num[:, k, half], oT[0][:, k, half].bitcast(F32),
                                  ALU.subtract).then_inc(oT_lo.sem, 1)

            def input_rows(b):
                for c in range(C):
                    dve.wait_ge(x1_loaded[c].sem, x1_loaded[c].at(b, 16))
                    for t in range(TH * c, TH * c + TH):
                        ln_z.tile_stats(dve, b, t, z_next[:, t, :])
                    ln_z.half_moments(dve, b, c)
                for c in range(C):
                    ln_z.wait_rstd(dve, b, c)
                    for t in range(TH * c, TH * c + TH):
                        ln_z.normalise(dve, t, z_next[:, t, :], z_next[:, t, :]).then_inc(z_done.sem, 1)
                    for t in range(TH * c, TH * c + TH):
                        dve.wait_ge(z_done.sem, z_done.at(b, t + 1))
                        ln_a.tile_stats(dve, b, t, z_next[:, t, :])
                    ln_a.half_moments(dve, b, c)
                for c in range(C):
                    ln_a.wait_rstd(dve, b, c)
                    for t in range(TH * c, TH * c + TH):
                        ln_a.normalise(dve, t, v[:, t, :], z_next[:, t, :]).then_inc(a_normed.sem, 1)

            def second_residual(b, c):
                for t in range(TH * c, TH * c + TH):
                    dve.wait_ge(wo_ready.sem, wo_ready.at(b, t + 1))
                    dve.tensor_tensor(z[:, t, :], banks[:, (X, Y)[c] + t % 4, 0:D], z[:, t, :], ALU.add)\
                        .then_inc(x2_done.sem, 1)
                    dve.wait_ge(x2_done.sem, x2_done.at(b, t + 1))
                    ln_m.tile_stats(dve, b, t, z[:, t, :])
                ln_m.half_moments(dve, b, c)

            def expert_input(b, c):
                ln_m.wait_rstd(dve, b, c)
                for t in range(TH * c, TH * c + TH):
                    ln_m.normalise(dve, t, xn[:, t, :], z[:, t, :]).then_inc(m_normed.sem, 1)

            def expert_input_lo(b, c):
                for k in range(K):
                    dve.wait_ge(xf_hi.sem, xf_hi.at(b, K * c + k + 1))
                    dve.tensor_tensor(xfT[1][:, k, :], xf32[:, k, :], xfT[0][:, k, :].bitcast(F32), ALU.subtract)\
                        .then_inc(xf_lo.sem, 1)

            def choose_experts(b, c):
                half, done = slice(TH * c, TH * c + TH), STEPS * c

                def after(step):
                    dve.wait_ge(choose.sem, choose.at(b, done + step))

                def step(instruction):
                    instruction.then_inc(choose.sem, 1)

                bank = banks[:, X + 3, 0:TH * NE].rearrange("p (t e) -> p t e", e=NE)
                dve.wait_ge(gate_ready.sem, gate_ready.at(b, c + 1))
                step(dve.tensor_copy(gate[:, half, :], bank))
                after(1)
                dve.sem_inc(taken["dve"], 1)
                for t in range(TH * c, TH * c + TH):
                    step(dve.max(top[:, t, :], gate[:, t, :]))
                after(5)
                step(dve.tensor_tensor(gap[:, half], top[:, half, 1], top[:, half, 0], ALU.subtract))
                for t in range(TH * c, TH * c + TH):
                    step(dve.max_index(top_at[:, t, :], top[:, t, :], gate[:, t, :]))
                after(10)
                step(dve.tensor_copy(top_lane[:, half, :], top_at[:, half, 0:2]))
                dve.wait_ge(gap_exp_done.sem, gap_exp_done.at(b, c + 1))
                step(dve.tensor_scalar(gap_sum[:, half], gap_exp[:, half], 1.0, None, ALU.add))
                after(12)
                step(dve.reciprocal(share[:, half, 0], gap_sum[:, half]))
                after(13)
                step(dve.tensor_tensor(share[:, half, 1], gap_exp[:, half], share[:, half, 0], ALU.mult))
                for u in range(2):
                    step(dve.tensor_tensor(picked[:, u, :, :], lane[:, :, :],
                                           top_lane[:, half, u:u + 1].to_broadcast([P, TH, NE]), ALU.is_equal))
                after(16)
                for u in range(2):
                    step(dve.tensor_tensor(weighted[:, u, :, :], picked[:, u, :, :],
                                           share[:, half, u:u + 1].to_broadcast([P, TH, NE]), ALU.mult))
                after(18)
                step(dve.tensor_tensor(cw[:, half, :], weighted[:, 0, :, :], weighted[:, 1, :, :], ALU.add))

            def weights_out(b, c):
                dve.wait_ge(cwT_ready.sem, cwT_ready.at(b, c + 1))
                dve.tensor_copy(cwT[:, c, :], banks[0:TH * NE, X + 3, P:2 * P]).then_inc(cwT_copied.sem, 1)

            def expert_hidden(b, c):
                weights = cw_all.rearrange("p (t e s) -> p t e s", t=TH, e=NE)
                for n in range(NE * c, NE * c + NE):
                    e = n % NE

                    def lo(n):
                        dve.wait_ge(up_hi.sem, up_hi.at(b, n + 1))
                        dve.tensor_tensor(hidden[1][:, n % NE, :], f32[:, n % 2, :], hidden[0][:, n % NE, :]
                                          .bitcast(F32), ALU.subtract).then_inc(up_lo.sem, 1)

                    if e == 0:
                        dve.wait_ge(cw_spread.sem, cw_spread.at(b, c + 1))
                    dve.wait_ge(up_ready.sem, up_ready.at(b, n + 1))
                    if n >= 2:
                        dve.wait_ge(up_lo.sem, up_lo.at(b, n - 1))
                    dve.scalar_tensor_tensor(
                        out=f32[:, n % 2, :].rearrange("p (t s) -> p t s", t=TH),
                        in0=banks[:, X + n % 4, :].rearrange("p (t s) -> p t s", t=TH), scalar=0.0,
                        in1=weights[:, :, e, :], op0=ALU.max, op1=ALU.mult).then_inc(up_done.sem, 1)
                    if e > 0:
                        lo(n - 1)
                lo(NE * c + NE - 1)

            def block_rows(b, tiles):
                for t in tiles:
                    dve.wait_ge(down_ready.sem, down_ready.at(b, t + 1))
                    dve.tensor_tensor(xn[:, t, :], banks[:, Y + t % 4, 0:D], z[:, t, :], ALU.add)\
                        .then_inc(y_done.sem, 1)
                    dve.wait_ge(y_done.sem, y_done.at(b, t + 1))
                    ln_o.tile_stats(dve, b, t, xn[:, t, :])

            def block_output(b, c):
                ln_o.wait_rstd(dve, b, c)
                for t in range(TH * c, TH * c + TH):
                    ln_o.normalise(dve, t, xn[:, t, :], xn[:, t, :]).then_inc(y_normed.sem, 1)
                dve.wait_ge(res_loaded.sem, res_loaded.at(b, 16))
                for t in range(TH * c, TH * c + TH):
                    dve.wait_ge(y_normed.sem, y_normed.at(b, t + 1))
                    dve.tensor_tensor(xn[:, t, :], xn[:, t, :], x_res[:, t, :], ALU.add)\
                        .then_inc(out_done.sem, 1)

            for sig in out_stored:
                dve.sem_inc(sig.sem, sig.credit)

            def batch(b, last):
                for n in range(2 * K):
                    c, k = divmod(n, K)
                    half = slice(HALF * c, HALF * c + HALF)
                    dve.wait_ge(f_hi.sem, f_hi.at(b, n + 1))
                    dve.tensor_tensor(xT[1][:, k, half], f32[:, n % 2, :], xT[0][:, k, half].bitcast(F32),
                                      ALU.subtract).then_inc(f_lo.sem, 1)
                for n in range(NQ + 1):
                    if n < NQ:
                        scale = DK ** -0.5 if n // C % 2 == 0 else 1.0
                        if n < 2:
                            dve.wait_ge(f_lo.sem, f_lo.at(b, 2 * K))
                        else:
                            dve.wait_ge(part3_done.sem, part3_done.at(b, n - 1))
                        half = slice(HALF * (n % C), HALF * (n % C) + HALF)
                        dve.wait_ge(part1_done.sem, part1_done.at(b, n + 1))
                        dve.scalar_tensor_tensor(out=f32[:, n % 2, :], in0=banks[:, Y + n % 4, :], scalar=scale,
                                                 in1=parts[:, n // C, 0, half], op0=ALU.mult, op1=ALU.subtract)\
                            .then_inc(rest_done.sem, 1)
                    if n > 0:
                        own = parts[:, (n - 1) // C, :, HALF * ((n - 1) % C):HALF * ((n - 1) % C) + HALF]
                        dve.wait_ge(part2_done.sem, part2_done.at(b, n))
                        dve.tensor_tensor(own[:, 2, :], f32[:, (n - 1) % 2, :], own[:, 1, :], ALU.subtract)\
                            .then_inc(part3_done.sem, 1)
                for q in range(T):
                    tile_maximum(b, 0, 0, q, q + 1)
                negated_maxima(b, 0, 0, T + 1)
                for q in range(T):
                    tile_maximum(b, 0, 1, q, T + 1 + q + 1)
                with dve.Fori(0, NH // HPI - 1) as i:
                    heads(b, i, False)
                heads(b, NH // HPI - 1, True)
                if not last:
                    dve.wait_ge(vh_ready.sem, vh_ready.at(b, NH))
                    input_rows(b + 1)
                invert(b, NH // HPI - 1, HPI - 2)
                for c in range(C):
                    attention_lo(b, 0, c)
                invert(b, NH // HPI - 1, HPI - 1)
                for c in range(C):
                    normalise_o(b, 1, c)
                for c in range(C):
                    attention_lo(b, 1, c)
                for c in range(C):
                    dve.wait_ge(out_stored[c].sem, out_stored[c].at(b, 0))
                second_residual(b, 0)
                expert_input(b, 0)
                second_residual(b, 1)
                expert_input_lo(b, 0)
                choose_experts(b, 0)
                weights_out(b, 0)
                expert_input(b, 1)
                expert_hidden(b, 0)
                expert_input_lo(b, 1)
                choose_experts(b, 1)
                block_rows(b, (0, 1))
                weights_out(b, 1)
                block_rows(b, (2, 3))
                ln_o.half_moments(dve, b, 0)
                expert_hidden(b, 1)
                block_output(b, 0)
                block_rows(b, range(TH, T))
                ln_o.half_moments(dve, b, 1)
                block_output(b, 1)

            input_rows(0)
            with dve.Fori(0, B - 1) as b:
                batch(b, False)
            batch(B - 1, True)

        @block.tensor
        def _(pe):
            for sig in (pv_done,):
                pe.sem_inc(sig.sem, sig.credit)
            pe.wait_ge(prepared, 5)

            def max_tile(b, i, head, q, done):
                slot, pair_of = head % HPI, (done - 1) % 2
                if q == 0:
                    pe.wait_ge(stack_loaded[slot].sem, stack_loaded[slot].at(b, 32 * (head // HPI + 1), i * 32))
                if done > 2:
                    pe.wait_ge(max_read.sem, max_read.at(b, done - 2, i * HPI * NM))
                for c in range(C):
                    mm = pe.matmul(banks[:, 2 * pair_of + c, :], q_stack[0:STACK, slot, P * q:P * q + P],
                                   k_stack[0:STACK, slot, HALF * c:HALF * c + HALF], start=True, stop=True)
                mm.then_inc(max_ready.sem, 1)

            def transpose_maxima(b, i, head, done, need):
                pe.wait_ge(max_read.sem, max_read.at(b, need, i * HPI * NM))
                pe.transpose(banks[0:T, 2 * ((done - 1) % 2), 0:P], maxima[:, head % 2, :], ident[:, :])\
                    .then_inc(max_ready.sem, 1)

            def transposed_scores(b, i, j, n):
                kt, c, slot = n // C, n % C, j
                if n == 0:
                    turn = 32 * (j // HPI + 1)
                    pe.wait_ge(shift_loaded[slot].sem, shift_loaded[slot].at(b, turn, i * 32))
                pe.wait_ge(exp_done.sem, exp_done.at(b, NST * j + n - 1, i * HPI * NST))
                rows = STACK + SHIFT_ROWS
                pe.matmul(banks[:, ST + n % 2, :], k_stack[0:rows, slot, P * kt:P * kt + P],
                          q_stack[0:rows, slot, HALF * c:HALF * c + HALF], start=True, stop=True)\
                    .then_inc(st_ready.sem, 1)

            def weigh_values(b, i, j, g):
                pe.wait_ge(exp_done.sem, exp_done.at(b, NST * j + 4 * g + 4, i * HPI * NST))
                if g == 0:
                    pe.wait_ge(vh_ready.sem, vh_ready.at(b, j + 1, i * HPI))
                    pe.wait_ge(o_copied.sem, o_copied.at(b, j - 1, i * HPI))
                for kt in (2 * g, 2 * g + 1):
                    for u in range(4):
                        first = QUARTER * (u % 2)
                        mm = pe.matmul(banks[VW * u:VW * u + VW, PV + j % 2, 0:QUARTER], vh[:, j % 2, kt, :],
                                       probs[:, C * kt + u // 2, first:first + QUARTER],
                                       start=kt == 0, stop=kt == T - 1)
                mm.then_inc(pv_done.sem, 1)

            def heads(b, i, last):
                for j in range(HPI):
                    base, more = RING_0 + NM * j, not (last and j >= HPI - 2)
                    for g in range(4):
                        tail = j == HPI - 1 and g == 3
                        transposed_scores(b, i, j, 4 * g)
                        if more:
                            max_tile(b, i, j + 2, 2 * g, base + m_index(2 * g) + 1)
                        transposed_scores(b, i, j, 4 * g + 1)
                        if g > 0:
                            weigh_values(b, i, j, g - 1)
                        elif j > 0:
                            weigh_values(b, i, j - 1, 3)
                        transposed_scores(b, i, j, 4 * g + 2)
                        if tail:
                            transposed_scores(b, i, j, 4 * g + 3)
                        if more:
                            max_tile(b, i, j + 2, 2 * g + 1, base + m_index(2 * g + 1) + 1)
                        if not tail:
                            transposed_scores(b, i, j, 4 * g + 3)
                        if g == 0 and not (last and j == HPI - 1):
                            transpose_maxima(b, i, j + 1, base + (3 if more else 1), base + (1 if more else 0))
                weigh_values(b, i, HPI - 1, 3)

            def project_attention(b, c):
                for t in range(TH * c, TH * c + TH):
                    q = t % TH
                    if q == 0:
                        pe.wait_ge(oT_lo.sem, oT_lo.at(b, C + c + 1))
                    for k in range(K):
                        mm = three_products(pe, banks[:, (X, Y)[c] + q, 0:D],
                                            [w[:, k, P * t:P * t + P] for w in oT], [m[:, k, :] for m in wo],
                                            k == 0, k == K - 1)
                    mm.then_inc(wo_ready.sem, 1)

            def expert_input(b, c):
                pe.wait_ge(x2_done.sem, x2_done.at(b, TH * (c + 1)))
                pe.wait_ge(m_normed.sem, m_normed.at(b, TH * (c + 1)))
                for k in range(K):
                    for q in range(TH):
                        mm = pe.transpose(banks[:, (X, Y)[c] + k, P * q:P * q + P],
                                          xn[:, TH * c + q, P * k:P * k + P], ident[:, :])
                    mm.then_inc(xfT_ready.sem, 1)
                pe.wait_ge(xf_done.sem, xf_done.at(b, K * (c + 1)))
                for k in range(K):
                    mm = pe.matmul(banks[0:NE, (X, Y)[c] + 2, :], wg[:, k, :], xf32[:, k, :], start=k == 0,
                                   stop=k == K - 1)
                mm.then_inc(gT_ready.sem, 1)

            def gate_rows(b, c):
                pe.wait_ge(gT_copied.sem, gT_copied.at(b, c + 1))
                if c > 0:
                    pe.wait_ge(up_done.sem, up_done.at(b, NE * c))
                pe.sem_inc(taken["pe"], 1)
                for q in range(TH):
                    mm = pe.transpose(banks[:, X + 3, NE * q:NE * q + NE], f32[0:NE, c, P * q:P * q + P],
                                      ident[0:NE, 0:NE])
                mm.then_inc(gate_ready.sem, 1)

            def weight_columns(b, c):
                pe.wait_ge(choose.sem, choose.at(b, STEPS * (c + 1)))
                pe.transpose(banks[0:TH * NE, X + 3, P:2 * P],
                             cw[:, TH * c:TH * c + TH, :].rearrange("p t e -> p (t e)"), ident[:, :])\
                    .then_inc(cwT_ready.sem, 1)

            def experts_up(b, c):
                for n in range(NE * c, NE * c + NE):
                    e = n % NE
                    if e == 0:
                        pe.wait_ge(xf_lo.sem, xf_lo.at(b, K * (c + 1)))
                        pe.wait_ge(gT_copied.sem, gT_copied.at(b, c + 1))
                    if e == 3:
                        pe.wait_ge(cwT_copied.sem, cwT_copied.at(b, c + 1))
                    if e >= 4:
                        pe.wait_ge(up_done.sem, up_done.at(b, n - 3))
                    for k in range(K):
                        mm = three_products(pe, banks[:, X + e % 4, :], [w[:, k, EH * e:EH * e + EH] for w in w1],
                                            [m[:, k, :] for m in xfT], k == 0, k == K - 1)
                    mm.then_inc(up_ready.sem, 1)

            def experts_down(b, c, tiles):
                for t in tiles:
                    q = t % TH
                    if q == 0:
                        pe.wait_ge(gT_copied.sem, gT_copied.at(b, C))
                        pe.wait_ge(xf_lo.sem, xf_lo.at(b, K * C))
                        if c > 0:
                            pe.wait_ge(y_done.sem, y_done.at(b, TH * c))
                    for e in range(NE):
                        if q == 0:
                            pe.wait_ge(up_lo.sem, up_lo.at(b, NE * c + e + 1))
                        mm = three_products(pe, banks[:, Y + q, 0:D], [h[:, e, P * q:P * q + P] for h in hidden],
                                            [w[:, e, :] for w in w2], e == 0, e == NE - 1)
                    mm.then_inc(down_ready.sem, 1)

            with pe.Fori(0, B) as b:
                for n in range(2 * K):
                    c, k = divmod(n, K)
                    if n == 0:
                        pe.wait_ge(up_done.sem, up_done.at(b, 0))
                    pe.wait_ge(a_normed.sem, a_normed.at(b, TH * c + TH))
                    for q in range(TH):
                        mm = pe.transpose(banks[:, X + n, P * q:P * q + P],
                                          v[:, TH * c + q, P * k:P * k + P], ident[:, :])
                    mm.then_inc(xT_ready.sem, 1)
                for n in range(NQ):
                    m, which, c = n // (2 * C), n // C % 2, n % C
                    if n == 0:
                        pe.wait_ge(y_done.sem, y_done.at(b, 0))
                    if n < C:
                        pe.wait_ge(f_lo.sem, f_lo.at(b, K * (n + 1)))
                    if n >= 4:
                        pe.wait_ge(rest_done.sem, rest_done.at(b, n - 3))
                    for k in range(K):
                        first = D * which + P * m
                        mm = three_products(pe, banks[:, Y + n % 4, :], [w[:, k, first:first + P] for w in wqk],
                                            [x[:, k, HALF * c:HALF * c + HALF] for x in xT], k == 0, k == K - 1)
                    mm.then_inc(qk_ready.sem, 1)
                for t in range(T):
                    max_tile(b, 0, 0, t, t + 1)
                    n, u = divmod(t, 2)
                    if u == 0:
                        pe.wait_ge(rest_done.sem, rest_done.at(b, NQ - 4 + n + 1))
                    for k in range(K):
                        mm = three_products(pe, banks[:, Y + n, D * u:D * u + D],
                                            [w[:, k, P * t:P * t + P] for w in xT], [m[:, k, :] for m in wv],
                                            k == 0, k == K - 1)
                    if u == 1:
                        mm.then_inc(v_ready.sem, 1)
                transpose_maxima(b, 0, 0, T + 1, T)
                for q in range(T):
                    max_tile(b, 0, 1, q, T + 1 + q + 1)
                pe.wait_ge(v_copied.sem, v_copied.at(b, T // 2))
                pe.sem_inc(taken["pe"], 1)
                with pe.Fori(0, NH // HPI - 1) as i:
                    heads(b, i, False)
                heads(b, NH // HPI - 1, True)
                pe.wait_ge(max_read.sem, max_read.at(b, NMT))
                pe.wait_ge(exp_done.sem, exp_done.at(b, NH * NST))
                pe.wait_ge(o_copied.sem, o_copied.at(b, NH))
                project_attention(b, 0)
                project_attention(b, 1)
                expert_input(b, 0)
                gate_rows(b, 0)
                weight_columns(b, 0)
                experts_up(b, 0)
                expert_input(b, 1)
                gate_rows(b, 1)
                experts_down(b, 0, (0, 1))
                weight_columns(b, 1)
                experts_down(b, 0, (2, 3))
                experts_up(b, 1)
                experts_down(b, 1, range(TH, T))


def build(nc, a, out):
    x = a["x"]
    x1 = nc.dram_tensor("x1_rows", [B, S, D], F32).ap()
    with ExitStack() as ctx:
        ident = ctx.enter_context(nc.sbuf_tensor("ident", [P, P], F32))
        mhalf = ctx.enter_context(nc.sbuf_tensor("minus_half", [P, 2 * T], F32))

        def rows(w):
            return w.rearrange("(k p) n -> p k n", p=P)

        def pair(inner, name, shape):
            return tuple(inner.enter_context(nc.sbuf_tensor(f"{name}_{part}", shape, F32R)) for part in ("hi", "lo"))

        with nc.cleanup_on_exit(), ExitStack() as inner:
            wqk, wv, w1 = (pair(inner, n, [P, K, w]) for n, w in (("wqk", 2 * D), ("wv", D), ("w1", D)))
            w2, w3 = pair(inner, "w2", [P, K, HID]), pair(inner, "w3", [P, M2, D])
            split_weights(nc, ident, mhalf, [(rows(a[n]), *w) for n, w in (("WqkT", wqk), ("WvT", wv), ("W1T", w1),
                                                                           ("W2T", w2), ("W3T", w3))])
            cosine_block(nc, inner, ident, mhalf, x, x1, (wqk, wv, w1, w2, w3), (a["bq"], a["bk"]), a["bv"],
                         a["b1"], a["b2"], a["b3"])
        with ExitStack() as inner:
            wqk, wv, wo = (pair(inner, n, [P, K, w]) for n, w in (("uqk", 2 * D), ("uv", D), ("uo", D)))
            w1, w2 = pair(inner, "u1", [P, K, NE * EH]), pair(inner, "u2", [P, NE, D])
            split_weights(nc, None, None, [(rows(a[n]), *w) for n, w in (("Uqk", wqk), ("Uv", wv), ("Uo", wo),
                                                                         ("U1", w1), ("U2", w2))])
            expert_block(nc, ident, mhalf, x1, out, (wqk, wv, wo, w1, w2), a["Ug"],
                         {n: a[f"f{n}"] for n in ("g1", "b1", "g2", "b2")})


def layout(inputs):
    import numpy as np

    a = {n.removeprefix("L0_attn_"): np.asarray(v) for n, v in inputs.items() if n.startswith("L0_attn_")}
    f = {n.removeprefix("L0_ffn_"): np.asarray(v) for n, v in inputs.items() if n.startswith("L0_ffn_")}
    arrays = {"x": a["x"], "WqkT": np.concatenate([a["Wq"].T, a["Wk"].T], axis=1)}
    arrays |= {f"W{n}T": a[f"W{n}"].T for n in "v123"}
    arrays |= {n: a[n].reshape(1, -1) for n in ("bq", "bk", "bv", "b3")}
    arrays |= {n: a[n].reshape(-1, P).T for n in ("b1", "b2")}
    arrays |= {"Uqk": np.concatenate([f["Wq"], f["Wk"]], axis=1), "Uv": f["Wv"], "Uo": f["Wo"], "Ug": f["Wg"]}
    arrays |= {"U1": f["W1"].transpose(1, 0, 2).reshape(D, -1), "U2": f["W2"].reshape(-1, D)}
    arrays |= {f"f{n}": f[n].reshape(-1, P).T for n in ("g1", "b1", "g2", "b2")}
    return {n: np.ascontiguousarray(v) for n, v in arrays.items()}


def kernel(**inputs):
    import concourse.bacc as bacc
    from concourse.bass_utils import run_bass_kernel_spmd

    nc = bacc.Bacc("TRN2", target_bir_lowering=False, num_devices=1)
    arrays = layout(inputs)
    aps = {n: nc.dram_tensor(f"in_{n}", v.shape, F32, kind="ExternalInput").ap() for n, v in arrays.items()}
    out = nc.dram_tensor("out", [B, S, D], F32, kind="ExternalOutput").ap()
    build(nc, aps, out)
    run = run_bass_kernel_spmd(nc, [{f"in_{n}": v for n, v in arrays.items()}], core_ids=[0])
    return run.results[0]["out"]
```

```python
from contextlib import ExitStack

import concourse.bass as bass
from concourse import mybir

ACT = mybir.ActivationFunctionType
ALU = mybir.AluOpType
AX = mybir.AxisListType
F32 = mybir.dt.float32
F32R = mybir.dt.float32r
BF16 = mybir.dt.bfloat16
U32 = mybir.dt.uint32

P = 128
B, S, D = 4, 1024, 256
HID = 1024
NH, DK = 16, 16
NE, EH = 8, 128
T = S // P
K = D // P
HALF = 512
C = S // HALF
TH = T // C
M2 = HID // P
LN_EPS = 1e-5
NORM_FLOOR = 1e-24
PARTS = 3
NPOS = 6
STACK = NPOS * DK
SHIFT_ROWS = 2
QUARTER = S // 4
HPI = 4
EARLY = NH - HPI
VW = 32
LAST_M = 9


class Signal:

    def __init__(self, ctx, nc, name, per, credit=0):
        self.sem, self.per, self.credit = nc.alloc_semaphore(name), per, credit

    def at(self, b, n, more=0):
        n += self.credit
        assert n > 0
        return b * self.per + more + n


def split_weights(nc, ident, mhalf, sources):
    with ExitStack() as ctx:
        stages = [ctx.enter_context(nc.sbuf_tensor(f"stage_{hi.name}", list(dram.shape), F32))
                  for dram, hi, lo in sources]
        loaded = [nc.alloc_semaphore(f"loaded_{hi.name}") for _, hi, _ in sources]
        hi_done = nc.alloc_semaphore(f"hi_done_from_{sources[0][1].name}")
        zeroed = nc.alloc_semaphore(f"ident_zeroed_{sources[0][1].name}")
        block = ctx.enter_context(nc.Block())

        @block.sync
        def _(sp):
            for (dram, hi, lo), stage, sem in zip(sources, stages, loaded):
                sp.dma_start(stage[:], dram).then_inc(sem, 16)

        @block.gpsimd
        def _(pool):
            if ident is not None:
                pool.memset(mhalf[:, :], -0.5)
                pool.memset(ident[:, :], 0.0).then_inc(zeroed, 1)
                pool.wait_ge(zeroed, 1)
                pool.affine_select(out=ident[:, :], in_=ident[:, :], compare_op=ALU.not_equal, fill=1.0,
                                   base=0, pattern=[[-1, P]], channel_multiplier=1)

        @block.scalar
        def _(act):
            for (dram, hi, lo), stage, sem in zip(sources, stages, loaded):
                act.wait_ge(sem, 16)
                act.activation(hi[:], stage[:], ACT.Copy).then_inc(hi_done, 1)

        @block.vector
        def _(dve):
            for n, ((dram, hi, lo), stage) in enumerate(zip(sources, stages)):
                dve.wait_ge(hi_done, n + 1)
                dve.tensor_tensor(lo[:], stage[:], hi[:].bitcast(F32), ALU.subtract)


class LayerNorm:

    def __init__(self, ctx, nc, name, mhalf):
        self.stats = ctx.enter_context(nc.sbuf_tensor(f"{name}_stats", [P, T, 6], F32))
        self.mean_var = ctx.enter_context(nc.sbuf_tensor(f"{name}_mean_var", [P, T, 2], F32))
        self.var_eps = ctx.enter_context(nc.sbuf_tensor(f"{name}_var_eps", [P, T], F32))
        self.rstd = ctx.enter_context(nc.sbuf_tensor(f"{name}_rstd", [P, T], F32))
        self.mhalf = mhalf
        self.stats_done = Signal(ctx, nc, f"{name}_stats_done", T)
        self.stats_seen = nc.alloc_semaphore(f"{name}_stats_seen")
        self.moments_done = Signal(ctx, nc, f"{name}_moments_done", T)
        self.eps_added = Signal(ctx, nc, f"{name}_eps_added", C)
        self.rstd_ready = Signal(ctx, nc, f"{name}_rstd_ready", C)

    def tile_stats(self, dve, b, t, src):
        dve.bn_stats(self.stats[:, t, :], src).then_inc(self.stats_done.sem, 1)

    def half_moments(self, dve, b, c):
        dve.wait_ge(self.stats_done.sem, self.stats_done.at(b, TH * c + TH))
        dve.sem_inc(self.stats_seen, 1)
        for t in range(TH * c, TH * c + TH):
            dve.bn_aggr(self.mean_var[:, t, :], self.stats[:, t, :]).then_inc(self.moments_done.sem, 1)
        dve.wait_ge(self.moments_done.sem, self.moments_done.at(b, TH * c + TH))
        dve.tensor_scalar(self.var_eps[:, TH * c:TH * c + TH], self.mean_var[:, TH * c:TH * c + TH, 1],
                          LN_EPS, None, ALU.add).then_inc(self.eps_added.sem, 1)

    def half_rstd(self, pool, b, c):
        pool.wait_ge(self.eps_added.sem, self.eps_added.at(b, c + 1))
        half = slice(TH * c, TH * c + TH)
        pool.tensor_tensor(self.rstd[:, half], self.var_eps[:, half], self.mhalf[:, 0:TH],
                           ALU.pow).then_inc(self.rstd_ready.sem, 1)

    def wait_rstd(self, eng, b, c):
        eng.wait_ge(self.rstd_ready.sem, self.rstd_ready.at(b, c + 1))

    def normalise(self, dve, t, dst, src):
        return dve.tensor_scalar(dst, src, self.mean_var[:, t, 0:1], self.rstd[:, t:t + 1],
                                 ALU.subtract, ALU.mult)


def three_products(pe, out, w, m, first, last):
    pe.matmul(out, w[0], m[0], start=first, stop=False)
    pe.matmul(out, w[0], m[1], start=False, stop=False)
    return pe.matmul(out, w[1], m[0], start=False, stop=last)


def cosine_block(nc, outer, ident, mhalf, x, x1, weights, b_qk, b_v, b_1, b_2, b_3):
    wqk, wv, w1, w2, w3 = weights
    with ExitStack() as ctx:
        def sb(name, shape, dt=F32):
            return ctx.enter_context(nc.sbuf_tensor(name, shape, dt))

        def signal(name, per, credit=0):
            return Signal(ctx, nc, name, per, credit)

        def pair(name, shape):
            return sb(f"{name}_hi", shape, F32R), sb(f"{name}_lo", shape, F32R)

        x_in = sb("x_in", [P, T, D])
        tok = sb("tok", [P, T, D])
        qk = sb("qk", [P, T, 2 * D])
        x_res = qk[:, 0:T // 2, :].rearrange("p t (u d) -> p (t u) d", u=2)
        xn = qk[:, T // 2:T, :].rearrange("p t (u d) -> p (t u) d", u=2)
        xT = pair("xT", [P, K, S])
        qT = pair("qT", [P, K, S])
        kT = pair("kT", [P, K, S])
        v = pair("v", [P, T, D + 2])
        wide = pair("wide", [P, M2, HALF])
        oT = pair("oT", [P, K, HALF])
        h1T = pair("h1T", [P, K, HALF])
        f32 = sb("f32", [P, 2, HALF])
        v32 = f32[:, :, :].rearrange("p n (u d) -> p n u d", u=2)
        bqk_row = sb("bqk_row", [P, 2 * D])
        bv_row = sb("bv_row", [P, 2, D])
        b3_row = sb("b3_row", [P, D])
        b1_col = sb("b1_col", [P, K])
        b2_col = sb("b2_col", [P, M2])
        squares = sb("squares", [P, 2, D])
        ssq = sb("ssq", [P, T, 2])
        ssq_floor = sb("ssq_floor", [P, T, 2])
        rnorm = sb("rnorm", [P, T, 2])
        rden = sb("rden", [P, T])
        banks = ctx.enter_context(nc.psum_tensor("banks", [P, 8, HALF], F32))
        X, Y = 0, 4

        ln_in = LayerNorm(ctx, nc, "ln_in", mhalf)
        ln_out = LayerNorm(ctx, nc, "ln_out", mhalf)
        consts = nc.alloc_semaphore("consts_loaded")
        ones_set = nc.alloc_semaphore("v_ones_set")
        x_loaded = [signal(f"x_loaded{c}", 16) for c in range(C)]
        xres_loaded = signal("xres_loaded", 16)
        x1_stored = [signal(f"x1_stored{c}", 16, 16) for c in range(C)]
        x_normed = signal("x_normed", T)
        xT_ready = signal("xT_ready", 2 * K)
        xT_hi = signal("xT_hi", 2 * K)
        xT_lo = signal("xT_lo", 2 * K)
        qk_ready = signal("qk_ready", T)
        qk_biased = signal("qk_biased", T)
        squared = signal("squared", 2 * T, 2)
        floored = signal("floored", C)
        rnorm_ready = signal("rnorm_ready", C)
        q_scaled = signal("q_scaled", T)
        v_ready = signal("v_ready", T // 2)
        v_biased = signal("v_biased", T // 2)
        v_hi = signal("v_hi", T // 2)
        v_lo = signal("v_lo", T // 4)
        v_lo_rest = signal("v_lo_rest", T // 4)
        qkT_ready = signal("qkT_ready", 4 * K)
        qkT_hi = signal("qkT_hi", 4 * K)
        qkT_lo = signal("qkT_lo", 4 * K)
        NF = 2 * (T + K + M2)
        tile_ready = signal("tile_ready", NF)
        f32_done = signal("f32_done", NF, NF)
        hi_done = signal("hi_done", NF)
        lo_done = signal("lo_done", NF, 2)
        o_ready = signal("o_ready", T)
        den_inverted = signal("den_inverted", T)
        o_done = signal("o_done", T)
        oT_ready = signal("oT_ready", 2 * K)
        oT_hi = signal("oT_hi", 2 * K)
        oT_lo = signal("oT_lo", 2 * K)
        h3_ready = signal("h3_ready", T)
        h3_biased = signal("h3_biased", T, T)
        h3_normed = signal("h3_normed", T)
        x1_done = signal("x1_done", T, T)
        CUT_P = [0, T]
        CUT_H1 = [2 * T, 2 * T + K + M2]
        CUT_H2 = [2 * T + K, 2 * T + 2 * K + M2]

        def bank_of(n):
            if n < 2 * T:
                return X + n % 4
            for c in range(C):
                if CUT_H1[c] <= n < CUT_H1[c] + K:
                    return Y + K + n - CUT_H1[c]
            return Y + (n - CUT_H2[0]) % 4 if n < CUT_H1[1] else X + (n - CUT_H2[1]) % 4

        xb = x.rearrange("b (t p) d -> b p t d", p=P)
        x1b = x1.rearrange("b (t p) d -> b p t d", p=P)
        block = ctx.enter_context(nc.Block())

        @block.sync
        def _(sp):
            for dst, src in ((bqk_row[:, 0:D], b_qk[0]), (bqk_row[:, D:2 * D], b_qk[1]), (bv_row[:, 0, :], b_v),
                             (bv_row[:, 1, :], b_v), (b3_row[:, :], b_3)):
                sp.dma_start(dst, src.to_broadcast([P, D])).then_inc(consts, 16)
            sp.dma_start(b1_col[:, :], b_1).then_inc(consts, 16)
            sp.dma_start(b2_col[:, :], b_2).then_inc(consts, 16)

            def load_x(b):
                for c in range(C):
                    sp.dma_start(x_in[:, TH * c:TH * c + TH, :], xb[b, :, TH * c:TH * c + TH, :])\
                        .then_inc(x_loaded[c].sem, 16)

            def batch(b, last):
                if not last:
                    sp.wait_ge(x_normed.sem, x_normed.at(b, T))
                    load_x(b + 1)
                sp.wait_ge(qkT_ready.sem, qkT_ready.at(b, 4 * K))
                sp.dma_start(x_res, xb[b]).then_inc(xres_loaded.sem, 16)
                for c in range(C):
                    sp.wait_ge(x1_done.sem, x1_done.at(b, TH * c + TH))
                    sp.dma_start(x1b[b, :, TH * c:TH * c + TH, :], tok[:, TH * c:TH * c + TH, :])\
                        .then_inc(x1_stored[c].sem, 16)

            load_x(0)
            with sp.Fori(0, B - 1) as b:
                batch(b, False)
            batch(B - 1, True)
            for c in range(C):
                sp.wait_ge(x1_stored[c].sem, x1_stored[c].at(B - 1, 16))

        @block.gpsimd
        def _(pool):
            for part, value in zip(v, (1.0, 0.0)):
                pool.memset(part[:, :, D:D + 2].bitcast(F32), value).then_inc(ones_set, 1)

            def batch(b, last):
                for c in range(C):
                    pool.wait_ge(floored.sem, floored.at(b, c + 1))
                    half = slice(TH * c, TH * c + TH)
                    pool.tensor_tensor(rnorm[:, half, :], ssq_floor[:, half, :],
                                       mhalf[:, 0:2 * TH].rearrange("p (t u) -> p t u", u=2),
                                       ALU.pow).then_inc(rnorm_ready.sem, 1)
                for n in range(T // 4, T // 2):
                    two = slice(2 * n, 2 * n + 2)
                    pool.wait_ge(v_hi.sem, v_hi.at(b, n + 1))
                    pool.tensor_tensor(v[1][:, two, 0:D], v32[:, n % 2, :, :], v[0][:, two, 0:D].bitcast(F32),
                                       ALU.subtract).then_inc(v_lo_rest.sem, 1)
                if not last:
                    for c in range(C):
                        ln_in.half_rstd(pool, b + 1, c)
                for c in range(C):
                    ln_out.half_rstd(pool, b, c)

            for c in range(C):
                ln_in.half_rstd(pool, 0, c)
            with pool.Fori(0, B - 1) as b:
                batch(b, False)
            batch(B - 1, True)

        @block.scalar
        def _(act):
            for sig in (squared,):
                act.sem_inc(sig.sem, sig.credit)
            act.sem_inc(f32_done.sem, f32_done.credit)
            act.wait_ge(consts, 16 * 7)

            def cut_hi(b, n, hi):
                act.wait_ge(f32_done.sem, f32_done.at(b, n + 1))
                act.activation(hi, f32[:, n % 2, :], ACT.Copy).then_inc(hi_done.sem, 1)

            def make(b, n, func, **kw):
                act.wait_ge(tile_ready.sem, tile_ready.at(b, n + 1))
                act.wait_ge(lo_done.sem, lo_done.at(b, n - 1))
                act.activation(f32[:, n % 2, :], banks[:, bank_of(n), :], func, **kw).then_inc(f32_done.sem, 1)

            def o_transposed_hi(b, c):
                for k in range(K):
                    act.wait_ge(oT_ready.sem, oT_ready.at(b, K * c + k + 1))
                    act.activation(oT[0][:, k, :], banks[:, Y + k, :], ACT.Copy).then_inc(oT_hi.sem, 1)

            def hidden_1(b, c):
                for m in range(K):
                    n = CUT_H1[c] + m
                    make(b, n, ACT.Relu, bias=b1_col[:, m:m + 1])
                    cut_hi(b, n, h1T[0][:, m, :])

            def hidden_2(b, c):
                for m in range(M2):
                    n = CUT_H2[c] + m
                    make(b, n, ACT.Relu, bias=b2_col[:, m:m + 1])
                    cut_hi(b, n, wide[0][:, m, :])

            def scale_q(b, c):
                act.wait_ge(rnorm_ready.sem, rnorm_ready.at(b, c + 1))
                act.wait_ge(squared.sem, squared.at(b, 2 * TH * (c + 1)))
                for t in range(TH * c, TH * c + TH):
                    act.activation(qk[:, t, 0:D], qk[:, t, 0:D], ACT.Copy, scale=rnorm[:, t, 0:1])\
                        .then_inc(q_scaled.sem, 1)

            def values_hi(b, n):
                act.wait_ge(v_biased.sem, v_biased.at(b, n + 1))
                act.activation(v[0][:, 2 * n:2 * n + 2, 0:D], v32[:, n % 2, :, :], ACT.Copy).then_inc(v_hi.sem, 1)

            def qk_transposed_hi(b, tiles):
                for n in tiles:
                    which, c, k = 1 - n // (C * K), n // K % 2, n % K
                    act.wait_ge(qkT_ready.sem, qkT_ready.at(b, n + 1))
                    dst = (qT, kT)[which][0]
                    act.activation(dst[:, k, HALF * c:HALF * c + HALF], banks[:, Y + n % 4, :], ACT.Copy)\
                        .then_inc(qkT_hi.sem, 1)

            def probabilities(b, c, tiles):
                for kt in tiles:
                    n = CUT_P[c] + kt
                    make(b, n, ACT.Exp, scale=rnorm[:, kt, 1:2])
                    cut_hi(b, n, wide[0][:, kt, :])

            with act.Fori(0, B) as b:
                for n in range(2 * K):
                    c, k = divmod(n, K)
                    act.wait_ge(xT_ready.sem, xT_ready.at(b, n + 1))
                    act.activation(xT[0][:, k, HALF * c:HALF * c + HALF], banks[:, X + n, :], ACT.Copy)\
                        .then_inc(xT_hi.sem, 1)
                for t in range(T):
                    act.wait_ge(qk_biased.sem, qk_biased.at(b, t + 1))
                    for u in range(2):
                        act.wait_ge(squared.sem, squared.at(b, 2 * t + u - 1))
                        act.activation(squares[:, u, :], qk[:, t, D * u:D * u + D], ACT.Square,
                                       accum_out=ssq[:, t, u:u + 1]).then_inc(squared.sem, 1)
                values_hi(b, 0)
                qk_transposed_hi(b, range(2 * K))
                values_hi(b, 1)
                scale_q(b, 0)
                values_hi(b, 2)
                qk_transposed_hi(b, range(2 * K, 3 * K))
                values_hi(b, 3)
                scale_q(b, 1)
                act.wait_ge(rnorm_ready.sem, rnorm_ready.at(b, C))
                act.wait_ge(v_lo.sem, v_lo.at(b, T // 4))
                act.wait_ge(v_lo_rest.sem, v_lo_rest.at(b, T // 4))
                probabilities(b, 0, range(T // 2))
                qk_transposed_hi(b, range(3 * K, 4 * K))
                probabilities(b, 0, range(T // 2, T))
                probabilities(b, 1, range(T))
                o_transposed_hi(b, 0)
                hidden_1(b, 0)
                hidden_2(b, 0)
                o_transposed_hi(b, 1)
                hidden_1(b, 1)
                hidden_2(b, 1)

        @block.vector
        def _(dve):
            for sig in (lo_done, h3_biased, x1_done):
                dve.sem_inc(sig.sem, sig.credit)
            for sig in x1_stored:
                dve.sem_inc(sig.sem, sig.credit)
            dve.wait_ge(consts, 16 * 7)

            def cut_lo(b, n, hi, lo):
                dve.wait_ge(hi_done.sem, hi_done.at(b, n + 1))
                dve.tensor_tensor(lo, f32[:, n % 2, :], hi.bitcast(F32), ALU.subtract).then_inc(lo_done.sem, 1)

            def attention_rows(b, c):
                for t in range(TH * c, TH * c + TH):
                    bank = banks[:, (Y, X)[c] + t % 4, :]
                    dve.wait_ge(o_ready.sem, o_ready.at(b, t + 1))
                    dve.reciprocal(rden[:, t:t + 1], bank[:, D:D + 1]).then_inc(den_inverted.sem, 1)
                    dve.wait_ge(den_inverted.sem, den_inverted.at(b, t + 1))
                    dve.tensor_scalar(tok[:, t, :], bank[:, 0:D], rden[:, t:t + 1], None, ALU.mult)\
                        .then_inc(o_done.sem, 1)

            def o_transposed_lo(b, c):
                for k in range(K):
                    dve.wait_ge(oT_hi.sem, oT_hi.at(b, K * c + k + 1))
                    dve.tensor_tensor(oT[1][:, k, :], banks[:, Y + k, :], oT[0][:, k, :].bitcast(F32),
                                      ALU.subtract).then_inc(oT_lo.sem, 1)

            def values_biased(b, n):
                dve.wait_ge(v_ready.sem, v_ready.at(b, n + 1))
                if n >= 2:
                    dve.wait_ge(v_lo.sem, v_lo.at(b, n - 1))
                dve.tensor_tensor(v32[:, n % 2, :, :], banks[:, X + n, :].rearrange("p (u d) -> p u d", u=2),
                                  bv_row[:, :, :], ALU.add).then_inc(v_biased.sem, 1)

            def values_lo(b, n):
                two = slice(2 * n, 2 * n + 2)
                dve.wait_ge(v_hi.sem, v_hi.at(b, n + 1))
                dve.tensor_tensor(v[1][:, two, 0:D], v32[:, n % 2, :, :], v[0][:, two, 0:D].bitcast(F32),
                                  ALU.subtract).then_inc(v_lo.sem, 1)

            def floor_norms(b, c):
                half = slice(TH * c, TH * c + TH)
                dve.wait_ge(squared.sem, squared.at(b, 2 * TH * (c + 1)))
                dve.tensor_scalar(ssq_floor[:, half, :], ssq[:, half, :], NORM_FLOOR, None, ALU.max)\
                    .then_inc(floored.sem, 1)

            def qk_transposed_lo(b, n):
                which, c, k = 1 - n // (C * K), n // K % 2, n % K
                half = slice(HALF * c, HALF * c + HALF)
                dst = (qT, kT)[which]
                dve.wait_ge(qkT_hi.sem, qkT_hi.at(b, n + 1))
                dve.tensor_tensor(dst[1][:, k, half], banks[:, Y + n % 4, :], dst[0][:, k, half].bitcast(F32),
                                  ALU.subtract).then_inc(qkT_lo.sem, 1)

            def cut_many(b, first, tiles, dst):
                for m in tiles:
                    cut_lo(b, first + m, dst[0][:, m, :], dst[1][:, m, :])

            def mlp_rows(b, c, tiles):
                for t in tiles:
                    dve.wait_ge(h3_ready.sem, h3_ready.at(b, t + 1))
                    dve.tensor_tensor(tok[:, t, :], banks[:, (X, Y)[c] + t % 4, 0:D], b3_row[:, :], ALU.add)\
                        .then_inc(h3_biased.sem, 1)
                    dve.wait_ge(h3_biased.sem, h3_biased.at(b, t + 1))
                    ln_out.tile_stats(dve, b, t, tok[:, t, :])

            def block_output(b, c):
                ln_out.wait_rstd(dve, b, c)
                if c == 0:
                    dve.wait_ge(xres_loaded.sem, xres_loaded.at(b, 16))
                for t in range(TH * c, TH * c + TH):
                    ln_out.normalise(dve, t, tok[:, t, :], tok[:, t, :]).then_inc(h3_normed.sem, 1)
                for t in range(TH * c, TH * c + TH):
                    dve.wait_ge(h3_normed.sem, h3_normed.at(b, t + 1))
                    dve.tensor_tensor(tok[:, t, :], tok[:, t, :], x_res[:, t, :], ALU.add)\
                        .then_inc(x1_done.sem, 1)

            def input_rows(b):
                for c in range(C):
                    dve.wait_ge(x_loaded[c].sem, x_loaded[c].at(b, 16))
                    for t in range(TH * c, TH * c + TH):
                        ln_in.tile_stats(dve, b, t, x_in[:, t, :])
                    ln_in.half_moments(dve, b, c)
                for c in range(C):
                    ln_in.wait_rstd(dve, b, c)
                    for t in range(TH * c, TH * c + TH):
                        ln_in.normalise(dve, t, xn[:, t, :], x_in[:, t, :]).then_inc(x_normed.sem, 1)

            def x_transposed_lo(b):
                for n in range(2 * K):
                    c, k = divmod(n, K)
                    half = slice(HALF * c, HALF * c + HALF)
                    dve.wait_ge(xT_hi.sem, xT_hi.at(b, n + 1))
                    dve.tensor_tensor(xT[1][:, k, half], banks[:, X + n, :], xT[0][:, k, half].bitcast(F32),
                                      ALU.subtract).then_inc(xT_lo.sem, 1)

            def batch(b, last):
                for t in range(T):
                    if t == 0:
                        dve.wait_ge(x1_done.sem, x1_done.at(b, 0))
                    dve.wait_ge(qk_ready.sem, qk_ready.at(b, t + 1))
                    dve.tensor_tensor(qk[:, t, :], banks[:, Y + t % 4, :], bqk_row[:, :], ALU.add)\
                        .then_inc(qk_biased.sem, 1)
                values_biased(b, 0)
                floor_norms(b, 0)
                floor_norms(b, 1)
                values_lo(b, 0)
                qk_transposed_lo(b, 0)
                qk_transposed_lo(b, 1)
                values_biased(b, 1)
                qk_transposed_lo(b, 2)
                values_biased(b, 2)
                qk_transposed_lo(b, 3)
                values_lo(b, 1)
                values_biased(b, 3)
                for n in range(2 * K, 3 * K):
                    qk_transposed_lo(b, n)
                cut_many(b, CUT_P[0], range(T // 2), wide)
                for n in range(3 * K, 4 * K):
                    qk_transposed_lo(b, n)
                cut_many(b, CUT_P[0], range(T // 2, T), wide)
                for c in range(C):
                    dve.wait_ge(x1_stored[c].sem, x1_stored[c].at(b, 0))
                attention_rows(b, 0)
                cut_many(b, CUT_P[1], range(T), wide)
                o_transposed_lo(b, 0)
                cut_many(b, CUT_H1[0], range(K), h1T)
                if not last:
                    input_rows(b + 1)
                attention_rows(b, 1)
                cut_many(b, CUT_H2[0], range(M2), wide)
                o_transposed_lo(b, 1)
                mlp_rows(b, 0, (0, 1))
                cut_many(b, CUT_H1[1], range(K), h1T)
                mlp_rows(b, 0, (2, 3))
                ln_out.half_moments(dve, b, 0)
                cut_many(b, CUT_H2[1], range(M2), wide)
                block_output(b, 0)
                mlp_rows(b, 1, range(TH, T))
                ln_out.half_moments(dve, b, 1)
                if not last:
                    x_transposed_lo(b + 1)
                block_output(b, 1)

            input_rows(0)
            x_transposed_lo(0)
            with dve.Fori(0, B - 1) as b:
                batch(b, False)
            batch(B - 1, True)

        @block.tensor
        def _(pe):
            pe.wait_ge(ones_set, 2)

            def values(b, n):
                for u in range(2):
                    t = 2 * n + u
                    for k in range(K):
                        mm = three_products(pe, banks[:, X + n, D * u:D * u + D],
                                            [w[:, k, P * t:P * t + P] for w in xT], [m[:, k, :] for m in wv],
                                            k == 0, k == K - 1)
                mm.then_inc(v_ready.sem, 1)

            def transpose_qk(b, tiles):
                for n in tiles:
                    which, c, k = 1 - n // (C * K), n // K % 2, n % K
                    if n == 0:
                        pe.wait_ge(qk_biased.sem, qk_biased.at(b, T))
                    if which == 0:
                        pe.wait_ge(q_scaled.sem, q_scaled.at(b, TH * (c + 1)))
                    if n >= 4:
                        pe.wait_ge(qkT_lo.sem, qkT_lo.at(b, n - 3))
                    for q in range(TH):
                        mm = pe.transpose(banks[:, Y + n % 4, P * q:P * q + P],
                                          qk[:, TH * c + q, D * which + P * k:D * which + P * k + P], ident[:, :])
                    mm.then_inc(qkT_ready.sem, 1)

            def scores(b, c, tiles):
                for kt in tiles:
                    n = CUT_P[c] + kt
                    bank = banks[:, bank_of(n), :]
                    if n >= 4:
                        pe.wait_ge(f32_done.sem, f32_done.at(b, n - 3))
                    if n == 0:
                        pe.wait_ge(v_biased.sem, v_biased.at(b, T // 2))
                    if kt == 0:
                        pe.wait_ge(qkT_lo.sem, qkT_lo.at(b, C * K + K * (c + 1)))
                    for k in range(K):
                        mm = three_products(pe, bank, [w[:, k, P * kt:P * kt + P] for w in kT],
                                            [m[:, k, HALF * c:HALF * c + HALF] for m in qT], k == 0, k == K - 1)
                    mm.then_inc(tile_ready.sem, 1)

            def attend(b, c):
                for t in range(TH * c, TH * c + TH):
                    bank = banks[:, (Y, X)[c] + t % 4, 0:D + 2]
                    if t == 0:
                        pe.wait_ge(v_lo.sem, v_lo.at(b, T // 4))
                        pe.wait_ge(v_lo_rest.sem, v_lo_rest.at(b, T // 4))
                        pe.wait_ge(qkT_lo.sem, qkT_lo.at(b, 4 * K))
                    if t == TH:
                        pe.wait_ge(f32_done.sem, f32_done.at(b, 2 * T))
                    for kt in range(T):
                        if t % TH == 0:
                            pe.wait_ge(lo_done.sem, lo_done.at(b, CUT_P[c] + kt + 1))
                        q = t % TH
                        mm = three_products(pe, bank, [w[:, kt, P * q:P * q + P] for w in wide],
                                            [m[:, kt, :] for m in v], kt == 0, kt == T - 1)
                    mm.then_inc(o_ready.sem, 1)

            def transpose_o(b, c):
                for k in range(K):
                    if c == 0:
                        pe.wait_ge(o_done.sem, o_done.at(b, TH))
                    else:
                        pe.wait_ge(o_done.sem, o_done.at(b, T))
                        pe.wait_ge(f32_done.sem, f32_done.at(b, CUT_H2[0] + M2))
                    for q in range(TH):
                        mm = pe.transpose(banks[:, Y + k, P * q:P * q + P],
                                          tok[:, TH * c + q, P * k:P * k + P], ident[:, :])
                    mm.then_inc(oT_ready.sem, 1)

            def hidden_1(b, c):
                for m in range(K):
                    for k in range(K):
                        pe.wait_ge(oT_lo.sem, oT_lo.at(b, K * c + k + 1))
                        mm = three_products(pe, banks[:, bank_of(CUT_H1[c] + m), :],
                                            [w[:, k, P * m:P * m + P] for w in w1], [o[:, k, :] for o in oT],
                                            k == 0, k == K - 1)
                    mm.then_inc(tile_ready.sem, 1)

            def hidden_2(b, c):
                for m in range(M2):
                    n = CUT_H2[c] + m
                    if m == 0 and c == 0:
                        pe.wait_ge(oT_lo.sem, oT_lo.at(b, K))
                        pe.wait_ge(f32_done.sem, f32_done.at(b, CUT_H1[0] + K))
                    if m < 4 and c == 1:
                        pe.wait_ge(h3_biased.sem, h3_biased.at(b, m + 1))
                    if m >= 4:
                        pe.wait_ge(f32_done.sem, f32_done.at(b, n - 3))
                    for k in range(K):
                        pe.wait_ge(lo_done.sem, lo_done.at(b, CUT_H1[c] + k + 1))
                        mm = three_products(pe, banks[:, bank_of(n), :], [w[:, k, P * m:P * m + P] for w in w2],
                                            [h[:, k, :] for h in h1T], k == 0, k == K - 1)
                    mm.then_inc(tile_ready.sem, 1)

            def mlp_out(b, c, tiles):
                for t in tiles:
                    bank, q = banks[:, (X, Y)[c] + t % 4, 0:D], t % TH
                    if t == 0:
                        pe.wait_ge(o_done.sem, o_done.at(b, T))
                    if t == TH:
                        pe.wait_ge(oT_lo.sem, oT_lo.at(b, 2 * K))
                        pe.wait_ge(f32_done.sem, f32_done.at(b, CUT_H1[1] + K))
                    for m in range(M2):
                        if q == 0:
                            pe.wait_ge(lo_done.sem, lo_done.at(b, CUT_H2[c] + m + 1))
                        mm = three_products(pe, bank, [h[:, m, P * q:P * q + P] for h in wide],
                                            [w[:, m, :] for w in w3], m == 0, m == M2 - 1)
                    mm.then_inc(h3_ready.sem, 1)

            with pe.Fori(0, B) as b:
                for n in range(2 * K):
                    c, k = divmod(n, K)
                    if n == 0:
                        pe.wait_ge(f32_done.sem, f32_done.at(b, 0))
                    pe.wait_ge(x_normed.sem, x_normed.at(b, TH * c + TH))
                    for q in range(TH):
                        mm = pe.transpose(banks[:, X + n, P * q:P * q + P],
                                          xn[:, TH * c + q, P * k:P * k + P], ident[:, :])
                    mm.then_inc(xT_ready.sem, 1)
                for t in range(T):
                    if t == 0:
                        pe.wait_ge(h3_biased.sem, h3_biased.at(b, 0))
                    if t % TH == 0:
                        pe.wait_ge(xT_lo.sem, xT_lo.at(b, K * (t // TH + 1)))
                    if t >= 4:
                        pe.wait_ge(qk_biased.sem, qk_biased.at(b, t - 3))
                    for k in range(K):
                        mm = three_products(pe, banks[:, Y + t % 4, :], [w[:, k, P * t:P * t + P] for w in xT],
                                            [m[:, k, :] for m in wqk], k == 0, k == K - 1)
                    mm.then_inc(qk_ready.sem, 1)
                values(b, 0)
                transpose_qk(b, range(2 * K))
                for n in range(1, T // 2):
                    values(b, n)
                transpose_qk(b, range(2 * K, 3 * K))
                scores(b, 0, range(T // 2))
                transpose_qk(b, range(3 * K, 4 * K))
                scores(b, 0, range(T // 2, T))
                attend(b, 0)
                scores(b, 1, range(T))
                transpose_o(b, 0)
                hidden_1(b, 0)
                attend(b, 1)
                hidden_2(b, 0)
                transpose_o(b, 1)
                mlp_out(b, 0, (0, 1))
                hidden_1(b, 1)
                mlp_out(b, 0, (2, 3))
                hidden_2(b, 1)
                mlp_out(b, 1, range(TH, T))


def expert_block(nc, ident, mhalf, x1, out, weights, wg_in, cols):
    wqk, wv, wo, w1, w2 = weights
    with ExitStack() as ctx:
        def sb(name, shape, dt=F32):
            return ctx.enter_context(nc.sbuf_tensor(name, shape, dt))

        def signal(name, per, credit=0):
            return Signal(ctx, nc, name, per, credit)

        def pair(name, shape):
            return sb(f"{name}_hi", shape, F32R), sb(f"{name}_lo", shape, F32R)

        z = sb("z", [P, T, D])
        z_next = sb("z_next", [P, T, D])
        xn = sb("xn", [P, T, D])
        cut = pair("cut", [P, NE * HALF])
        xT = [m[:, 0:K * S].rearrange("p (k s) -> p k s", k=K) for m in cut]
        oT = [m[:, K * S:2 * K * S].rearrange("p (k s) -> p k s", k=K) for m in cut]
        hidden = [m[:, :].rearrange("p (e s) -> p e s", e=NE) for m in cut]
        v = sb("v_rows", [P, T, D])
        vh = sb("v_head", [P, 2, T, VW])
        f32 = sb("f32_b", [P, 2, HALF])
        q_stack = sb("q_stack", [P, HPI, S], BF16)
        k_stack = sb("k_stack", [P, HPI, S], BF16)
        probs = sb("probs", [P, 2 * T, HALF])
        parts = probs[:, 0:2 * K * PARTS, :].bitcast(BF16).rearrange("p (n a) s -> p n a s", a=PARTS)
        cw_all = probs[:, 0:8, :].rearrange("p n s -> p (n s)")
        cw_row = probs[:, 8:16, :].rearrange("p n s -> p (n s)")
        o_out = sb("o_out", [P, 2, QUARTER])
        inv_out = sb("inv_out", [P, 2, QUARTER])
        early_den = sb("early_den", [EARLY * T, P])
        early_inv = sb("early_inv", [EARLY * T, P])
        o_num = sb("o_num", [P, K, S])
        o_inv = sb("o_inv", [P, K, S])
        xf32 = o_num[:, 0, :].rearrange("p (k s) -> p k s", k=K)
        gT = o_num[0:NE, 1, :].rearrange("p (c s) -> p c s", c=C)
        x_res = o_inv[:, :, :].rearrange("p k (t d) -> p (k t) d", d=D)
        xfT = pair("xfT", [P, K, HALF])
        maxima = sb("maxima", [P, 2, T])
        neg = sb("neg", [T, 2, P])
        neg_hi = sb("neg_hi", [T, 2, P], BF16)
        neg_lo = sb("neg_lo", [T, 2, P], BF16)
        wg = sb("wg", [P, K, NE])
        col = {n: sb(f"norm_{n}", [P, K]) for n in cols}
        lane = sb("lane", [P, TH, NE])
        gate = sb("gate", [P, T, NE])
        top = sb("top", [P, T, 8])
        top_at = sb("top_at", [P, T, 8], U32)
        top_lane = sb("top_lane", [P, T, 2])
        gap = sb("gap", [P, T])
        gap_exp = sb("gap_exp", [P, T])
        gap_sum = sb("gap_sum", [P, T])
        share = sb("share", [P, T, 2])
        picked = sb("picked", [P, 2, TH, NE])
        weighted = sb("weighted", [P, 2, TH, NE])
        cw = sb("cw", [P, T, NE])
        cwT = sb("cwT", [TH * NE, C, P])
        banks = ctx.enter_context(nc.psum_tensor("banks_b", [P, 8, HALF], F32))
        X, Y = 0, 4
        ST, PV = 4, 6

        q_dram = nc.dram_tensor("q_parts", [B, D, NPOS, S], BF16).ap()
        k_dram = nc.dram_tensor("k_parts", [B, D, NPOS, S], BF16).ap()
        o_dram = nc.dram_tensor("o_rows", [B, NH, VW, S], F32).ap()
        inv_dram = nc.dram_tensor("inv_rows", [B, NH, S], F32).ap()

        ln_z = LayerNorm(ctx, nc, "ln_z", mhalf)
        ln_a = LayerNorm(ctx, nc, "ln_a", mhalf)
        ln_m = LayerNorm(ctx, nc, "ln_m", mhalf)
        ln_o = LayerNorm(ctx, nc, "ln_o", mhalf)
        STEPS, STEP_GAP = 19, 6
        NST, NM, NMT = 2 * T, T + 1, NH * (T + 1)
        consts = nc.alloc_semaphore("b_consts_loaded")
        prepared = nc.alloc_semaphore("b_buffers_prepared")
        taken = {eng: nc.alloc_semaphore(f"wait_taken_{eng}") for eng in ("sp", "pool", "dve", "pe")}
        x1_loaded = [signal(f"b_x1_loaded{c}", 16) for c in range(C)]
        z_done = signal("z_done", T)
        a_normed = signal("a_normed", T)
        xT_ready = signal("b_xT_ready", 2 * K)
        f_done = signal("f_done", 2 * K)
        f_hi = signal("f_hi", 2 * K)
        f_lo = signal("f_lo", 2 * K, 2)
        NQ = 2 * K * C
        qk_ready = signal("b_qk_ready", NQ)
        part1_done = signal("part1_done", NQ)
        rest_done = signal("rest_done", NQ)
        part2_done = signal("part2_done", NQ)
        part3_done = signal("part3_done", NQ)
        parts_stored = signal("parts_stored", 16 * 3 * 2 * (K + 1))
        z_copied = signal("z_copied", 1)
        v_ready = signal("b_v_ready", T // 2)
        v_copied = signal("v_copied", T // 2)
        vh_ready = signal("vh_ready", NH)
        stack_loaded = [signal(f"stack_loaded{n}", 2 * 16 * NH // HPI) for n in range(HPI)]
        shift_loaded = [signal(f"shift_loaded{n}", 2 * 16 * NH // HPI, 32 * (n >= HPI - 2)) for n in range(HPI)]
        max_ready = signal("max_ready", NMT)
        max_read = signal("max_read", NMT, 2)
        neg_hi_done = signal("neg_hi_done", NH, 2)
        neg_lo_done = signal("neg_lo_done", NH, 2)
        st_ready = signal("st_ready", NH * NST)
        exp_done = signal("exp_done", NH * NST, 2)
        pv_done = signal("pv_done", 4 * NH, 8)
        o_copied = signal("o_copied", NH, 2)
        o_stored = [signal(f"o_stored{n}", 16 * NH // 2, 16) for n in range(2)]
        early_loaded = signal("early_loaded", 16)
        early_inverted = signal("early_inverted", 1)
        early_stored = signal("early_stored", 16)
        inverted = signal("inverted", HPI)
        inv_stored = [signal(f"inv_stored{n}", 16 * HPI // 2, 16) for n in range(2)]
        o_loaded = signal("o_loaded", 16 * 2 * K)
        o_normed = [signal(f"o_normed{k}", C) for k in range(K)]
        oT_hi = signal("b_oT_hi", K * C)
        oT_lo = signal("b_oT_lo", K * C)
        wo_ready = signal("wo_ready", T)
        x2_done = signal("x2_done", T)
        m_normed = signal("m_normed", T)
        xfT_ready = signal("xfT_ready", 2 * K)
        xf_done = signal("xf_done", 2 * K)
        xf_hi = signal("xf_hi", 2 * K)
        xf_lo = signal("xf_lo", 2 * K)
        gT_ready = signal("gT_ready", C)
        gT_copied = signal("gT_copied", C)
        gate_ready = signal("gate_ready", C)
        choose = signal("choose", STEPS * C)
        gap_exp_done = signal("gap_exp_done", C)
        cwT_ready = signal("cwT_ready", C)
        cwT_copied = signal("cwT_copied", C)
        cw_row_loaded = signal("cw_row_loaded", 16 * C)
        cw_spread = signal("cw_spread", C)
        up_ready = signal("up_ready", C * NE)
        up_done = signal("up_done", C * NE, C * NE)
        up_hi = signal("up_hi", C * NE)
        up_lo = signal("up_lo", C * NE)
        down_ready = signal("down_ready", T)
        y_done = signal("y_done", T, T)
        y_normed = signal("y_normed", T)
        out_done = signal("out_done", T)
        res_loaded = signal("res_loaded", 16)
        out_stored = [signal(f"out_stored{c}", 16, 16) for c in range(C)]

        x1b = x1.rearrange("b (t p) d -> b p t d", p=P)
        outb = out.rearrange("b (t p) d -> b p t d", p=P)

        def m_index(q):
            return q if q < 2 else q + 1

        LAG = 3
        RING_0 = 2 * T + 1
        block = ctx.enter_context(nc.Block())

        @block.sync
        def _(sp):
            for n in cols:
                sp.dma_start(col[n][:, :], cols[n]).then_inc(consts, 16)
            sp.dma_start(wg[:, :, :], wg_in.rearrange("(k p) e -> p k e", p=P)).then_inc(consts, 16)

            def load_x1(b):
                for c in range(C):
                    sp.dma_start(z_next[:, TH * c:TH * c + TH, :], x1b[b, :, TH * c:TH * c + TH, :])\
                        .then_inc(x1_loaded[c].sem, 16)

            def store_parts(b, m, which, rows):
                own = parts[rows, 2 * m + which, :, :]
                many_rows = rows.stop - rows.start
                sources = ((own, own[:, 0:2, :], own[:, 0:1, :]) if which else
                           (own[:, 0:1, :].to_broadcast([many_rows, 3, S]),
                            own[:, 1:2, :].to_broadcast([many_rows, 2, S]), own[:, 2:3, :]))
                sp.wait_ge(part3_done.sem, part3_done.at(b, (2 * m + which + 1) * C))
                for first, many, src in zip((0, 3, 5), (3, 2, 1), sources):
                    sp.dma_start((q_dram, k_dram)[which][b, P * m + rows.start:P * m + rows.stop,
                                                         first:first + many, :], src)\
                        .then_inc(parts_stored.sem, 16)

            def load_stack(b, slot, row):
                for stack, rows in ((q_stack, q_dram), (k_stack, k_dram)):
                    sp.dma_start(stack[0:STACK, slot, :], rows[b, bass.ds(row, DK), :, :]
                                 .rearrange("r a s -> (r a) s")).then_inc(stack_loaded[slot].sem, 16)

            def heads(b, i, last):
                for j in range(HPI):
                    if not last:
                        sp.wait_ge(st_ready.sem, st_ready.at(b, NST * (j + 1), i * HPI * NST))
                        sp.sem_inc(taken["sp"], 1)
                        load_stack(b, j, i * HPI * DK + (HPI + j) * DK)
                    sp.wait_ge(o_copied.sem, o_copied.at(b, j + 1, i * HPI))
                    sp.sem_inc(taken["sp"], 1)
                    sp.dma_start(o_dram[b, i * HPI + j].rearrange("d (u s) -> u d s", u=4), o_out[:, j % 2, :])\
                        .then_inc(o_stored[j % 2].sem, 16)
                    if last:
                        sp.wait_ge(inverted.sem, inverted.at(b, j + 1))
                        sp.sem_inc(taken["sp"], 1)
                        sp.dma_start(inv_dram[b, EARLY + j].rearrange("(u s) -> u s", u=4),
                                     inv_out[DK:P:VW, j % 2, :]).then_inc(inv_stored[j % 2].sem, 16)
                    if last and j == 0:
                        sp.wait_ge(early_inverted.sem, early_inverted.at(b, 1))
                        sp.sem_inc(taken["sp"], 1)
                        sp.dma_start(inv_dram[b, 0:EARLY].rearrange("h (c s) -> (h c) s", c=T), early_inv[:, :])\
                            .then_inc(early_stored.sem, 16)
                    if last and j == 1:
                        sp.wait_ge(early_stored.sem, early_stored.at(b, 16))
                        load_o(b, 0)

            def load_early_denominators(b):
                for u in range(2):
                    sp.wait_ge(o_stored[u].sem, o_stored[u].at(b, 16 * EARLY // 2))
                sp.sem_inc(taken["sp"], 1)
                sp.dma_start(early_den[:, :], o_dram[b, 0:EARLY, DK, :].rearrange("h (c s) -> h c s", c=T))\
                    .then_inc(early_loaded.sem, 16)

            def load_o(b, k):
                if k > 0:
                    for u in range(2):
                        sp.wait_ge(o_stored[u].sem, o_stored[u].at(b, 16 * NH // 2))
                        sp.wait_ge(inv_stored[u].sem, inv_stored[u].at(b, 16 * HPI // 2))
                sp.sem_inc(taken["sp"], 1)
                some = slice(NH // K * k, NH // K * (k + 1))
                sp.dma_start(o_num[:, k, :], o_dram[b, some, 0:DK, :]).then_inc(o_loaded.sem, 16)
                sp.dma_start(o_inv[:, k, :], inv_dram[b, some, :].rearrange("h (o s) -> h o s", o=1)
                             .to_broadcast([NH // K, DK, S]))\
                    .then_inc(o_loaded.sem, 16)

            def batch(b, last):
                for which in range(2):
                    store_parts(b, 0, which, slice(0, 2 * DK))
                sp.wait_ge(parts_stored.sem, parts_stored.at(b, 16 * 3 * 2))
                sp.sem_inc(taken["sp"], 1)
                for slot in range(2):
                    load_stack(b, slot, slot * DK)
                for which in range(2):
                    store_parts(b, 0, which, slice(2 * DK, P))
                for m in range(1, K):
                    for which in range(2):
                        store_parts(b, m, which, slice(0, P))
                sp.wait_ge(parts_stored.sem, parts_stored.at(b, 16 * 3 * 2 * (K + 1)))
                sp.sem_inc(taken["sp"], 1)
                for slot in range(2, HPI):
                    load_stack(b, slot, slot * DK)
                if not last:
                    sp.wait_ge(z_copied.sem, z_copied.at(b, 1))
                    sp.sem_inc(taken["sp"], 1)
                    load_x1(b + 1)
                with sp.Fori(0, NH // HPI - 1) as i:
                    heads(b, i, False)
                load_early_denominators(b)
                heads(b, NH // HPI - 1, True)
                load_o(b, 1)
                for k in range(K):
                    sp.wait_ge(o_normed[k].sem, o_normed[k].at(b, C))
                sp.dma_start(x_res, x1b[b]).then_inc(res_loaded.sem, 16)
                for c in range(C):
                    sp.wait_ge(cwT_copied.sem, cwT_copied.at(b, c + 1))
                    if c > 0:
                        sp.wait_ge(cw_spread.sem, cw_spread.at(b, c))
                    sp.dma_start(cw_row[0:1, :].rearrange("o (r p) -> o r p", p=P), cwT[:, c, :])\
                        .then_inc(cw_row_loaded.sem, 16)
                for c in range(C):
                    sp.wait_ge(out_done.sem, out_done.at(b, TH * c + TH))
                    sp.dma_start(outb[b, :, TH * c:TH * c + TH, :], xn[:, TH * c:TH * c + TH, :])\
                        .then_inc(out_stored[c].sem, 16)

            load_x1(0)
            with sp.Fori(0, B - 1) as b:
                batch(b, False)
            batch(B - 1, True)
            for c in range(C):
                sp.wait_ge(out_stored[c].sem, out_stored[c].at(B - 1, 16))

        @block.gpsimd
        def _(pool):
            for sig in (neg_hi_done, neg_lo_done):
                pool.sem_inc(sig.sem, sig.credit)
            pool.memset(q_stack[96:P, :, :], 0.0).then_inc(prepared, 1)
            pool.memset(k_stack[96:P, :, :], 1.0).then_inc(prepared, 1)
            pool.wait_ge(prepared, 2)
            pool.memset(vh[:, :, :, :], 1.0).then_inc(prepared, 1)
            pool.iota(lane[:, :, :], [[0, TH], [1, NE]], base=0, channel_multiplier=0,
                      allow_small_or_imprecise_dtypes=True).then_inc(prepared, 1)
            pool.memset(neg_hi[:, :, :], 0.0).then_inc(prepared, 1)
            pool.wait_ge(prepared, 5)
            for slot in range(HPI - 2, HPI):
                for row in (STACK, STACK + 1):
                    pool.dma_start(q_stack[row:row + 1, slot, :].rearrange("o (t p) -> o t p", p=P),
                                   neg_hi[:, slot % 2, :]).then_inc(shift_loaded[slot].sem, 16)

            def negate_max(b, i, j, ring):
                slot = j % HPI
                pool.wait_ge(max_read.sem, max_read.at(b, ring, i * HPI * NM))
                before, turn = (slot + 2) % HPI, (j - 2) // HPI + 1
                pool.wait_ge(shift_loaded[before].sem, shift_loaded[before].at(b, 32 * turn, i * 32))
                pool.sem_inc(taken["pool"], 1)
                pool.tensor_copy(neg_hi[:, j % 2, :], neg[:, j % 2, :]).then_inc(neg_hi_done.sem, 1)
                pool.wait_ge(neg_hi_done.sem, neg_hi_done.at(b, j + 1, i * HPI))
                pool.tensor_tensor(neg_lo[:, j % 2, :], neg[:, j % 2, :], neg_hi[:, j % 2, :],
                                   ALU.subtract).then_inc(neg_lo_done.sem, 1)
                pool.wait_ge(neg_lo_done.sem, neg_lo_done.at(b, j + 1, i * HPI))
                pool.sem_inc(taken["pool"], 1)
                for row, src in ((STACK, neg_hi), (STACK + 1, neg_lo)):
                    pool.dma_start(q_stack[row:row + 1, slot, :].rearrange("o (t p) -> o t p", p=P),
                                   src[:, j % 2, :]).then_inc(shift_loaded[slot].sem, 16)

            def head_values(b, i, j):
                pool.wait_ge(pv_done.sem, pv_done.at(b, 4 * (j - 1), i * HPI * 4))
                pool.sem_inc(taken["pool"], 1)
                first = i * HPI * DK + j * DK
                pool.tensor_copy(vh[:, j % 2, :, 0:DK], v[:, :, bass.ds(first, DK)]).then_inc(vh_ready.sem, 1)

            def heads(b, i, last):
                for j in range(HPI):
                    if not (last and j == HPI - 1):
                        done = RING_0 + NM * j + (3 if not (last and j == HPI - 2) else 1)
                        negate_max(b, i, j + 1, done)
                        head_values(b, i, j + 1)

            def normalise_o(b, k, c):
                half = slice(HALF * c, HALF * c + HALF)
                pool.wait_ge(o_loaded.sem, o_loaded.at(b, 16 * 2 * (k + 1)))
                pool.tensor_tensor(o_num[:, k, half], o_num[:, k, half], o_inv[:, k, half], ALU.mult)\
                    .then_inc(o_normed[k].sem, 1)

            def batch(b, last):
                negate_max(b, 0, 0, T + 1)
                pool.wait_ge(v_copied.sem, v_copied.at(b, T // 2))
                head_values(b, 0, 0)
                with pool.Fori(0, NH // HPI - 1) as i:
                    heads(b, i, False)
                heads(b, NH // HPI - 1, True)
                if not last:
                    for c in range(C):
                        ln_z.half_rstd(pool, b + 1, c)
                for c in range(C):
                    normalise_o(b, 0, c)
                if not last:
                    for c in range(C):
                        ln_a.half_rstd(pool, b + 1, c)
                for c in range(C):
                    ln_m.half_rstd(pool, b, c)
                for c in range(C):
                    pool.wait_ge(cw_row_loaded.sem, cw_row_loaded.at(b, 16 * (c + 1)))
                    if c > 0:
                        pool.wait_ge(up_done.sem, up_done.at(b, NE * c))
                    pool.sem_inc(taken["pool"], 1)
                    pool.partition_broadcast(cw_all, cw_row[0:1, :], channels=P).then_inc(cw_spread.sem, 1)
                for c in range(C):
                    ln_o.half_rstd(pool, b, c)

            for ln in (ln_z, ln_a):
                for c in range(C):
                    ln.half_rstd(pool, 0, c)
            with pool.Fori(0, B - 1) as b:
                batch(b, False)
            batch(B - 1, True)

        @block.scalar
        def _(act):
            for sig in (exp_done, o_copied, *o_stored):
                act.sem_inc(sig.sem, sig.credit)
            act.wait_ge(consts, 16 * (len(cols) + 1))

            def exponential(b, i, j, n):
                act.wait_ge(st_ready.sem, st_ready.at(b, NST * j + n + 1, i * HPI * NST))
                if n % 4 == 0:
                    act.wait_ge(pv_done.sem, pv_done.at(b, 4 * j + n // 4 - 3, i * HPI * 4))
                act.activation(probs[:, n, :], banks[:, ST + n % 2, :], ACT.Exp).then_inc(exp_done.sem, 1)

            def copy_o(b, i, j, last):
                act.wait_ge(pv_done.sem, pv_done.at(b, 4 * (j + 1), i * HPI * 4))
                act.wait_ge(o_stored[j % 2].sem, o_stored[j % 2].at(b, 16 * (j // 2), i * 16 * HPI // 2))
                if last and j >= 2:
                    act.wait_ge(inverted.sem, inverted.at(b, j - 1))
                act.activation(o_out[:, j % 2, :], banks[:, PV + j % 2, 0:QUARTER], ACT.Copy).then_inc(o_copied.sem, 1)

            def attention_hi(b, k):
                for c in range(C):
                    half = slice(HALF * c, HALF * c + HALF)
                    act.wait_ge(o_normed[k].sem, o_normed[k].at(b, c + 1))
                    act.activation(oT[0][:, k, half], o_num[:, k, half], ACT.Copy).then_inc(oT_hi.sem, 1)

            def heads(b, i, last):
                for j in range(HPI):
                    for n in range(NST):
                        exponential(b, i, j, n)
                        if n == C * LAG and j > 0:
                            copy_o(b, i, j - 1, last)
                        if last and j == HPI - 1 and n == 7:
                            attention_hi(b, 0)
                copy_o(b, i, HPI - 1, last)

            def expert_input_hi(b, c):
                for k in range(K):
                    act.wait_ge(xf_done.sem, xf_done.at(b, K * c + k + 1))
                    act.activation(xfT[0][:, k, :], xf32[:, k, :], ACT.Copy).then_inc(xf_hi.sem, 1)

            def expert_hidden_hi(b, c):
                for n in range(NE * c, NE * c + NE):
                    act.wait_ge(up_done.sem, up_done.at(b, n + 1))
                    act.activation(hidden[0][:, n % NE, :], f32[:, n % 2, :], ACT.Copy).then_inc(up_hi.sem, 1)

            with act.Fori(0, B) as b:
                for n in range(2 * K):
                    c, k = divmod(n, K)
                    act.wait_ge(xT_ready.sem, xT_ready.at(b, n + 1))
                    act.wait_ge(f_lo.sem, f_lo.at(b, n - 1))
                    act.activation(f32[:, n % 2, :], banks[:, X + n, :], ACT.Identity, bias=col["b1"][:, k:k + 1],
                                   scale=col["g1"][:, k:k + 1]).then_inc(f_done.sem, 1)
                    act.wait_ge(f_done.sem, f_done.at(b, n + 1))
                    act.activation(xT[0][:, k, HALF * c:HALF * c + HALF], f32[:, n % 2, :], ACT.Copy)\
                        .then_inc(f_hi.sem, 1)
                for n in range(NQ):
                    scale = DK ** -0.5 if n // C % 2 == 0 else 1.0
                    act.wait_ge(qk_ready.sem, qk_ready.at(b, n + 1))
                    half = slice(HALF * (n % C), HALF * (n % C) + HALF)
                    act.activation(parts[:, n // C, 0, half], banks[:, Y + n % 4, :], ACT.Copy, scale=scale)\
                        .then_inc(part1_done.sem, 1)
                    act.wait_ge(rest_done.sem, rest_done.at(b, n + 1))
                    act.activation(parts[:, n // C, 1, half], f32[:, n % 2, :], ACT.Copy).then_inc(part2_done.sem, 1)
                for n in range(T // 2):
                    act.wait_ge(v_ready.sem, v_ready.at(b, n + 1))
                    act.activation(v[:, 2 * n:2 * n + 2, :], banks[:, Y + n, :].rearrange("p (u d) -> p u d", u=2),
                                   ACT.Copy).then_inc(v_copied.sem, 1)
                act.wait_ge(y_done.sem, y_done.at(b, 0))
                act.activation(z[:, :, :], z_next[:, :, :], ACT.Copy).then_inc(z_copied.sem, 1)
                act.wait_ge(parts_stored.sem, parts_stored.at(b, 16 * 3 * 2 * (K + 1)))
                with act.Fori(0, NH // HPI - 1) as i:
                    heads(b, i, False)
                heads(b, NH // HPI - 1, True)
                attention_hi(b, 1)
                for c in range(C):
                    for k in range(K):
                        n = K * c + k
                        act.wait_ge(xfT_ready.sem, xfT_ready.at(b, n + 1))
                        if c > 0:
                            act.wait_ge(xf_lo.sem, xf_lo.at(b, K * c))
                        act.activation(xf32[:, k, :], banks[:, (X, Y)[c] + k, :], ACT.Identity,
                                       bias=col["b2"][:, k:k + 1], scale=col["g2"][:, k:k + 1]).then_inc(xf_done.sem, 1)
                    if c == 0:
                        expert_input_hi(b, 0)
                    act.wait_ge(gT_ready.sem, gT_ready.at(b, c + 1))
                    act.activation(gT[:, c, :], banks[0:NE, (X, Y)[c] + 2, :], ACT.Copy).then_inc(gT_copied.sem, 1)
                    act.wait_ge(choose.sem, choose.at(b, STEPS * c + STEP_GAP))
                    act.activation(gap_exp[:, TH * c:TH * c + TH], gap[:, TH * c:TH * c + TH], ACT.Exp)\
                        .then_inc(gap_exp_done.sem, 1)
                expert_hidden_hi(b, 0)
                act.wait_ge(up_ready.sem, up_ready.at(b, NE))
                expert_input_hi(b, 1)
                expert_hidden_hi(b, 1)

        @block.vector
        def _(dve):
            for sig in (f_lo, max_read, up_done, y_done, *inv_stored):
                dve.sem_inc(sig.sem, sig.credit)
            dve.wait_ge(consts, 16 * (len(cols) + 1))
            dve.wait_ge(prepared, 5)

            def negated_maxima(b, i, head, done):
                step = done - 1
                dve.wait_ge(max_ready.sem, max_ready.at(b, done, i * HPI * NM))
                dve.wait_ge(neg_lo_done.sem, neg_lo_done.at(b, head - 1, i * HPI))
                dve.tensor_scalar(neg[:, head % 2, :], banks[0:T, 2 * (step % 2), 0:P], -1.0, None, ALU.mult)\
                    .then_inc(max_read.sem, 1)

            def tile_maximum(b, i, head, q, done):
                step = done - 1
                dve.wait_ge(max_ready.sem, max_ready.at(b, done, i * HPI * NM))
                dve.tensor_reduce(maxima[:, head % 2, q:q + 1], banks[:, 2 * (step % 2):2 * (step % 2) + 2, :],
                                  AX.XY, ALU.max).then_inc(max_read.sem, 1)

            def invert(b, j):
                dve.wait_ge(o_copied.sem, o_copied.at(b, EARLY + j + 1))
                dve.wait_ge(inv_stored[j % 2].sem, inv_stored[j % 2].at(b, 16 * (j // 2)))
                dve.reciprocal(inv_out[:, j % 2, :], o_out[:, j % 2, :]).then_inc(inverted.sem, 1)

            def input_moments(b):
                for c in range(C):
                    dve.wait_ge(x1_loaded[c].sem, x1_loaded[c].at(b, 16))
                    for t in range(TH * c, TH * c + TH):
                        ln_z.tile_stats(dve, b, t, z_next[:, t, :])
                    ln_z.half_moments(dve, b, c)

            def heads(b, i, last, last_batch=False):
                for j in range(HPI):
                    base, more = RING_0 + NM * j, not (last and j >= HPI - 2)
                    for q in range(T):
                        if more:
                            tile_maximum(b, i, j + 2, q, base + m_index(q) + 1)
                        if q == 4 and last and j == 1:
                            invert(b, 0)
                        if q == 6 and last and j == 0:
                            dve.wait_ge(early_loaded.sem, early_loaded.at(b, 16))
                            dve.reciprocal(early_inv[:, :], early_den[:, :]).then_inc(early_inverted.sem, 1)
                        if q == 1 and not (last and j == HPI - 1):
                            negated_maxima(b, i, j + 1, base + (3 if more else 1))
                    if last and not last_batch and j == HPI - 3:
                        input_moments(b + 1)

            def normalise_o(b, k, c):
                half = slice(HALF * c, HALF * c + HALF)
                dve.wait_ge(o_loaded.sem, o_loaded.at(b, 16 * 2 * (k + 1)))
                dve.tensor_tensor(o_num[:, k, half], o_num[:, k, half], o_inv[:, k, half], ALU.mult)\
                    .then_inc(o_normed[k].sem, 1)

            def attention_lo(b, k, c):
                half = slice(HALF * c, HALF * c + HALF)
                dve.wait_ge(oT_hi.sem, oT_hi.at(b, C * k + c + 1))
                dve.tensor_tensor(oT[1][:, k, half], o_num[:, k, half], oT[0][:, k, half].bitcast(F32),
                                  ALU.subtract).then_inc(oT_lo.sem, 1)

            def input_rows(b):
                for c in range(C):
                    ln_z.wait_rstd(dve, b, c)
                    for t in range(TH * c, TH * c + TH):
                        ln_z.normalise(dve, t, z_next[:, t, :], z_next[:, t, :]).then_inc(z_done.sem, 1)
                    for t in range(TH * c, TH * c + TH):
                        dve.wait_ge(z_done.sem, z_done.at(b, t + 1))
                        ln_a.tile_stats(dve, b, t, z_next[:, t, :])
                    ln_a.half_moments(dve, b, c)
                for c in range(C):
                    ln_a.wait_rstd(dve, b, c)
                    for t in range(TH * c, TH * c + TH):
                        ln_a.normalise(dve, t, v[:, t, :], z_next[:, t, :]).then_inc(a_normed.sem, 1)

            def second_residual(b, c):
                for t in range(TH * c, TH * c + TH):
                    dve.wait_ge(wo_ready.sem, wo_ready.at(b, t + 1))
                    dve.tensor_tensor(z[:, t, :], banks[:, (X, Y)[c] + t % 4, 0:D], z[:, t, :], ALU.add)\
                        .then_inc(x2_done.sem, 1)
                    dve.wait_ge(x2_done.sem, x2_done.at(b, t + 1))
                    ln_m.tile_stats(dve, b, t, z[:, t, :])
                ln_m.half_moments(dve, b, c)

            def expert_input(b, c):
                ln_m.wait_rstd(dve, b, c)
                for t in range(TH * c, TH * c + TH):
                    ln_m.normalise(dve, t, xn[:, t, :], z[:, t, :]).then_inc(m_normed.sem, 1)

            def expert_input_lo(b, c):
                for k in range(K):
                    dve.wait_ge(xf_hi.sem, xf_hi.at(b, K * c + k + 1))
                    dve.tensor_tensor(xfT[1][:, k, :], xf32[:, k, :], xfT[0][:, k, :].bitcast(F32), ALU.subtract)\
                        .then_inc(xf_lo.sem, 1)

            def choose_experts(b, c):
                half, done = slice(TH * c, TH * c + TH), STEPS * c

                def after(step):
                    dve.wait_ge(choose.sem, choose.at(b, done + step))

                def step(instruction):
                    instruction.then_inc(choose.sem, 1)

                bank = banks[:, Y + 3, 0:TH * NE].rearrange("p (t e) -> p t e", e=NE)
                dve.wait_ge(gate_ready.sem, gate_ready.at(b, c + 1))
                step(dve.tensor_copy(gate[:, half, :], bank))
                after(1)
                dve.sem_inc(taken["dve"], 1)
                for t in range(TH * c, TH * c + TH):
                    step(dve.max(top[:, t, :], gate[:, t, :]))
                after(5)
                step(dve.tensor_tensor(gap[:, half], top[:, half, 1], top[:, half, 0], ALU.subtract))
                for t in range(TH * c, TH * c + TH):
                    step(dve.max_index(top_at[:, t, :], top[:, t, :], gate[:, t, :]))
                after(10)
                step(dve.tensor_copy(top_lane[:, half, :], top_at[:, half, 0:2]))
                dve.wait_ge(gap_exp_done.sem, gap_exp_done.at(b, c + 1))
                step(dve.tensor_scalar(gap_sum[:, half], gap_exp[:, half], 1.0, None, ALU.add))
                after(12)
                step(dve.reciprocal(share[:, half, 0], gap_sum[:, half]))
                after(13)
                step(dve.tensor_tensor(share[:, half, 1], gap_exp[:, half], share[:, half, 0], ALU.mult))
                for u in range(2):
                    step(dve.tensor_tensor(picked[:, u, :, :], lane[:, :, :],
                                           top_lane[:, half, u:u + 1].to_broadcast([P, TH, NE]), ALU.is_equal))
                after(16)
                for u in range(2):
                    step(dve.tensor_tensor(weighted[:, u, :, :], picked[:, u, :, :],
                                           share[:, half, u:u + 1].to_broadcast([P, TH, NE]), ALU.mult))
                after(18)
                step(dve.tensor_tensor(cw[:, half, :], weighted[:, 0, :, :], weighted[:, 1, :, :], ALU.add))

            def weights_out(b, c):
                dve.wait_ge(cwT_ready.sem, cwT_ready.at(b, c + 1))
                dve.tensor_copy(cwT[:, c, :], banks[0:TH * NE, Y + 3, P:2 * P]).then_inc(cwT_copied.sem, 1)

            def expert_hidden(b, c):
                weights = cw_all.rearrange("p (t e s) -> p t e s", t=TH, e=NE)
                for n in range(NE * c, NE * c + NE):
                    e = n % NE

                    def lo(n):
                        dve.wait_ge(up_hi.sem, up_hi.at(b, n + 1))
                        dve.tensor_tensor(hidden[1][:, n % NE, :], f32[:, n % 2, :], hidden[0][:, n % NE, :]
                                          .bitcast(F32), ALU.subtract).then_inc(up_lo.sem, 1)

                    if e == 0:
                        dve.wait_ge(cw_spread.sem, cw_spread.at(b, c + 1))
                    dve.wait_ge(up_ready.sem, up_ready.at(b, n + 1))
                    if n >= 2:
                        dve.wait_ge(up_lo.sem, up_lo.at(b, n - 1))
                    dve.scalar_tensor_tensor(
                        out=f32[:, n % 2, :].rearrange("p (t s) -> p t s", t=TH),
                        in0=banks[:, X + n % 4, :].rearrange("p (t s) -> p t s", t=TH), scalar=0.0,
                        in1=weights[:, :, e, :], op0=ALU.max, op1=ALU.mult).then_inc(up_done.sem, 1)
                    if e > 0:
                        lo(n - 1)
                lo(NE * c + NE - 1)

            def block_rows(b, tiles):
                for t in tiles:
                    dve.wait_ge(down_ready.sem, down_ready.at(b, t + 1))
                    dve.tensor_tensor(xn[:, t, :], banks[:, (X, Y)[t // TH] + t % 4, 0:D], z[:, t, :],
                                      ALU.add).then_inc(y_done.sem, 1)
                    dve.wait_ge(y_done.sem, y_done.at(b, t + 1))
                    ln_o.tile_stats(dve, b, t, xn[:, t, :])

            def block_output(b, c):
                ln_o.wait_rstd(dve, b, c)
                for t in range(TH * c, TH * c + TH):
                    ln_o.normalise(dve, t, xn[:, t, :], xn[:, t, :]).then_inc(y_normed.sem, 1)
                dve.wait_ge(res_loaded.sem, res_loaded.at(b, 16))
                for t in range(TH * c, TH * c + TH):
                    dve.wait_ge(y_normed.sem, y_normed.at(b, t + 1))
                    dve.tensor_tensor(xn[:, t, :], xn[:, t, :], x_res[:, t, :], ALU.add)\
                        .then_inc(out_done.sem, 1)

            for sig in out_stored:
                dve.sem_inc(sig.sem, sig.credit)

            def x_transposed_lo(b):
                for n in range(2 * K):
                    c, k = divmod(n, K)
                    half = slice(HALF * c, HALF * c + HALF)
                    dve.wait_ge(f_hi.sem, f_hi.at(b, n + 1))
                    dve.tensor_tensor(xT[1][:, k, half], f32[:, n % 2, :], xT[0][:, k, half].bitcast(F32),
                                      ALU.subtract).then_inc(f_lo.sem, 1)

            def batch(b, last):
                for n in range(NQ + 1):
                    if n < NQ:
                        scale = DK ** -0.5 if n // C % 2 == 0 else 1.0
                        if n < 2:
                            dve.wait_ge(f_lo.sem, f_lo.at(b, 2 * K))
                        else:
                            dve.wait_ge(part3_done.sem, part3_done.at(b, n - 1))
                        half = slice(HALF * (n % C), HALF * (n % C) + HALF)
                        dve.wait_ge(part1_done.sem, part1_done.at(b, n + 1))
                        dve.scalar_tensor_tensor(out=f32[:, n % 2, :], in0=banks[:, Y + n % 4, :], scalar=scale,
                                                 in1=parts[:, n // C, 0, half], op0=ALU.mult, op1=ALU.subtract)\
                            .then_inc(rest_done.sem, 1)
                    if n > 0:
                        own = parts[:, (n - 1) // C, :, HALF * ((n - 1) % C):HALF * ((n - 1) % C) + HALF]
                        dve.wait_ge(part2_done.sem, part2_done.at(b, n))
                        dve.tensor_tensor(own[:, 2, :], f32[:, (n - 1) % 2, :], own[:, 1, :], ALU.subtract)\
                            .then_inc(part3_done.sem, 1)
                for q in range(T):
                    tile_maximum(b, 0, 0, q, q + 1)
                negated_maxima(b, 0, 0, T + 1)
                for q in range(T):
                    tile_maximum(b, 0, 1, q, T + 1 + q + 1)
                with dve.Fori(0, NH // HPI - 1) as i:
                    heads(b, i, False)
                heads(b, NH // HPI - 1, True, last)
                invert(b, 1)
                if not last:
                    dve.wait_ge(vh_ready.sem, vh_ready.at(b, NH))
                    input_rows(b + 1)
                invert(b, HPI - 2)
                for c in range(C):
                    attention_lo(b, 0, c)
                invert(b, HPI - 1)
                for c in range(C):
                    normalise_o(b, 1, c)
                for c in range(C):
                    attention_lo(b, 1, c)
                for c in range(C):
                    dve.wait_ge(out_stored[c].sem, out_stored[c].at(b, 0))
                second_residual(b, 0)
                second_residual(b, 1)
                expert_input(b, 0)
                expert_input(b, 1)
                expert_input_lo(b, 0)
                for c in range(C):
                    choose_experts(b, c)
                    weights_out(b, c)
                expert_hidden(b, 0)
                expert_input_lo(b, 1)
                block_rows(b, range(TH))
                ln_o.half_moments(dve, b, 0)
                expert_hidden(b, 1)
                block_output(b, 0)
                block_rows(b, range(TH, T))
                ln_o.half_moments(dve, b, 1)
                if not last:
                    x_transposed_lo(b + 1)
                block_output(b, 1)

            input_moments(0)
            input_rows(0)
            x_transposed_lo(0)
            with dve.Fori(0, B - 1) as b:
                batch(b, False)
            batch(B - 1, True)

        @block.tensor
        def _(pe):
            for sig in (pv_done,):
                pe.sem_inc(sig.sem, sig.credit)
            pe.wait_ge(prepared, 5)

            def max_tile(b, i, head, q, done):
                slot, pair_of = head % HPI, (done - 1) % 2
                if q == 0:
                    pe.wait_ge(stack_loaded[slot].sem, stack_loaded[slot].at(b, 32 * (head // HPI + 1), i * 32))
                if done > 2:
                    pe.wait_ge(max_read.sem, max_read.at(b, done - 2, i * HPI * NM))
                for c in range(C):
                    mm = pe.matmul(banks[:, 2 * pair_of + c, :], q_stack[0:STACK, slot, P * q:P * q + P],
                                   k_stack[0:STACK, slot, HALF * c:HALF * c + HALF], start=True, stop=True)
                mm.then_inc(max_ready.sem, 1)

            def transpose_maxima(b, i, head, done, need):
                pe.wait_ge(max_read.sem, max_read.at(b, need, i * HPI * NM))
                pe.transpose(banks[0:T, 2 * ((done - 1) % 2), 0:P], maxima[:, head % 2, :], ident[:, :])\
                    .then_inc(max_ready.sem, 1)

            def transposed_scores(b, i, j, n):
                kt, c, slot = n // C, n % C, j
                if n == 0:
                    turn = 32 * (j // HPI + 1)
                    pe.wait_ge(shift_loaded[slot].sem, shift_loaded[slot].at(b, turn, i * 32))
                pe.wait_ge(exp_done.sem, exp_done.at(b, NST * j + n - 1, i * HPI * NST))
                rows = STACK + SHIFT_ROWS
                pe.matmul(banks[:, ST + n % 2, :], k_stack[0:rows, slot, P * kt:P * kt + P],
                          q_stack[0:rows, slot, HALF * c:HALF * c + HALF], start=True, stop=True)\
                    .then_inc(st_ready.sem, 1)

            def weigh_values(b, i, j, kt):
                if kt % 2 == 0:
                    pe.wait_ge(exp_done.sem, exp_done.at(b, NST * j + C * (kt + 2), i * HPI * NST))
                if kt == 0:
                    pe.wait_ge(vh_ready.sem, vh_ready.at(b, j + 1, i * HPI))
                    pe.wait_ge(o_copied.sem, o_copied.at(b, j - 1, i * HPI))
                for u in range(4):
                    first = QUARTER * (u % 2)
                    mm = pe.matmul(banks[VW * u:VW * u + VW, PV + j % 2, 0:QUARTER], vh[:, j % 2, kt, :],
                                   probs[:, C * kt + u // 2, first:first + QUARTER], start=kt == 0, stop=kt == T - 1)
                if kt % 2 == 1:
                    mm.then_inc(pv_done.sem, 1)

            def heads(b, i, last):
                for j in range(HPI):
                    base, more = RING_0 + NM * j, not (last and j >= HPI - 2)
                    for kt in range(T):
                        tail = j == HPI - 1 and kt == T - 1
                        transposed_scores(b, i, j, C * kt)
                        if tail:
                            transposed_scores(b, i, j, C * kt + 1)
                        if more:
                            max_tile(b, i, j + 2, kt, base + m_index(kt) + 1)
                        if not tail:
                            transposed_scores(b, i, j, C * kt + 1)
                        if kt >= LAG:
                            weigh_values(b, i, j, kt - LAG)
                        elif j > 0:
                            weigh_values(b, i, j - 1, T + kt - LAG)
                        if kt == 1 and not (last and j == HPI - 1):
                            transpose_maxima(b, i, j + 1, base + (3 if more else 1), base + (1 if more else 0))
                for kt in range(T - LAG, T):
                    weigh_values(b, i, HPI - 1, kt)

            def project_attention(b, c):
                for t in range(TH * c, TH * c + TH):
                    q = t % TH
                    if q == 0:
                        pe.wait_ge(oT_lo.sem, oT_lo.at(b, C + c + 1))
                    for k in range(K):
                        mm = three_products(pe, banks[:, (X, Y)[c] + q, 0:D],
                                            [w[:, k, P * t:P * t + P] for w in oT], [m[:, k, :] for m in wo],
                                            k == 0, k == K - 1)
                    mm.then_inc(wo_ready.sem, 1)

            def expert_input(b, c):
                pe.wait_ge(x2_done.sem, x2_done.at(b, TH * (c + 1)))
                pe.wait_ge(m_normed.sem, m_normed.at(b, TH * (c + 1)))
                for k in range(K):
                    for q in range(TH):
                        mm = pe.transpose(banks[:, (X, Y)[c] + k, P * q:P * q + P],
                                          xn[:, TH * c + q, P * k:P * k + P], ident[:, :])
                    mm.then_inc(xfT_ready.sem, 1)
                pe.wait_ge(xf_done.sem, xf_done.at(b, K * (c + 1)))
                for k in range(K):
                    mm = pe.matmul(banks[0:NE, (X, Y)[c] + 2, :], wg[:, k, :], xf32[:, k, :], start=k == 0,
                                   stop=k == K - 1)
                mm.then_inc(gT_ready.sem, 1)

            def gate_rows(b, c):
                pe.wait_ge(gT_copied.sem, gT_copied.at(b, c + 1))
                if c == 0:
                    pe.wait_ge(x2_done.sem, x2_done.at(b, T))
                else:
                    pe.wait_ge(cwT_copied.sem, cwT_copied.at(b, c))
                pe.sem_inc(taken["pe"], 1)
                for q in range(TH):
                    mm = pe.transpose(banks[:, Y + 3, NE * q:NE * q + NE], gT[:, c, P * q:P * q + P],
                                      ident[0:NE, 0:NE])
                mm.then_inc(gate_ready.sem, 1)

            def weight_columns(b, c):
                pe.wait_ge(choose.sem, choose.at(b, STEPS * (c + 1)))
                pe.transpose(banks[0:TH * NE, Y + 3, P:2 * P],
                             cw[:, TH * c:TH * c + TH, :].rearrange("p t e -> p (t e)"), ident[:, :])\
                    .then_inc(cwT_ready.sem, 1)

            def experts_up(b, c, experts):
                for e in experts:
                    n = NE * c + e
                    if e == 0:
                        pe.wait_ge(xf_lo.sem, xf_lo.at(b, K * (c + 1)))
                    if e == 2 and c == 0:
                        pe.wait_ge(gT_copied.sem, gT_copied.at(b, 1))
                    if e >= 4:
                        pe.wait_ge(up_done.sem, up_done.at(b, n - 3))
                    elif c > 0:
                        pe.wait_ge(y_done.sem, y_done.at(b, e + 1))
                    for k in range(K):
                        mm = three_products(pe, banks[:, X + e % 4, :], [w[:, k, EH * e:EH * e + EH] for w in w1],
                                            [m[:, k, :] for m in xfT], k == 0, k == K - 1)
                    mm.then_inc(up_ready.sem, 1)

            def experts_down(b, c):
                for t in range(TH * c, TH * c + TH):
                    q = t % TH
                    if c == 0:
                        pe.wait_ge(up_done.sem, up_done.at(b, NE - TH + q + 1))
                    elif q == 0:
                        pe.wait_ge(xf_done.sem, xf_done.at(b, K * C))
                        pe.wait_ge(gT_copied.sem, gT_copied.at(b, C))
                        pe.wait_ge(cwT_copied.sem, cwT_copied.at(b, C))
                    for e in range(NE):
                        if q == 0:
                            pe.wait_ge(up_lo.sem, up_lo.at(b, NE * c + e + 1))
                        mm = three_products(pe, banks[:, (X, Y)[c] + q, 0:D], [h[:, e, P * q:P * q + P] for h in hidden],
                                            [w[:, e, :] for w in w2], e == 0, e == NE - 1)
                    mm.then_inc(down_ready.sem, 1)

            with pe.Fori(0, B) as b:
                for n in range(2 * K):
                    c, k = divmod(n, K)
                    if n == 0:
                        pe.wait_ge(up_done.sem, up_done.at(b, 0))
                    pe.wait_ge(a_normed.sem, a_normed.at(b, TH * c + TH))
                    for q in range(TH):
                        mm = pe.transpose(banks[:, X + n, P * q:P * q + P],
                                          v[:, TH * c + q, P * k:P * k + P], ident[:, :])
                    mm.then_inc(xT_ready.sem, 1)
                for n in range(NQ):
                    m, which, c = n // (2 * C), n // C % 2, n % C
                    if n == 0:
                        pe.wait_ge(y_done.sem, y_done.at(b, 0))
                    if n < C:
                        pe.wait_ge(f_lo.sem, f_lo.at(b, K * (n + 1)))
                    if n >= 4:
                        pe.wait_ge(rest_done.sem, rest_done.at(b, n - 3))
                    for k in range(K):
                        first = D * which + P * m
                        mm = three_products(pe, banks[:, Y + n % 4, :], [w[:, k, first:first + P] for w in wqk],
                                            [x[:, k, HALF * c:HALF * c + HALF] for x in xT], k == 0, k == K - 1)
                    mm.then_inc(qk_ready.sem, 1)
                for t in range(T):
                    max_tile(b, 0, 0, t, t + 1)
                    n, u = divmod(t, 2)
                    if u == 0:
                        pe.wait_ge(rest_done.sem, rest_done.at(b, NQ - 4 + n + 1))
                    for k in range(K):
                        mm = three_products(pe, banks[:, Y + n, D * u:D * u + D],
                                            [w[:, k, P * t:P * t + P] for w in xT], [m[:, k, :] for m in wv],
                                            k == 0, k == K - 1)
                    if u == 1:
                        mm.then_inc(v_ready.sem, 1)
                transpose_maxima(b, 0, 0, T + 1, T)
                for q in range(T):
                    max_tile(b, 0, 1, q, T + 1 + q + 1)
                pe.wait_ge(v_copied.sem, v_copied.at(b, T // 2))
                pe.sem_inc(taken["pe"], 1)
                with pe.Fori(0, NH // HPI - 1) as i:
                    heads(b, i, False)
                heads(b, NH // HPI - 1, True)
                pe.wait_ge(max_read.sem, max_read.at(b, NMT))
                pe.wait_ge(exp_done.sem, exp_done.at(b, NH * NST))
                pe.wait_ge(o_copied.sem, o_copied.at(b, NH))
                project_attention(b, 0)
                project_attention(b, 1)
                expert_input(b, 0)
                experts_up(b, 0, (0,))
                gate_rows(b, 0)
                experts_up(b, 0, (1, 2))
                weight_columns(b, 0)
                expert_input(b, 1)
                experts_up(b, 0, (3,))
                gate_rows(b, 1)
                weight_columns(b, 1)
                experts_up(b, 0, range(4, NE))
                experts_down(b, 0)
                experts_up(b, 1, range(NE))
                experts_down(b, 1)


def build(nc, a, out):
    x = a["x"]
    x1 = nc.dram_tensor("x1_rows", [B, S, D], F32).ap()
    with ExitStack() as ctx:
        ident = ctx.enter_context(nc.sbuf_tensor("ident", [P, P], F32))
        mhalf = ctx.enter_context(nc.sbuf_tensor("minus_half", [P, 2 * T], F32))

        def rows(w):
            return w.rearrange("(k p) n -> p k n", p=P)

        def pair(inner, name, shape):
            return tuple(inner.enter_context(nc.sbuf_tensor(f"{name}_{part}", shape, F32R)) for part in ("hi", "lo"))

        with nc.cleanup_on_exit(), ExitStack() as inner:
            wqk, wv, w1 = (pair(inner, n, [P, K, w]) for n, w in (("wqk", 2 * D), ("wv", D), ("w1", D)))
            w2, w3 = pair(inner, "w2", [P, K, HID]), pair(inner, "w3", [P, M2, D])
            split_weights(nc, ident, mhalf, [(rows(a[n]), *w) for n, w in (("WqkT", wqk), ("WvT", wv), ("W1T", w1),
                                                                           ("W2T", w2), ("W3T", w3))])
            cosine_block(nc, inner, ident, mhalf, x, x1, (wqk, wv, w1, w2, w3), (a["bq"], a["bk"]), a["bv"],
                         a["b1"], a["b2"], a["b3"])
        with ExitStack() as inner:
            wqk, wv, wo = (pair(inner, n, [P, K, w]) for n, w in (("uqk", 2 * D), ("uv", D), ("uo", D)))
            w1, w2 = pair(inner, "u1", [P, K, NE * EH]), pair(inner, "u2", [P, NE, D])
            split_weights(nc, None, None, [(rows(a[n]), *w) for n, w in (("Uqk", wqk), ("Uv", wv), ("Uo", wo),
                                                                         ("U1", w1), ("U2", w2))])
            expert_block(nc, ident, mhalf, x1, out, (wqk, wv, wo, w1, w2), a["Ug"],
                         {n: a[f"f{n}"] for n in ("g1", "b1", "g2", "b2")})


def layout(inputs):
    import numpy as np

    a = {n.removeprefix("L0_attn_"): np.asarray(v) for n, v in inputs.items() if n.startswith("L0_attn_")}
    f = {n.removeprefix("L0_ffn_"): np.asarray(v) for n, v in inputs.items() if n.startswith("L0_ffn_")}
    arrays = {"x": a["x"], "WqkT": np.concatenate([a["Wq"].T, a["Wk"].T], axis=1)}
    arrays |= {f"W{n}T": a[f"W{n}"].T for n in "v123"}
    arrays |= {n: a[n].reshape(1, -1) for n in ("bq", "bk", "bv", "b3")}
    arrays |= {n: a[n].reshape(-1, P).T for n in ("b1", "b2")}
    arrays |= {"Uqk": np.concatenate([f["Wq"], f["Wk"]], axis=1), "Uv": f["Wv"], "Uo": f["Wo"], "Ug": f["Wg"]}
    arrays |= {"U1": f["W1"].transpose(1, 0, 2).reshape(D, -1), "U2": f["W2"].reshape(-1, D)}
    arrays |= {f"f{n}": f[n].reshape(-1, P).T for n in ("g1", "b1", "g2", "b2")}
    return {n: np.ascontiguousarray(v) for n, v in arrays.items()}


def kernel(**inputs):
    import concourse.bacc as bacc
    from concourse.bass_utils import run_bass_kernel_spmd

    nc = bacc.Bacc("TRN2", target_bir_lowering=False, num_devices=1)
    arrays = layout(inputs)
    aps = {n: nc.dram_tensor(f"in_{n}", v.shape, F32, kind="ExternalInput").ap() for n, v in arrays.items()}
    out = nc.dram_tensor("out", [B, S, D], F32, kind="ExternalOutput").ap()
    build(nc, aps, out)
    run = run_bass_kernel_spmd(nc, [{f"in_{n}": v for n, v in arrays.items()}], core_ids=[0])
    return run.results[0]["out"]
```

```python
from contextlib import ExitStack

import concourse.bass as bass
from concourse import mybir

ACT = mybir.ActivationFunctionType
ALU = mybir.AluOpType
AX = mybir.AxisListType
F32 = mybir.dt.float32
F32R = mybir.dt.float32r
BF16 = mybir.dt.bfloat16
U32 = mybir.dt.uint32

P = 128
B, S, D = 4, 1024, 256
HID = 1024
NH, DK = 16, 16
NE, EH = 8, 128
T = S // P
K = D // P
HALF = 512
C = S // HALF
TH = T // C
M2 = HID // P
LN_EPS = 1e-5
NORM_FLOOR = 1e-24
PARTS = 3
NPOS = 6
STACK = NPOS * DK
SHIFT_ROWS = 2
QUARTER = S // 4
HPI = 4
EARLY = NH - HPI
VW = 32


class Signal:

    def __init__(self, ctx, nc, name, per, credit=0):
        self.sem, self.per, self.credit = nc.alloc_semaphore(name), per, credit

    def at(self, b, n, more=0):
        n += self.credit
        assert n > 0
        return b * self.per + more + n


class Weights:

    def __init__(self, nc, name, sources):
        self.sources = sources
        self.loaded = [nc.alloc_semaphore(f"{name}_loaded{n}") for n in range(len(sources))]
        self.hi_done = nc.alloc_semaphore(f"{name}_hi_done")
        self.lo_done = nc.alloc_semaphore(f"{name}_lo_done")

    def load(self, sp, n):
        dram, stage, _, _ = self.sources[n]
        sp.dma_start(stage, dram).then_inc(self.loaded[n], 16)

    def cut_hi(self, act, n):
        _, stage, hi, _ = self.sources[n]
        act.wait_ge(self.loaded[n], 16)
        act.activation(hi[:], stage, ACT.Copy).then_inc(self.hi_done, 1)

    def cut_lo(self, dve, n):
        _, stage, hi, lo = self.sources[n]
        dve.wait_ge(self.hi_done, n + 1)
        dve.tensor_tensor(lo[:], stage, hi[:].bitcast(F32), ALU.subtract).then_inc(self.lo_done, 1)

    def wait(self, eng, n):
        eng.wait_ge(self.lo_done, n + 1)


class LayerNorm:

    def __init__(self, ctx, nc, name, mhalf):
        self.stats = ctx.enter_context(nc.sbuf_tensor(f"{name}_stats", [P, T, 6], F32))
        self.mean_var = ctx.enter_context(nc.sbuf_tensor(f"{name}_mean_var", [P, T, 2], F32))
        self.var_eps = ctx.enter_context(nc.sbuf_tensor(f"{name}_var_eps", [P, T], F32))
        self.rstd = ctx.enter_context(nc.sbuf_tensor(f"{name}_rstd", [P, T], F32))
        self.mhalf = mhalf
        self.stats_done = Signal(ctx, nc, f"{name}_stats_done", T)
        self.stats_seen = nc.alloc_semaphore(f"{name}_stats_seen")
        self.moments_done = Signal(ctx, nc, f"{name}_moments_done", T)
        self.eps_added = Signal(ctx, nc, f"{name}_eps_added", C)
        self.rstd_ready = Signal(ctx, nc, f"{name}_rstd_ready", C)

    def tile_stats(self, dve, b, t, src):
        dve.bn_stats(self.stats[:, t, :], src).then_inc(self.stats_done.sem, 1)

    def half_moments(self, dve, b, c):
        dve.wait_ge(self.stats_done.sem, self.stats_done.at(b, TH * c + TH))
        dve.sem_inc(self.stats_seen, 1)
        for t in range(TH * c, TH * c + TH):
            dve.bn_aggr(self.mean_var[:, t, :], self.stats[:, t, :]).then_inc(self.moments_done.sem, 1)
        dve.wait_ge(self.moments_done.sem, self.moments_done.at(b, TH * c + TH))
        dve.tensor_scalar(self.var_eps[:, TH * c:TH * c + TH], self.mean_var[:, TH * c:TH * c + TH, 1],
                          LN_EPS, None, ALU.add).then_inc(self.eps_added.sem, 1)

    def half_rstd(self, pool, b, c):
        pool.wait_ge(self.eps_added.sem, self.eps_added.at(b, c + 1))
        half = slice(TH * c, TH * c + TH)
        pool.tensor_tensor(self.rstd[:, half], self.var_eps[:, half], self.mhalf[:, 0:TH],
                           ALU.pow).then_inc(self.rstd_ready.sem, 1)

    def wait_rstd(self, eng, b, c):
        eng.wait_ge(self.rstd_ready.sem, self.rstd_ready.at(b, c + 1))

    def normalise(self, dve, t, dst, src):
        return dve.tensor_scalar(dst, src, self.mean_var[:, t, 0:1], self.rstd[:, t:t + 1],
                                 ALU.subtract, ALU.mult)


def three_products(pe, out, w, m, first, last):
    pe.matmul(out, w[0], m[0], start=first, stop=False)
    pe.matmul(out, w[0], m[1], start=False, stop=False)
    return pe.matmul(out, w[1], m[0], start=False, stop=last)


def cosine_block(nc, ident, mhalf, x, x1, w_in, b_qk, b_v, b_1, b_2, b_3):
    with ExitStack() as ctx:
        def sb(name, shape, dt=F32):
            return ctx.enter_context(nc.sbuf_tensor(name, shape, dt))

        def signal(name, per, credit=0):
            return Signal(ctx, nc, name, per, credit)

        def pair(name, shape):
            return sb(f"{name}_hi", shape, F32R), sb(f"{name}_lo", shape, F32R)

        wqk, wv, w1 = (pair(n, [P, K, w]) for n, w in (("wqk", 2 * D), ("wv", D), ("w1", D)))
        w2, w3 = pair("w2", [P, K, HID]), pair("w3", [P, M2, D])
        x_in = sb("x_in", [P, T, D])
        tok = sb("tok", [P, T, D])
        qk = sb("qk", [P, T, 2 * D])
        x_res = qk[:, 0:T // 2, :].rearrange("p t (u d) -> p (t u) d", u=2)
        xn = qk[:, T // 2:T, :].rearrange("p t (u d) -> p (t u) d", u=2)
        xT = pair("xT", [P, K, S])
        qT = pair("qT", [P, K, S])
        kT = pair("kT", [P, K, S])
        v = pair("v", [P, T, D + 2])
        wide = pair("wide", [P, M2, HALF])
        oT = pair("oT", [P, K, HALF])
        h1T = pair("h1T", [P, K, HALF])
        f32 = sb("f32", [P, 2, HALF])
        v32 = f32[:, :, :].rearrange("p n (u d) -> p n u d", u=2)
        bqk_row = sb("bqk_row", [P, 2 * D])
        bv_row = sb("bv_row", [P, 2, D])
        b3_row = sb("b3_row", [P, D])
        b1_col = sb("b1_col", [P, K])
        b2_col = sb("b2_col", [P, M2])
        squares = sb("squares", [P, 2, D])
        ssq = sb("ssq", [P, T, 2])
        ssq_floor = sb("ssq_floor", [P, T, 2])
        rnorm = sb("rnorm", [P, T, 2])
        rden = sb("rden", [P, T])
        banks = ctx.enter_context(nc.psum_tensor("banks", [P, 8, HALF], F32))
        X, Y = 0, 4

        staged = Weights(nc, "w", (
            (w_in["WqkT"], f32[:, :, :], *wqk),
            (w_in["WvT"], squares[:, :, :], *wv),
            (w_in["W2T"], qk[:, 0:T // 2, :].rearrange("p (k u) d -> p k (u d)", k=K), *w2),
            (w_in["W3T"], tok[:, :, :], *w3),
            (w_in["W1T"], f32[:, :, 0:D], *w1)))
        WQK, WV, W2, W3, W1 = range(5)
        ident_zeroed = nc.alloc_semaphore("ident_zeroed")
        ident_ready = nc.alloc_semaphore("ident_ready")
        ln_in = LayerNorm(ctx, nc, "ln_in", mhalf)
        ln_out = LayerNorm(ctx, nc, "ln_out", mhalf)
        consts = nc.alloc_semaphore("consts_loaded")
        ones_set = nc.alloc_semaphore("v_ones_set")
        x_loaded = [signal(f"x_loaded{c}", 16) for c in range(C)]
        xres_loaded = signal("xres_loaded", 16)
        x1_stored = [signal(f"x1_stored{c}", 16, 16) for c in range(C)]
        x_normed = signal("x_normed", T)
        xT_ready = signal("xT_ready", 2 * K)
        xT_hi = signal("xT_hi", 2 * K)
        xT_lo = signal("xT_lo", 2 * K)
        qk_ready = signal("qk_ready", T)
        qk_biased = signal("qk_biased", T)
        squared = signal("squared", 2 * T, 2)
        floored = signal("floored", C)
        rnorm_ready = signal("rnorm_ready", C)
        q_scaled = signal("q_scaled", T)
        v_ready = signal("v_ready", T // 2)
        v_biased = signal("v_biased", T // 2)
        v_hi = signal("v_hi", T // 2)
        v_lo = signal("v_lo", T // 4)
        v_lo_rest = signal("v_lo_rest", T // 4)
        qkT_ready = signal("qkT_ready", 4 * K)
        qkT_hi = signal("qkT_hi", 4 * K)
        qkT_lo = signal("qkT_lo", 4 * K)
        NF = 2 * (T + K + M2)
        tile_ready = signal("tile_ready", NF)
        f32_done = signal("f32_done", NF, NF)
        hi_done = signal("hi_done", NF)
        lo_done = signal("lo_done", NF, 2)
        o_ready = signal("o_ready", T)
        den_inverted = signal("den_inverted", T)
        o_done = signal("o_done", T)
        oT_ready = signal("oT_ready", 2 * K)
        oT_hi = signal("oT_hi", 2 * K)
        oT_lo = signal("oT_lo", 2 * K)
        h3_ready = signal("h3_ready", T)
        h3_biased = signal("h3_biased", T, T)
        h3_normed = signal("h3_normed", T)
        x1_done = signal("x1_done", T, T)
        CUT_P = [0, T]
        CUT_H1 = [2 * T, 2 * T + K + M2]
        CUT_H2 = [2 * T + K, 2 * T + 2 * K + M2]

        def bank_of(n):
            if n < 2 * T:
                return X + n % 4
            for c in range(C):
                if CUT_H1[c] <= n < CUT_H1[c] + K:
                    return Y + K + n - CUT_H1[c]
            return Y + (n - CUT_H2[0]) % 4 if n < CUT_H1[1] else X + (n - CUT_H2[1]) % 4

        xb = x.rearrange("b (t p) d -> b p t d", p=P)
        x1b = x1.rearrange("b (t p) d -> b p t d", p=P)
        block = ctx.enter_context(nc.Block())

        @block.sync
        def _(sp):
            def load_x(b):
                for c in range(C):
                    sp.dma_start(x_in[:, TH * c:TH * c + TH, :], xb[b, :, TH * c:TH * c + TH, :])\
                        .then_inc(x_loaded[c].sem, 16)

            def batch(b, last):
                if not last:
                    sp.wait_ge(x_normed.sem, x_normed.at(b, T))
                    load_x(b + 1)
                sp.wait_ge(qkT_ready.sem, qkT_ready.at(b, 4 * K))
                sp.dma_start(x_res, xb[b]).then_inc(xres_loaded.sem, 16)
                for c in range(C):
                    sp.wait_ge(x1_done.sem, x1_done.at(b, TH * c + TH))
                    sp.dma_start(x1b[b, :, TH * c:TH * c + TH, :], tok[:, TH * c:TH * c + TH, :])\
                        .then_inc(x1_stored[c].sem, 16)

            load_x(0)
            staged.load(sp, WQK)
            for dst, src in ((bqk_row[:, 0:D], b_qk[0]), (bqk_row[:, D:2 * D], b_qk[1]), (bv_row[:, 0, :], b_v),
                             (bv_row[:, 1, :], b_v), (b3_row[:, :], b_3)):
                sp.dma_start(dst, src.to_broadcast([P, D])).then_inc(consts, 16)
            sp.dma_start(b1_col[:, :], b_1).then_inc(consts, 16)
            sp.dma_start(b2_col[:, :], b_2).then_inc(consts, 16)
            for n in (WV, W2, W3):
                staged.load(sp, n)
            staged.wait(sp, WQK)
            staged.load(sp, W1)
            with sp.Fori(0, B - 1) as b:
                batch(b, False)
            batch(B - 1, True)
            for c in range(C):
                sp.wait_ge(x1_stored[c].sem, x1_stored[c].at(B - 1, 16))

        @block.gpsimd
        def _(pool):
            pool.memset(ident[:, :], 0.0).then_inc(ident_zeroed, 1)
            pool.memset(mhalf[:, :], -0.5).then_inc(ident_zeroed, 1)
            pool.wait_ge(ident_zeroed, 2)
            pool.affine_select(out=ident[:, :], in_=ident[:, :], compare_op=ALU.not_equal, fill=1.0, base=0,
                               pattern=[[-1, P]], channel_multiplier=1).then_inc(ident_ready, 1)
            for part, value in zip(v, (1.0, 0.0)):
                pool.memset(part[:, :, D:D + 2].bitcast(F32), value).then_inc(ones_set, 1)

            def batch(b, last):
                for c in range(C):
                    pool.wait_ge(floored.sem, floored.at(b, c + 1))
                    half = slice(TH * c, TH * c + TH)
                    pool.tensor_tensor(rnorm[:, half, :], ssq_floor[:, half, :],
                                       mhalf[:, 0:2 * TH].rearrange("p (t u) -> p t u", u=2),
                                       ALU.pow).then_inc(rnorm_ready.sem, 1)
                for n in range(T // 4, T // 2):
                    two = slice(2 * n, 2 * n + 2)
                    pool.wait_ge(v_hi.sem, v_hi.at(b, n + 1))
                    pool.tensor_tensor(v[1][:, two, 0:D], v32[:, n % 2, :, :], v[0][:, two, 0:D].bitcast(F32),
                                       ALU.subtract).then_inc(v_lo_rest.sem, 1)
                if not last:
                    for c in range(C):
                        ln_in.half_rstd(pool, b + 1, c)
                for c in range(C):
                    ln_out.half_rstd(pool, b, c)

            for c in range(C):
                ln_in.half_rstd(pool, 0, c)
            with pool.Fori(0, B - 1) as b:
                batch(b, False)
            batch(B - 1, True)

        @block.scalar
        def _(act):
            for sig in (squared,):
                act.sem_inc(sig.sem, sig.credit)
            act.sem_inc(f32_done.sem, f32_done.credit)

            def cut_hi(b, n, hi):
                act.wait_ge(f32_done.sem, f32_done.at(b, n + 1))
                act.activation(hi, f32[:, n % 2, :], ACT.Copy).then_inc(hi_done.sem, 1)

            def make(b, n, func, **kw):
                act.wait_ge(tile_ready.sem, tile_ready.at(b, n + 1))
                act.wait_ge(lo_done.sem, lo_done.at(b, n - 1))
                act.activation(f32[:, n % 2, :], banks[:, bank_of(n), :], func, **kw).then_inc(f32_done.sem, 1)

            def o_transposed_hi(b, c):
                for k in range(K):
                    act.wait_ge(oT_ready.sem, oT_ready.at(b, K * c + k + 1))
                    act.activation(oT[0][:, k, :], banks[:, Y + k, :], ACT.Copy).then_inc(oT_hi.sem, 1)

            def hidden_1(b, c):
                for m in range(K):
                    n = CUT_H1[c] + m
                    make(b, n, ACT.Relu, bias=b1_col[:, m:m + 1])
                    cut_hi(b, n, h1T[0][:, m, :])

            def hidden_2(b, c):
                for m in range(M2):
                    n = CUT_H2[c] + m
                    make(b, n, ACT.Relu, bias=b2_col[:, m:m + 1])
                    cut_hi(b, n, wide[0][:, m, :])

            def scale_q(b, c):
                act.wait_ge(rnorm_ready.sem, rnorm_ready.at(b, c + 1))
                act.wait_ge(squared.sem, squared.at(b, 2 * TH * (c + 1)))
                for t in range(TH * c, TH * c + TH):
                    act.activation(qk[:, t, 0:D], qk[:, t, 0:D], ACT.Copy, scale=rnorm[:, t, 0:1])\
                        .then_inc(q_scaled.sem, 1)

            def values_hi(b, n):
                act.wait_ge(v_biased.sem, v_biased.at(b, n + 1))
                act.activation(v[0][:, 2 * n:2 * n + 2, 0:D], v32[:, n % 2, :, :], ACT.Copy).then_inc(v_hi.sem, 1)

            def qk_transposed_hi(b, tiles):
                for n in tiles:
                    which, c, k = 1 - n // (C * K), n // K % 2, n % K
                    act.wait_ge(qkT_ready.sem, qkT_ready.at(b, n + 1))
                    dst = (qT, kT)[which][0]
                    act.activation(dst[:, k, HALF * c:HALF * c + HALF], banks[:, Y + n % 4, :], ACT.Copy)\
                        .then_inc(qkT_hi.sem, 1)

            def probabilities(b, c, tiles):
                for kt in tiles:
                    n = CUT_P[c] + kt
                    make(b, n, ACT.Exp, scale=rnorm[:, kt, 1:2])
                    cut_hi(b, n, wide[0][:, kt, :])

            def x_transposed_hi(b):
                for n in range(2 * K):
                    c, k = divmod(n, K)
                    act.wait_ge(xT_ready.sem, xT_ready.at(b, n + 1))
                    act.activation(xT[0][:, k, HALF * c:HALF * c + HALF], banks[:, X + n, :], ACT.Copy)\
                        .then_inc(xT_hi.sem, 1)

            def batch(b, last):
                for t in range(T):
                    act.wait_ge(qk_biased.sem, qk_biased.at(b, t + 1))
                    for u in range(2):
                        act.wait_ge(squared.sem, squared.at(b, 2 * t + u - 1))
                        act.activation(squares[:, u, :], qk[:, t, D * u:D * u + D], ACT.Square,
                                       accum_out=ssq[:, t, u:u + 1]).then_inc(squared.sem, 1)
                values_hi(b, 0)
                qk_transposed_hi(b, range(2 * K))
                values_hi(b, 1)
                scale_q(b, 0)
                values_hi(b, 2)
                qk_transposed_hi(b, range(2 * K, 3 * K))
                values_hi(b, 3)
                scale_q(b, 1)
                act.wait_ge(rnorm_ready.sem, rnorm_ready.at(b, C))
                act.wait_ge(v_lo.sem, v_lo.at(b, T // 4))
                act.wait_ge(v_lo_rest.sem, v_lo_rest.at(b, T // 4))
                probabilities(b, 0, range(T // 2))
                qk_transposed_hi(b, range(3 * K, 4 * K))
                probabilities(b, 0, range(T // 2, T))
                probabilities(b, 1, range(T))
                o_transposed_hi(b, 0)
                hidden_1(b, 0)
                hidden_2(b, 0)
                o_transposed_hi(b, 1)
                hidden_1(b, 1)
                hidden_2(b, 1)
                if not last:
                    x_transposed_hi(b + 1)

            staged.cut_hi(act, WQK)
            x_transposed_hi(0)
            for n in (WV, W2, W3, W1):
                staged.cut_hi(act, n)
            act.wait_ge(consts, 16 * 7)
            staged.wait(act, W1)
            with act.Fori(0, B - 1) as b:
                batch(b, False)
            batch(B - 1, True)

        @block.vector
        def _(dve):
            for sig in (lo_done, h3_biased, x1_done):
                dve.sem_inc(sig.sem, sig.credit)
            for sig in x1_stored:
                dve.sem_inc(sig.sem, sig.credit)

            def cut_lo(b, n, hi, lo):
                dve.wait_ge(hi_done.sem, hi_done.at(b, n + 1))
                dve.tensor_tensor(lo, f32[:, n % 2, :], hi.bitcast(F32), ALU.subtract).then_inc(lo_done.sem, 1)

            def attention_rows(b, c):
                for t in range(TH * c, TH * c + TH):
                    bank = banks[:, (Y, X)[c] + t % 4, :]
                    dve.wait_ge(o_ready.sem, o_ready.at(b, t + 1))
                    dve.reciprocal(rden[:, t:t + 1], bank[:, D:D + 1]).then_inc(den_inverted.sem, 1)
                    dve.wait_ge(den_inverted.sem, den_inverted.at(b, t + 1))
                    dve.tensor_scalar(tok[:, t, :], bank[:, 0:D], rden[:, t:t + 1], None, ALU.mult)\
                        .then_inc(o_done.sem, 1)

            def o_transposed_lo(b, c):
                for k in range(K):
                    dve.wait_ge(oT_hi.sem, oT_hi.at(b, K * c + k + 1))
                    dve.tensor_tensor(oT[1][:, k, :], banks[:, Y + k, :], oT[0][:, k, :].bitcast(F32),
                                      ALU.subtract).then_inc(oT_lo.sem, 1)

            def values_biased(b, n):
                dve.wait_ge(v_ready.sem, v_ready.at(b, n + 1))
                if n >= 2:
                    dve.wait_ge(v_lo.sem, v_lo.at(b, n - 1))
                dve.tensor_tensor(v32[:, n % 2, :, :], banks[:, X + n, :].rearrange("p (u d) -> p u d", u=2),
                                  bv_row[:, :, :], ALU.add).then_inc(v_biased.sem, 1)

            def values_lo(b, n):
                two = slice(2 * n, 2 * n + 2)
                dve.wait_ge(v_hi.sem, v_hi.at(b, n + 1))
                dve.tensor_tensor(v[1][:, two, 0:D], v32[:, n % 2, :, :], v[0][:, two, 0:D].bitcast(F32),
                                  ALU.subtract).then_inc(v_lo.sem, 1)

            def floor_norms(b, c):
                half = slice(TH * c, TH * c + TH)
                dve.wait_ge(squared.sem, squared.at(b, 2 * TH * (c + 1)))
                dve.tensor_scalar(ssq_floor[:, half, :], ssq[:, half, :], NORM_FLOOR, None, ALU.max)\
                    .then_inc(floored.sem, 1)

            def qk_transposed_lo(b, n):
                which, c, k = 1 - n // (C * K), n // K % 2, n % K
                half = slice(HALF * c, HALF * c + HALF)
                dst = (qT, kT)[which]
                dve.wait_ge(qkT_hi.sem, qkT_hi.at(b, n + 1))
                dve.tensor_tensor(dst[1][:, k, half], banks[:, Y + n % 4, :], dst[0][:, k, half].bitcast(F32),
                                  ALU.subtract).then_inc(qkT_lo.sem, 1)

            def cut_many(b, first, tiles, dst):
                for m in tiles:
                    cut_lo(b, first + m, dst[0][:, m, :], dst[1][:, m, :])

            def mlp_rows(b, c, tiles):
                for t in tiles:
                    dve.wait_ge(h3_ready.sem, h3_ready.at(b, t + 1))
                    dve.tensor_tensor(tok[:, t, :], banks[:, (X, Y)[c] + t % 4, 0:D], b3_row[:, :], ALU.add)\
                        .then_inc(h3_biased.sem, 1)
                    dve.wait_ge(h3_biased.sem, h3_biased.at(b, t + 1))
                    ln_out.tile_stats(dve, b, t, tok[:, t, :])

            def block_output(b, c):
                ln_out.wait_rstd(dve, b, c)
                if c == 0:
                    dve.wait_ge(xres_loaded.sem, xres_loaded.at(b, 16))
                for t in range(TH * c, TH * c + TH):
                    ln_out.normalise(dve, t, tok[:, t, :], tok[:, t, :]).then_inc(h3_normed.sem, 1)
                for t in range(TH * c, TH * c + TH):
                    dve.wait_ge(h3_normed.sem, h3_normed.at(b, t + 1))
                    dve.tensor_tensor(tok[:, t, :], tok[:, t, :], x_res[:, t, :], ALU.add)\
                        .then_inc(x1_done.sem, 1)

            def input_moments(b):
                for c in range(C):
                    dve.wait_ge(x_loaded[c].sem, x_loaded[c].at(b, 16))
                    for t in range(TH * c, TH * c + TH):
                        ln_in.tile_stats(dve, b, t, x_in[:, t, :])
                    ln_in.half_moments(dve, b, c)

            def input_rows(b):
                for c in range(C):
                    ln_in.wait_rstd(dve, b, c)
                    for t in range(TH * c, TH * c + TH):
                        ln_in.normalise(dve, t, xn[:, t, :], x_in[:, t, :]).then_inc(x_normed.sem, 1)

            def x_transposed_lo(b):
                for n in range(2 * K):
                    c, k = divmod(n, K)
                    half = slice(HALF * c, HALF * c + HALF)
                    dve.wait_ge(xT_hi.sem, xT_hi.at(b, n + 1))
                    dve.tensor_tensor(xT[1][:, k, half], banks[:, X + n, :], xT[0][:, k, half].bitcast(F32),
                                      ALU.subtract).then_inc(xT_lo.sem, 1)

            def batch(b, last):
                for t in range(T):
                    if t == 0:
                        dve.wait_ge(x1_done.sem, x1_done.at(b, 0))
                    dve.wait_ge(qk_ready.sem, qk_ready.at(b, t + 1))
                    dve.tensor_tensor(qk[:, t, :], banks[:, Y + t % 4, :], bqk_row[:, :], ALU.add)\
                        .then_inc(qk_biased.sem, 1)
                values_biased(b, 0)
                floor_norms(b, 0)
                floor_norms(b, 1)
                values_lo(b, 0)
                qk_transposed_lo(b, 0)
                qk_transposed_lo(b, 1)
                values_biased(b, 1)
                qk_transposed_lo(b, 2)
                values_biased(b, 2)
                qk_transposed_lo(b, 3)
                values_lo(b, 1)
                values_biased(b, 3)
                for n in range(2 * K, 3 * K):
                    qk_transposed_lo(b, n)
                cut_many(b, CUT_P[0], range(T // 2), wide)
                for n in range(3 * K, 4 * K):
                    qk_transposed_lo(b, n)
                cut_many(b, CUT_P[0], range(T // 2, T), wide)
                for c in range(C):
                    dve.wait_ge(x1_stored[c].sem, x1_stored[c].at(b, 0))
                attention_rows(b, 0)
                cut_many(b, CUT_P[1], range(T), wide)
                o_transposed_lo(b, 0)
                cut_many(b, CUT_H1[0], range(K), h1T)
                if not last:
                    input_moments(b + 1)
                    input_rows(b + 1)
                attention_rows(b, 1)
                cut_many(b, CUT_H2[0], range(M2), wide)
                o_transposed_lo(b, 1)
                mlp_rows(b, 0, (0, 1))
                cut_many(b, CUT_H1[1], range(K), h1T)
                mlp_rows(b, 0, (2, 3))
                ln_out.half_moments(dve, b, 0)
                cut_many(b, CUT_H2[1], range(M2), wide)
                block_output(b, 0)
                mlp_rows(b, 1, range(TH, T))
                ln_out.half_moments(dve, b, 1)
                if not last:
                    x_transposed_lo(b + 1)
                block_output(b, 1)

            input_moments(0)
            staged.cut_lo(dve, WQK)
            input_rows(0)
            x_transposed_lo(0)
            for n in (WV, W2, W3, W1):
                staged.cut_lo(dve, n)
            dve.wait_ge(consts, 16 * 7)
            staged.wait(dve, W1)
            with dve.Fori(0, B - 1) as b:
                batch(b, False)
            batch(B - 1, True)

        @block.tensor
        def _(pe):
            pe.wait_ge(ident_ready, 1)

            def values(b, n):
                for u in range(2):
                    t = 2 * n + u
                    staged.wait(pe, WV)
                    for k in range(K):
                        mm = three_products(pe, banks[:, X + n, D * u:D * u + D],
                                            [w[:, k, P * t:P * t + P] for w in xT], [m[:, k, :] for m in wv],
                                            k == 0, k == K - 1)
                mm.then_inc(v_ready.sem, 1)

            def transpose_qk(b, tiles):
                for n in tiles:
                    which, c, k = 1 - n // (C * K), n // K % 2, n % K
                    if n == 0:
                        pe.wait_ge(qk_biased.sem, qk_biased.at(b, T))
                    if which == 0:
                        pe.wait_ge(q_scaled.sem, q_scaled.at(b, TH * (c + 1)))
                    if n >= 4:
                        pe.wait_ge(qkT_lo.sem, qkT_lo.at(b, n - 3))
                    for q in range(TH):
                        mm = pe.transpose(banks[:, Y + n % 4, P * q:P * q + P],
                                          qk[:, TH * c + q, D * which + P * k:D * which + P * k + P], ident[:, :])
                    mm.then_inc(qkT_ready.sem, 1)

            def scores(b, c, tiles):
                for kt in tiles:
                    pe.wait_ge(ones_set, 2)
                    n = CUT_P[c] + kt
                    bank = banks[:, bank_of(n), :]
                    if n >= 4:
                        pe.wait_ge(f32_done.sem, f32_done.at(b, n - 3))
                    if n == 0:
                        pe.wait_ge(v_biased.sem, v_biased.at(b, T // 2))
                    if kt == 0:
                        pe.wait_ge(qkT_lo.sem, qkT_lo.at(b, C * K + K * (c + 1)))
                    for k in range(K):
                        mm = three_products(pe, bank, [w[:, k, P * kt:P * kt + P] for w in kT],
                                            [m[:, k, HALF * c:HALF * c + HALF] for m in qT], k == 0, k == K - 1)
                    mm.then_inc(tile_ready.sem, 1)

            def attend(b, c):
                for t in range(TH * c, TH * c + TH):
                    bank = banks[:, (Y, X)[c] + t % 4, 0:D + 2]
                    if t == 0:
                        pe.wait_ge(v_lo.sem, v_lo.at(b, T // 4))
                        pe.wait_ge(v_lo_rest.sem, v_lo_rest.at(b, T // 4))
                        pe.wait_ge(qkT_lo.sem, qkT_lo.at(b, 4 * K))
                    if t == TH:
                        pe.wait_ge(f32_done.sem, f32_done.at(b, 2 * T))
                    for kt in range(T):
                        if t % TH == 0:
                            pe.wait_ge(lo_done.sem, lo_done.at(b, CUT_P[c] + kt + 1))
                        q = t % TH
                        mm = three_products(pe, bank, [w[:, kt, P * q:P * q + P] for w in wide],
                                            [m[:, kt, :] for m in v], kt == 0, kt == T - 1)
                    mm.then_inc(o_ready.sem, 1)

            def transpose_o(b, c):
                for k in range(K):
                    if c == 0:
                        pe.wait_ge(o_done.sem, o_done.at(b, TH))
                    else:
                        pe.wait_ge(o_done.sem, o_done.at(b, T))
                        pe.wait_ge(f32_done.sem, f32_done.at(b, CUT_H2[0] + M2))
                    for q in range(TH):
                        mm = pe.transpose(banks[:, Y + k, P * q:P * q + P],
                                          tok[:, TH * c + q, P * k:P * k + P], ident[:, :])
                    mm.then_inc(oT_ready.sem, 1)

            def hidden_1(b, c):
                staged.wait(pe, W1)
                for m in range(K):
                    for k in range(K):
                        pe.wait_ge(oT_lo.sem, oT_lo.at(b, K * c + k + 1))
                        mm = three_products(pe, banks[:, bank_of(CUT_H1[c] + m), :],
                                            [w[:, k, P * m:P * m + P] for w in w1], [o[:, k, :] for o in oT],
                                            k == 0, k == K - 1)
                    mm.then_inc(tile_ready.sem, 1)

            def hidden_2(b, c):
                staged.wait(pe, W2)
                for m in range(M2):
                    n = CUT_H2[c] + m
                    if m == 0 and c == 0:
                        pe.wait_ge(oT_lo.sem, oT_lo.at(b, K))
                        pe.wait_ge(f32_done.sem, f32_done.at(b, CUT_H1[0] + K))
                    if m < 4 and c == 1:
                        pe.wait_ge(h3_biased.sem, h3_biased.at(b, m + 1))
                    if m >= 4:
                        pe.wait_ge(f32_done.sem, f32_done.at(b, n - 3))
                    for k in range(K):
                        pe.wait_ge(lo_done.sem, lo_done.at(b, CUT_H1[c] + k + 1))
                        mm = three_products(pe, banks[:, bank_of(n), :], [w[:, k, P * m:P * m + P] for w in w2],
                                            [h[:, k, :] for h in h1T], k == 0, k == K - 1)
                    mm.then_inc(tile_ready.sem, 1)

            def mlp_out(b, c, tiles):
                staged.wait(pe, W3)
                for t in tiles:
                    bank, q = banks[:, (X, Y)[c] + t % 4, 0:D], t % TH
                    if t == 0:
                        pe.wait_ge(o_done.sem, o_done.at(b, T))
                    if t == TH:
                        pe.wait_ge(oT_lo.sem, oT_lo.at(b, 2 * K))
                        pe.wait_ge(f32_done.sem, f32_done.at(b, CUT_H1[1] + K))
                    for m in range(M2):
                        if q == 0:
                            pe.wait_ge(lo_done.sem, lo_done.at(b, CUT_H2[c] + m + 1))
                        mm = three_products(pe, bank, [h[:, m, P * q:P * q + P] for h in wide],
                                            [w[:, m, :] for w in w3], m == 0, m == M2 - 1)
                    mm.then_inc(h3_ready.sem, 1)

            with pe.Fori(0, B) as b:
                for n in range(2 * K):
                    c, k = divmod(n, K)
                    if n == 0:
                        pe.wait_ge(f32_done.sem, f32_done.at(b, 0))
                    pe.wait_ge(x_normed.sem, x_normed.at(b, TH * c + TH))
                    for q in range(TH):
                        mm = pe.transpose(banks[:, X + n, P * q:P * q + P],
                                          xn[:, TH * c + q, P * k:P * k + P], ident[:, :])
                    mm.then_inc(xT_ready.sem, 1)
                staged.wait(pe, WQK)
                for t in range(T):
                    if t == 0:
                        pe.wait_ge(h3_biased.sem, h3_biased.at(b, 0))
                    if t % TH == 0:
                        pe.wait_ge(xT_lo.sem, xT_lo.at(b, K * (t // TH + 1)))
                    if t >= 4:
                        pe.wait_ge(qk_biased.sem, qk_biased.at(b, t - 3))
                    for k in range(K):
                        mm = three_products(pe, banks[:, Y + t % 4, :], [w[:, k, P * t:P * t + P] for w in xT],
                                            [m[:, k, :] for m in wqk], k == 0, k == K - 1)
                    mm.then_inc(qk_ready.sem, 1)
                values(b, 0)
                transpose_qk(b, range(2 * K))
                for n in range(1, T // 2):
                    values(b, n)
                transpose_qk(b, range(2 * K, 3 * K))
                scores(b, 0, range(T // 2))
                transpose_qk(b, range(3 * K, 4 * K))
                scores(b, 0, range(T // 2, T))
                attend(b, 0)
                scores(b, 1, range(T))
                transpose_o(b, 0)
                hidden_1(b, 0)
                attend(b, 1)
                hidden_2(b, 0)
                transpose_o(b, 1)
                mlp_out(b, 0, (0, 1))
                hidden_1(b, 1)
                mlp_out(b, 0, (2, 3))
                hidden_2(b, 1)
                mlp_out(b, 1, range(TH, T))


def expert_block(nc, ident, mhalf, x1, out, w_in, cols):
    with ExitStack() as ctx:
        def sb(name, shape, dt=F32):
            return ctx.enter_context(nc.sbuf_tensor(name, shape, dt))

        def signal(name, per, credit=0):
            return Signal(ctx, nc, name, per, credit)

        def pair(name, shape):
            return sb(f"{name}_hi", shape, F32R), sb(f"{name}_lo", shape, F32R)

        wqk, wv, wo = (pair(n, [P, K, w]) for n, w in (("uqk", 2 * D), ("uv", D), ("uo", D)))
        w1, w2 = pair("u1", [P, K, NE * EH]), pair("u2", [P, NE, D])
        z = sb("z", [P, T, D])
        z_next = sb("z_next", [P, T, D])
        xn = sb("xn", [P, T, D])
        cut = pair("cut", [P, NE * HALF])
        xT = [m[:, 0:K * S].rearrange("p (k s) -> p k s", k=K) for m in cut]
        oT = [m[:, K * S:2 * K * S].rearrange("p (k s) -> p k s", k=K) for m in cut]
        hidden = [m[:, :].rearrange("p (e s) -> p e s", e=NE) for m in cut]
        v = sb("v_rows", [P, T, D])
        vh = sb("v_head", [P, 2, T, VW])
        f32 = sb("f32_b", [P, 2, HALF])
        q_stack = sb("q_stack", [P, HPI, S], BF16)
        k_stack = sb("k_stack", [P, HPI, S], BF16)
        probs = sb("probs", [P, 2 * T, HALF])
        parts = probs[:, 0:2 * K * PARTS, :].bitcast(BF16).rearrange("p (n a) s -> p n a s", a=PARTS)
        cw_all = probs[:, 0:8, :].rearrange("p n s -> p (n s)")
        cw_row = probs[:, 8:16, :].rearrange("p n s -> p (n s)")
        o_out = sb("o_out", [P, 2, QUARTER])
        inv_out = sb("inv_out", [P, 2, QUARTER])
        early_den = sb("early_den", [EARLY * T, P])
        early_inv = sb("early_inv", [EARLY * T, P])
        o_num = sb("o_num", [P, K, S])
        o_inv = sb("o_inv", [P, K, S])
        xf32 = o_num[:, 0, :].rearrange("p (k s) -> p k s", k=K)
        gT = o_num[0:NE, 1, :].rearrange("p (c s) -> p c s", c=C)
        x_res = o_inv[:, :, :].rearrange("p k (t d) -> p (k t) d", d=D)
        xfT = pair("xfT", [P, K, HALF])
        maxima = sb("maxima", [P, 2, T])
        neg = sb("neg", [T, 2, P])
        neg_hi = sb("neg_hi", [T, 2, P], BF16)
        neg_lo = sb("neg_lo", [T, 2, P], BF16)
        wg = sb("wg", [P, K, NE])
        col = {n: sb(f"norm_{n}", [P, K]) for n in cols}
        lane = sb("lane", [P, TH, NE])
        gate = sb("gate", [P, T, NE])
        top = sb("top", [P, T, 8])
        top_at = sb("top_at", [P, T, 8], U32)
        top_lane = sb("top_lane", [P, T, 2])
        gap = sb("gap", [P, T])
        gap_exp = sb("gap_exp", [P, T])
        gap_sum = sb("gap_sum", [P, T])
        share = sb("share", [P, T, 2])
        picked = sb("picked", [P, 2, TH, NE])
        weighted = sb("weighted", [P, 2, TH, NE])
        cw = sb("cw", [P, C, NE, TH])
        cwT = sb("cwT", [TH * NE, C, P])
        banks = ctx.enter_context(nc.psum_tensor("banks_b", [P, 8, HALF], F32))
        X, Y = 0, 4
        ST, PV = 4, 6

        q_dram = nc.dram_tensor("q_parts", [B, D, NPOS, S], BF16).ap()
        k_dram = nc.dram_tensor("k_parts", [B, D, NPOS, S], BF16).ap()
        o_dram = nc.dram_tensor("o_rows", [B, EARLY, VW, S], F32).ap()
        inv_dram = nc.dram_tensor("inv_rows", [B, EARLY, S], F32).ap()

        staged = Weights(nc, "u", (
            (w_in["Uqk"], xn[:, 0:4, :].rearrange("p (k u) d -> p k (u d)", k=K), *wqk),
            (w_in["Uv"], xn[:, 4:6, :], *wv),
            (w_in["Uo"], xn[:, 6:8, :], *wo),
            (w_in["U1"], z[:, :, :].rearrange("p (k u) d -> p k (u d)", k=K), *w1),
            (w_in["U2"], probs[:, 2 * T - 4:2 * T, :].rearrange("p n (u d) -> p (n u) d", u=2), *w2)))
        WQK, WV, WO, W1, W2 = range(5)
        ln_z = LayerNorm(ctx, nc, "ln_z", mhalf)
        ln_a = LayerNorm(ctx, nc, "ln_a", mhalf)
        ln_m = LayerNorm(ctx, nc, "ln_m", mhalf)
        ln_o = LayerNorm(ctx, nc, "ln_o", mhalf)
        STEPS, STEP_GAP = 19, 6
        NST, NM, NMT = 2 * T, T + 1, NH * (T + 1)
        consts = nc.alloc_semaphore("b_consts_loaded")
        prepared = nc.alloc_semaphore("b_buffers_prepared")
        taken = {eng: nc.alloc_semaphore(f"wait_taken_{eng}") for eng in ("sp", "pool", "dve", "pe")}
        x1_loaded = [signal(f"b_x1_loaded{c}", 16) for c in range(C)]
        z_done = signal("z_done", T)
        a_normed = signal("a_normed", T)
        xT_ready = signal("b_xT_ready", 2 * K)
        f_done = signal("f_done", 2 * K)
        f_hi = signal("f_hi", 2 * K)
        f_lo = signal("f_lo", 2 * K, 2)
        NQ = 2 * K * C
        qk_ready = signal("b_qk_ready", NQ)
        part1_done = signal("part1_done", NQ)
        rest_done = signal("rest_done", NQ)
        part2_done = signal("part2_done", NQ)
        part3_done = signal("part3_done", NQ)
        parts_stored = signal("parts_stored", 16 * 3 * 2 * (K + 1))
        z_copied = signal("z_copied", 1)
        v_ready = signal("b_v_ready", T // 2)
        v_copied = signal("v_copied", T // 2)
        vh_ready = signal("vh_ready", NH)
        stack_loaded = [signal(f"stack_loaded{n}", 2 * 16 * NH // HPI) for n in range(HPI)]
        shift_loaded = [signal(f"shift_loaded{n}", 2 * 16 * NH // HPI, 32 * (n >= HPI - 2)) for n in range(HPI)]
        max_ready = signal("max_ready", NMT)
        max_read = signal("max_read", NMT, 2)
        neg_hi_done = signal("neg_hi_done", NH, 2)
        neg_lo_done = signal("neg_lo_done", NH, 2)
        st_ready = signal("st_ready", NH * NST)
        exp_done = signal("exp_done", NH * NST, 2)
        pv_done = signal("pv_done", 4 * NH, 8)
        o_copied = signal("o_copied", NH, 2)
        o_stored = [signal(f"o_stored{n}", 16 * EARLY // 2, 16) for n in range(2)]
        early_loaded = signal("early_loaded", 16)
        early_inverted = signal("early_inverted", 1)
        early_stored = signal("early_stored", 16)
        inverted = signal("inverted", HPI)
        MOVES = 16 * 4
        o_moved = [[signal(f"o_moved{c}{n}", MOVES * HPI // 2) for n in range(2)] for c in range(C)]
        o_loaded = [signal(f"o_loaded{k}", 16 * 2) for k in range(K)]
        o_normed = [signal(f"o_normed{k}", C) for k in range(K)]
        oT_hi = signal("b_oT_hi", K * C)
        oT_lo = signal("b_oT_lo", K * C)
        wo_ready = signal("wo_ready", T)
        x2_done = signal("x2_done", T)
        m_normed = signal("m_normed", T)
        xfT_ready = signal("xfT_ready", 2 * K)
        xf_done = signal("xf_done", 2 * K)
        xf_hi = signal("xf_hi", 2 * K)
        xf_lo = signal("xf_lo", 2 * K)
        gT_ready = signal("gT_ready", C)
        gT_copied = signal("gT_copied", C)
        gate_ready = signal("gate_ready", C)
        choose = signal("choose", STEPS * C)
        gap_exp_done = signal("gap_exp_done", C)
        cwT_ready = signal("cwT_ready", C)
        cwT_copied = signal("cwT_copied", C)
        cw_row_loaded = signal("cw_row_loaded", 16 * C)
        cw_spread = signal("cw_spread", 2 * C)
        up_ready = signal("up_ready", C * NE)
        up_done = signal("up_done", C * NE, C * NE)
        up_hi = signal("up_hi", C * NE)
        up_lo = signal("up_lo", C * NE)
        down_ready = signal("down_ready", T)
        y_done = signal("y_done", T, T)
        y_normed = signal("y_normed", T)
        out_done = signal("out_done", T)
        res_loaded = signal("res_loaded", 16)
        out_stored = [signal(f"out_stored{c}", 16, 16) for c in range(C)]

        x1b = x1.rearrange("b (t p) d -> b p t d", p=P)
        outb = out.rearrange("b (t p) d -> b p t d", p=P)

        def m_index(q):
            return q if q < 2 else q + 1

        LAG = 3
        RING_0 = 2 * T + 1
        block = ctx.enter_context(nc.Block())

        @block.sync
        def _(sp):
            def load_x1(b):
                for c in range(C):
                    sp.dma_start(z_next[:, TH * c:TH * c + TH, :], x1b[b, :, TH * c:TH * c + TH, :])\
                        .then_inc(x1_loaded[c].sem, 16)

            def store_parts(b, m, which, rows):
                own = parts[rows, 2 * m + which, :, :]
                many_rows = rows.stop - rows.start
                sources = ((own, own[:, 0:2, :], own[:, 0:1, :]) if which else
                           (own[:, 0:1, :].to_broadcast([many_rows, 3, S]),
                            own[:, 1:2, :].to_broadcast([many_rows, 2, S]), own[:, 2:3, :]))
                sp.wait_ge(part3_done.sem, part3_done.at(b, (2 * m + which + 1) * C))
                for first, many, src in zip((0, 3, 5), (3, 2, 1), sources):
                    sp.dma_start((q_dram, k_dram)[which][b, P * m + rows.start:P * m + rows.stop,
                                                         first:first + many, :], src)\
                        .then_inc(parts_stored.sem, 16)

            def load_stack(b, slot, row):
                for stack, rows in ((q_stack, q_dram), (k_stack, k_dram)):
                    sp.dma_start(stack[0:STACK, slot, :], rows[b, bass.ds(row, DK), :, :]
                                 .rearrange("r a s -> (r a) s")).then_inc(stack_loaded[slot].sem, 16)

            def move_o(j, row, dst, src):
                own = slice(P - DK * (HPI - j), P - DK * (HPI - j - 1))
                for u in range(4):
                    sp.dma_start(dst[own, K - 1, QUARTER * u:QUARTER * u + QUARTER],
                                 src[VW * u + row:VW * u + row + DK, j % 2, :])\
                        .then_inc(o_moved[u // 2][j % 2].sem, 16)

            def heads(b, i, last):
                for j in range(HPI):
                    if not last:
                        sp.wait_ge(st_ready.sem, st_ready.at(b, NST * (j + 1), i * HPI * NST))
                        sp.sem_inc(taken["sp"], 1)
                        load_stack(b, j, i * HPI * DK + (HPI + j) * DK)
                    if last and j == 1:
                        sp.wait_ge(early_stored.sem, early_stored.at(b, 16))
                        sp.sem_inc(taken["sp"], 1)
                        load_o(b, 0, slice(0, NH // K))
                        load_o(b, 1, slice(NH // K, EARLY))
                    sp.wait_ge(o_copied.sem, o_copied.at(b, j + 1, i * HPI))
                    sp.sem_inc(taken["sp"], 1)
                    if not last:
                        sp.dma_start(o_dram[b, i * HPI + j].rearrange("d (u s) -> u d s", u=4), o_out[:, j % 2, :])\
                            .then_inc(o_stored[j % 2].sem, 16)
                    else:
                        move_o(j, 0, o_num, o_out)
                        sp.wait_ge(inverted.sem, inverted.at(b, j + 1))
                        move_o(j, DK, o_inv, inv_out)
                    if last and j == 0:
                        sp.wait_ge(early_inverted.sem, early_inverted.at(b, 1))
                        sp.sem_inc(taken["sp"], 1)
                        sp.dma_start(inv_dram[b, 0:EARLY].rearrange("h (c s) -> (h c) s", c=T), early_inv[:, :])\
                            .then_inc(early_stored.sem, 16)

            def load_early_denominators(b):
                for u in range(2):
                    sp.wait_ge(o_stored[u].sem, o_stored[u].at(b, 16 * EARLY // 2))
                sp.sem_inc(taken["sp"], 1)
                sp.dma_start(early_den[:, :], o_dram[b, 0:EARLY, DK, :].rearrange("h (c s) -> h c s", c=T))\
                    .then_inc(early_loaded.sem, 16)

            def load_o(b, k, some):
                own = slice(0, DK * (some.stop - some.start))
                sp.dma_start(o_num[own, k, :], o_dram[b, some, 0:DK, :]).then_inc(o_loaded[k].sem, 16)
                sp.dma_start(o_inv[own, k, :], inv_dram[b, some, :].rearrange("h (o s) -> h o s", o=1)
                             .to_broadcast([some.stop - some.start, DK, S])).then_inc(o_loaded[k].sem, 16)

            def batch(b, last):
                for which in range(2):
                    store_parts(b, 0, which, slice(0, 2 * DK))
                sp.wait_ge(parts_stored.sem, parts_stored.at(b, 16 * 3 * 2))
                sp.sem_inc(taken["sp"], 1)
                for slot in range(2):
                    load_stack(b, slot, slot * DK)
                for which in range(2):
                    store_parts(b, 0, which, slice(2 * DK, P))
                for m in range(1, K):
                    for which in range(2):
                        store_parts(b, m, which, slice(0, P))
                sp.wait_ge(parts_stored.sem, parts_stored.at(b, 16 * 3 * 2 * (K + 1)))
                sp.sem_inc(taken["sp"], 1)
                for slot in range(2, HPI):
                    load_stack(b, slot, slot * DK)
                if not last:
                    sp.wait_ge(z_copied.sem, z_copied.at(b, 1))
                    sp.sem_inc(taken["sp"], 1)
                    load_x1(b + 1)
                with sp.Fori(0, NH // HPI - 1) as i:
                    heads(b, i, False)
                load_early_denominators(b)
                heads(b, NH // HPI - 1, True)
                for k in range(K):
                    sp.wait_ge(o_normed[k].sem, o_normed[k].at(b, C))
                sp.dma_start(x_res, x1b[b]).then_inc(res_loaded.sem, 16)
                for c in range(C):
                    sp.wait_ge(cwT_copied.sem, cwT_copied.at(b, c + 1))
                    if c > 0:
                        sp.wait_ge(cw_spread.sem, cw_spread.at(b, 2 * c))
                    sp.dma_start(cw_row[0:1, :].rearrange("o (r p) -> o r p", p=P), cwT[:, c, :])\
                        .then_inc(cw_row_loaded.sem, 16)
                for c in range(C):
                    sp.wait_ge(out_done.sem, out_done.at(b, TH * c + TH))
                    sp.dma_start(outb[b, :, TH * c:TH * c + TH, :], xn[:, TH * c:TH * c + TH, :])\
                        .then_inc(out_stored[c].sem, 16)

            load_x1(0)
            staged.load(sp, WQK)
            for n in cols:
                sp.dma_start(col[n][:, :], cols[n]).then_inc(consts, 16)
            sp.dma_start(wg[:, :, :], w_in["Ug"]).then_inc(consts, 16)
            for n in (WV, WO, W1, W2):
                staged.load(sp, n)
            with sp.Fori(0, B - 1) as b:
                batch(b, False)
            batch(B - 1, True)
            for c in range(C):
                sp.wait_ge(out_stored[c].sem, out_stored[c].at(B - 1, 16))

        @block.gpsimd
        def _(pool):
            for sig in (neg_hi_done, neg_lo_done):
                pool.sem_inc(sig.sem, sig.credit)
            def negate_max(b, i, j, ring):
                slot = j % HPI
                pool.wait_ge(max_read.sem, max_read.at(b, ring, i * HPI * NM))
                before, turn = (slot + 2) % HPI, (j - 2) // HPI + 1
                pool.wait_ge(shift_loaded[before].sem, shift_loaded[before].at(b, 32 * turn, i * 32))
                pool.sem_inc(taken["pool"], 1)
                pool.tensor_copy(neg_hi[:, j % 2, :], neg[:, j % 2, :]).then_inc(neg_hi_done.sem, 1)
                pool.wait_ge(neg_hi_done.sem, neg_hi_done.at(b, j + 1, i * HPI))
                pool.tensor_tensor(neg_lo[:, j % 2, :], neg[:, j % 2, :], neg_hi[:, j % 2, :],
                                   ALU.subtract).then_inc(neg_lo_done.sem, 1)
                pool.wait_ge(neg_lo_done.sem, neg_lo_done.at(b, j + 1, i * HPI))
                pool.sem_inc(taken["pool"], 1)
                for row, src in ((STACK, neg_hi), (STACK + 1, neg_lo)):
                    pool.dma_start(q_stack[row:row + 1, slot, :].rearrange("o (t p) -> o t p", p=P),
                                   src[:, j % 2, :]).then_inc(shift_loaded[slot].sem, 16)

            def head_values(b, i, j):
                pool.wait_ge(pv_done.sem, pv_done.at(b, 4 * (j - 1), i * HPI * 4))
                pool.sem_inc(taken["pool"], 1)
                first = i * HPI * DK + j * DK
                pool.tensor_copy(vh[:, j % 2, :, 0:DK], v[:, :, bass.ds(first, DK)]).then_inc(vh_ready.sem, 1)

            def heads(b, i, last):
                for j in range(HPI):
                    if not (last and j == HPI - 1):
                        done = RING_0 + NM * j + (3 if not (last and j == HPI - 2) else 1)
                        negate_max(b, i, j + 1, done)
                        head_values(b, i, j + 1)

            def normalise_o(b, k, c):
                half = slice(HALF * c, HALF * c + HALF)
                pool.wait_ge(o_loaded[k].sem, o_loaded[k].at(b, 16 * 2))
                pool.tensor_tensor(o_num[:, k, half], o_num[:, k, half], o_inv[:, k, half], ALU.mult)\
                    .then_inc(o_normed[k].sem, 1)

            def batch(b, last):
                for n in range(NQ):
                    own = parts[:, n // C, :, HALF * (n % C):HALF * (n % C) + HALF]
                    pool.wait_ge(part2_done.sem, part2_done.at(b, n + 1))
                    pool.tensor_tensor(own[:, 2, :], f32[:, n % 2, :], own[:, 1, :], ALU.subtract)\
                        .then_inc(part3_done.sem, 1)
                negate_max(b, 0, 0, T + 1)
                pool.wait_ge(v_copied.sem, v_copied.at(b, T // 2))
                head_values(b, 0, 0)
                with pool.Fori(0, NH // HPI - 1) as i:
                    heads(b, i, False)
                heads(b, NH // HPI - 1, True)
                if not last:
                    for c in range(C):
                        ln_z.half_rstd(pool, b + 1, c)
                for c in range(C):
                    normalise_o(b, 0, c)
                if not last:
                    for c in range(C):
                        ln_a.half_rstd(pool, b + 1, c)
                for c in range(C):
                    ln_m.half_rstd(pool, b, c)
                for c in range(C):
                    pool.wait_ge(cw_row_loaded.sem, cw_row_loaded.at(b, 16 * (c + 1)))
                    if c > 0:
                        pool.wait_ge(up_done.sem, up_done.at(b, NE * c))
                    pool.sem_inc(taken["pool"], 1)
                    for some in (slice(0, NE * HALF // 2), slice(NE * HALF // 2, NE * HALF)):
                        pool.partition_broadcast(cw_all[:, some], cw_row[0:1, some], channels=P)\
                            .then_inc(cw_spread.sem, 1)
                for c in range(C):
                    ln_o.half_rstd(pool, b, c)

            for ln in (ln_z, ln_a):
                for c in range(C):
                    ln.half_rstd(pool, 0, c)
            ln_a.wait_rstd(pool, 0, C - 1)
            pool.memset(q_stack[96:P, :, :], 0.0).then_inc(prepared, 1)
            pool.memset(k_stack[96:P, :, :], 1.0).then_inc(prepared, 1)
            pool.wait_ge(prepared, 2)
            pool.memset(vh[:, :, :, :], 1.0).then_inc(prepared, 1)
            pool.iota(lane[:, :, :], [[0, TH], [1, NE]], base=0, channel_multiplier=0,
                      allow_small_or_imprecise_dtypes=True).then_inc(prepared, 1)
            pool.memset(neg_hi[:, :, :], 0.0).then_inc(prepared, 1)
            pool.wait_ge(prepared, 5)
            for slot in range(HPI - 2, HPI):
                for row in (STACK, STACK + 1):
                    pool.dma_start(q_stack[row:row + 1, slot, :].rearrange("o (t p) -> o t p", p=P),
                                   neg_hi[:, slot % 2, :]).then_inc(shift_loaded[slot].sem, 16)
            with pool.Fori(0, B - 1) as b:
                batch(b, False)
            batch(B - 1, True)

        @block.scalar
        def _(act):
            for sig in (exp_done, o_copied, *o_stored):
                act.sem_inc(sig.sem, sig.credit)

            def exponential(b, i, j, n):
                act.wait_ge(st_ready.sem, st_ready.at(b, NST * j + n + 1, i * HPI * NST))
                if n % 4 == 0:
                    act.wait_ge(pv_done.sem, pv_done.at(b, 4 * j + n // 4 - 3, i * HPI * 4))
                act.activation(probs[:, n, :], banks[:, ST + n % 2, :], ACT.Exp).then_inc(exp_done.sem, 1)

            def copy_o(b, i, j, last):
                act.wait_ge(pv_done.sem, pv_done.at(b, 4 * (j + 1), i * HPI * 4))
                if last and j >= 2:
                    for moved in o_moved:
                        act.wait_ge(moved[j % 2].sem, moved[j % 2].at(b, MOVES * (j // 2)))
                else:
                    act.wait_ge(o_stored[j % 2].sem, o_stored[j % 2].at(b, 16 * (j // 2), i * 16 * HPI // 2))
                act.activation(o_out[:, j % 2, :], banks[:, PV + j % 2, 0:QUARTER], ACT.Copy).then_inc(o_copied.sem, 1)

            def attention_hi(b, k):
                for c in range(C):
                    half = slice(HALF * c, HALF * c + HALF)
                    act.wait_ge(o_normed[k].sem, o_normed[k].at(b, c + 1))
                    act.activation(oT[0][:, k, half], o_num[:, k, half], ACT.Copy).then_inc(oT_hi.sem, 1)

            def heads(b, i, last):
                for j in range(HPI):
                    for n in range(NST):
                        exponential(b, i, j, n)
                        if n == C * LAG and j > 0:
                            copy_o(b, i, j - 1, last)
                        if last and j == HPI - 1 and n == 7:
                            attention_hi(b, 0)
                copy_o(b, i, HPI - 1, last)

            def expert_input_columns(b, c):
                for k in range(K):
                    act.wait_ge(xfT_ready.sem, xfT_ready.at(b, K * c + k + 1))
                    if c > 0:
                        act.wait_ge(xf_lo.sem, xf_lo.at(b, K * c))
                    act.activation(xf32[:, k, :], banks[:, (X, Y)[c] + k, :], ACT.Identity,
                                   bias=col["b2"][:, k:k + 1], scale=col["g2"][:, k:k + 1]).then_inc(xf_done.sem, 1)

            def copy_gates(b, c):
                act.wait_ge(gT_ready.sem, gT_ready.at(b, c + 1))
                act.activation(gT[:, c, :], banks[0:NE, (X, Y)[c] + 2, :], ACT.Copy).then_inc(gT_copied.sem, 1)

            def gap_exponential(b, c):
                half = slice(TH * c, TH * c + TH)
                act.wait_ge(choose.sem, choose.at(b, STEPS * c + STEP_GAP))
                act.activation(gap_exp[:, half], gap[:, half], ACT.Exp).then_inc(gap_exp_done.sem, 1)

            def expert_input_hi(b, c):
                for k in range(K):
                    act.wait_ge(xf_done.sem, xf_done.at(b, K * c + k + 1))
                    act.activation(xfT[0][:, k, :], xf32[:, k, :], ACT.Copy).then_inc(xf_hi.sem, 1)

            def expert_hidden_hi(b, c):
                for n in range(NE * c, NE * c + NE):
                    act.wait_ge(up_done.sem, up_done.at(b, n + 1))
                    act.activation(hidden[0][:, n % NE, :], f32[:, n % 2, :], ACT.Copy).then_inc(up_hi.sem, 1)

            def x_transposed_hi(b):
                for n in range(2 * K):
                    c, k = divmod(n, K)
                    act.wait_ge(xT_ready.sem, xT_ready.at(b, n + 1))
                    act.wait_ge(f_lo.sem, f_lo.at(b, n - 1))
                    act.activation(f32[:, n % 2, :], banks[:, X + n, :], ACT.Identity, bias=col["b1"][:, k:k + 1],
                                   scale=col["g1"][:, k:k + 1]).then_inc(f_done.sem, 1)
                    act.wait_ge(f_done.sem, f_done.at(b, n + 1))
                    act.activation(xT[0][:, k, HALF * c:HALF * c + HALF], f32[:, n % 2, :], ACT.Copy)\
                        .then_inc(f_hi.sem, 1)

            def batch(b, last):
                for n in range(NQ + 1):
                    if n < NQ:
                        scale = DK ** -0.5 if n // C % 2 == 0 else 1.0
                        half = slice(HALF * (n % C), HALF * (n % C) + HALF)
                        act.wait_ge(qk_ready.sem, qk_ready.at(b, n + 1))
                        act.activation(parts[:, n // C, 0, half], banks[:, Y + n % 4, :], ACT.Copy, scale=scale)\
                            .then_inc(part1_done.sem, 1)
                    if n > 0:
                        half = slice(HALF * ((n - 1) % C), HALF * ((n - 1) % C) + HALF)
                        act.wait_ge(rest_done.sem, rest_done.at(b, n))
                        act.activation(parts[:, (n - 1) // C, 1, half], f32[:, (n - 1) % 2, :], ACT.Copy)\
                            .then_inc(part2_done.sem, 1)
                for n in range(T // 2):
                    act.wait_ge(v_ready.sem, v_ready.at(b, n + 1))
                    act.activation(v[:, 2 * n:2 * n + 2, :], banks[:, Y + n, :].rearrange("p (u d) -> p u d", u=2),
                                   ACT.Copy).then_inc(v_copied.sem, 1)
                act.wait_ge(y_done.sem, y_done.at(b, 0))
                staged.wait(act, W1)
                act.activation(z[:, :, :], z_next[:, :, :], ACT.Copy).then_inc(z_copied.sem, 1)
                act.wait_ge(parts_stored.sem, parts_stored.at(b, 16 * 3 * 2 * (K + 1)))
                with act.Fori(0, NH // HPI - 1) as i:
                    heads(b, i, False)
                heads(b, NH // HPI - 1, True)
                attention_hi(b, 1)
                expert_input_columns(b, 0)
                expert_input_hi(b, 0)
                copy_gates(b, 0)
                expert_input_columns(b, 1)
                gap_exponential(b, 0)
                copy_gates(b, 1)
                gap_exponential(b, 1)
                expert_hidden_hi(b, 0)
                act.wait_ge(up_ready.sem, up_ready.at(b, NE))
                expert_input_hi(b, 1)
                expert_hidden_hi(b, 1)
                if not last:
                    x_transposed_hi(b + 1)

            staged.cut_hi(act, WQK)
            act.wait_ge(consts, 16 * (len(cols) + 1))
            x_transposed_hi(0)
            for n in (WV, WO, W1, W2):
                staged.cut_hi(act, n)
            with act.Fori(0, B - 1) as b:
                batch(b, False)
            batch(B - 1, True)

        @block.vector
        def _(dve):
            for sig in (f_lo, max_read, up_done, y_done):
                dve.sem_inc(sig.sem, sig.credit)

            def negated_maxima(b, i, head, done):
                step = done - 1
                dve.wait_ge(max_ready.sem, max_ready.at(b, done, i * HPI * NM))
                dve.wait_ge(neg_lo_done.sem, neg_lo_done.at(b, head - 1, i * HPI))
                dve.tensor_scalar(neg[:, head % 2, :], banks[0:T, 2 * (step % 2), 0:P], -1.0, None, ALU.mult)\
                    .then_inc(max_read.sem, 1)

            def tile_maximum(b, i, head, q, done):
                step = done - 1
                dve.wait_ge(max_ready.sem, max_ready.at(b, done, i * HPI * NM))
                dve.tensor_reduce(maxima[:, head % 2, q:q + 1], banks[:, 2 * (step % 2):2 * (step % 2) + 2, :],
                                  AX.XY, ALU.max).then_inc(max_read.sem, 1)

            def invert(b, j):
                dve.wait_ge(o_copied.sem, o_copied.at(b, EARLY + j + 1))
                if j >= 2:
                    for moved in o_moved:
                        dve.wait_ge(moved[j % 2].sem, moved[j % 2].at(b, MOVES * (j // 2)))
                dve.reciprocal(inv_out[:, j % 2, :], o_out[:, j % 2, :]).then_inc(inverted.sem, 1)

            def input_moments(b):
                for c in range(C):
                    dve.wait_ge(x1_loaded[c].sem, x1_loaded[c].at(b, 16))
                    for t in range(TH * c, TH * c + TH):
                        ln_z.tile_stats(dve, b, t, z_next[:, t, :])
                    ln_z.half_moments(dve, b, c)

            def heads(b, i, last, last_batch=False):
                for j in range(HPI):
                    base, more = RING_0 + NM * j, not (last and j >= HPI - 2)
                    for q in range(T):
                        if more:
                            tile_maximum(b, i, j + 2, q, base + m_index(q) + 1)
                        if q == 4 and last and j == 1:
                            invert(b, 0)
                        if q == 6 and last and j == 0:
                            dve.wait_ge(early_loaded.sem, early_loaded.at(b, 16))
                            dve.reciprocal(early_inv[:, :], early_den[:, :]).then_inc(early_inverted.sem, 1)
                        if q == 1 and not (last and j == HPI - 1):
                            negated_maxima(b, i, j + 1, base + (3 if more else 1))
                    if last and not last_batch and j == HPI - 3:
                        input_moments(b + 1)

            def normalise_o(b, k, c):
                half = slice(HALF * c, HALF * c + HALF)
                dve.wait_ge(o_loaded[k].sem, o_loaded[k].at(b, 16 * 2))
                if k == K - 1:
                    for moved in o_moved[c]:
                        dve.wait_ge(moved.sem, moved.at(b, MOVES * HPI // 2))
                dve.tensor_tensor(o_num[:, k, half], o_num[:, k, half], o_inv[:, k, half], ALU.mult)\
                    .then_inc(o_normed[k].sem, 1)

            def attention_lo(b, k, c):
                half = slice(HALF * c, HALF * c + HALF)
                dve.wait_ge(oT_hi.sem, oT_hi.at(b, C * k + c + 1))
                dve.tensor_tensor(oT[1][:, k, half], o_num[:, k, half], oT[0][:, k, half].bitcast(F32),
                                  ALU.subtract).then_inc(oT_lo.sem, 1)

            def input_rows(b):
                for c in range(C):
                    ln_z.wait_rstd(dve, b, c)
                    for t in range(TH * c, TH * c + TH):
                        ln_z.normalise(dve, t, z_next[:, t, :], z_next[:, t, :]).then_inc(z_done.sem, 1)
                    for t in range(TH * c, TH * c + TH):
                        dve.wait_ge(z_done.sem, z_done.at(b, t + 1))
                        ln_a.tile_stats(dve, b, t, z_next[:, t, :])
                    ln_a.half_moments(dve, b, c)

            def attention_input(b):
                for c in range(C):
                    ln_a.wait_rstd(dve, b, c)
                    for t in range(TH * c, TH * c + TH):
                        ln_a.normalise(dve, t, v[:, t, :], z_next[:, t, :]).then_inc(a_normed.sem, 1)

            def second_residual(b, tiles):
                for t in tiles:
                    c = t // TH
                    dve.wait_ge(wo_ready.sem, wo_ready.at(b, t + 1))
                    dve.tensor_tensor(z[:, t, :], banks[:, (X, Y)[c] + t % 4, 0:D], z[:, t, :], ALU.add)\
                        .then_inc(x2_done.sem, 1)
                    dve.wait_ge(x2_done.sem, x2_done.at(b, t + 1))
                    ln_m.tile_stats(dve, b, t, z[:, t, :])

            def expert_input(b, c):
                ln_m.wait_rstd(dve, b, c)
                for t in range(TH * c, TH * c + TH):
                    ln_m.normalise(dve, t, xn[:, t, :], z[:, t, :]).then_inc(m_normed.sem, 1)

            def expert_input_lo(b, c):
                for k in range(K):
                    dve.wait_ge(xf_hi.sem, xf_hi.at(b, K * c + k + 1))
                    dve.tensor_tensor(xfT[1][:, k, :], xf32[:, k, :], xfT[0][:, k, :].bitcast(F32), ALU.subtract)\
                        .then_inc(xf_lo.sem, 1)

            def choose_experts(b, c):
                half, done = slice(TH * c, TH * c + TH), STEPS * c

                def after(step):
                    dve.wait_ge(choose.sem, choose.at(b, done + step))

                def step(instruction):
                    instruction.then_inc(choose.sem, 1)

                bank = banks[:, Y + 3, 0:TH * NE].rearrange("p (t e) -> p t e", e=NE)
                dve.wait_ge(gate_ready.sem, gate_ready.at(b, c + 1))
                step(dve.tensor_copy(gate[:, half, :], bank))
                after(1)
                dve.sem_inc(taken["dve"], 1)
                for t in range(TH * c, TH * c + TH):
                    step(dve.max(top[:, t, :], gate[:, t, :]))
                after(5)
                step(dve.tensor_tensor(gap[:, half], top[:, half, 1], top[:, half, 0], ALU.subtract))
                for t in range(TH * c, TH * c + TH):
                    step(dve.max_index(top_at[:, t, :], top[:, t, :], gate[:, t, :]))
                after(10)
                step(dve.tensor_copy(top_lane[:, half, :], top_at[:, half, 0:2]))
                dve.wait_ge(gap_exp_done.sem, gap_exp_done.at(b, c + 1))
                step(dve.tensor_scalar(gap_sum[:, half], gap_exp[:, half], 1.0, None, ALU.add))
                after(12)
                step(dve.reciprocal(share[:, half, 0], gap_sum[:, half]))
                after(13)
                step(dve.tensor_tensor(share[:, half, 1], gap_exp[:, half], share[:, half, 0], ALU.mult))
                for u in range(2):
                    step(dve.tensor_tensor(picked[:, u, :, :], lane[:, :, :],
                                           top_lane[:, half, u:u + 1].to_broadcast([P, TH, NE]), ALU.is_equal))
                after(16)
                for u in range(2):
                    step(dve.tensor_tensor(weighted[:, u, :, :], picked[:, u, :, :],
                                           share[:, half, u:u + 1].to_broadcast([P, TH, NE]), ALU.mult))
                after(18)
                step(dve.tensor_tensor(cw[:, c, :, :].rearrange("p e t -> p t e"), weighted[:, 0, :, :],
                                       weighted[:, 1, :, :], ALU.add))

            def weights_out(b, c):
                dve.wait_ge(cwT_ready.sem, cwT_ready.at(b, c + 1))
                dve.tensor_copy(cwT[:, c, :], banks[0:TH * NE, (X + 2, Y)[c], 0:P]).then_inc(cwT_copied.sem, 1)

            def expert_hidden(b, c):
                for n in range(NE * c, NE * c + NE):
                    e = n % NE

                    def lo(n):
                        dve.wait_ge(up_hi.sem, up_hi.at(b, n + 1))
                        dve.tensor_tensor(hidden[1][:, n % NE, :], f32[:, n % 2, :], hidden[0][:, n % NE, :]
                                          .bitcast(F32), ALU.subtract).then_inc(up_lo.sem, 1)

                    if e % (NE // 2) == 0:
                        dve.wait_ge(cw_spread.sem, cw_spread.at(b, 2 * c + e // (NE // 2) + 1))
                    dve.wait_ge(up_ready.sem, up_ready.at(b, n + 1))
                    if n >= 2:
                        dve.wait_ge(up_lo.sem, up_lo.at(b, n - 1))
                    dve.scalar_tensor_tensor(
                        out=f32[:, n % 2, :], in0=banks[:, X + n % 4, :], scalar=0.0,
                        in1=cw_all[:, HALF * e:HALF * e + HALF], op0=ALU.max, op1=ALU.mult).then_inc(up_done.sem, 1)
                    if e > 0:
                        lo(n - 1)
                lo(NE * c + NE - 1)

            def block_rows(b, tiles):
                for t in tiles:
                    dve.wait_ge(down_ready.sem, down_ready.at(b, t + 1))
                    dve.tensor_tensor(xn[:, t, :], banks[:, (X, Y)[t // TH] + t % 4, 0:D], z[:, t, :],
                                      ALU.add).then_inc(y_done.sem, 1)
                    dve.wait_ge(y_done.sem, y_done.at(b, t + 1))
                    ln_o.tile_stats(dve, b, t, xn[:, t, :])

            def block_output(b, c):
                ln_o.wait_rstd(dve, b, c)
                for t in range(TH * c, TH * c + TH):
                    ln_o.normalise(dve, t, xn[:, t, :], xn[:, t, :]).then_inc(y_normed.sem, 1)
                dve.wait_ge(res_loaded.sem, res_loaded.at(b, 16))
                for t in range(TH * c, TH * c + TH):
                    dve.wait_ge(y_normed.sem, y_normed.at(b, t + 1))
                    dve.tensor_tensor(xn[:, t, :], xn[:, t, :], x_res[:, t, :], ALU.add)\
                        .then_inc(out_done.sem, 1)

            for sig in out_stored:
                dve.sem_inc(sig.sem, sig.credit)

            def x_transposed_lo(b):
                for n in range(2 * K):
                    c, k = divmod(n, K)
                    half = slice(HALF * c, HALF * c + HALF)
                    dve.wait_ge(f_hi.sem, f_hi.at(b, n + 1))
                    dve.tensor_tensor(xT[1][:, k, half], f32[:, n % 2, :], xT[0][:, k, half].bitcast(F32),
                                      ALU.subtract).then_inc(f_lo.sem, 1)

            def batch(b, last):
                for n in range(NQ):
                    scale = DK ** -0.5 if n // C % 2 == 0 else 1.0
                    if n < 2:
                        dve.wait_ge(f_lo.sem, f_lo.at(b, 2 * K))
                    else:
                        dve.wait_ge(part3_done.sem, part3_done.at(b, n - 1))
                    half = slice(HALF * (n % C), HALF * (n % C) + HALF)
                    dve.wait_ge(part1_done.sem, part1_done.at(b, n + 1))
                    dve.scalar_tensor_tensor(out=f32[:, n % 2, :], in0=banks[:, Y + n % 4, :], scalar=scale,
                                             in1=parts[:, n // C, 0, half], op0=ALU.mult, op1=ALU.subtract)\
                        .then_inc(rest_done.sem, 1)
                for q in range(T):
                    tile_maximum(b, 0, 0, q, q + 1)
                negated_maxima(b, 0, 0, T + 1)
                for q in range(T):
                    tile_maximum(b, 0, 1, q, T + 1 + q + 1)
                with dve.Fori(0, NH // HPI - 1) as i:
                    heads(b, i, False)
                heads(b, NH // HPI - 1, True, last)
                invert(b, 1)
                if not last:
                    input_rows(b + 1)
                invert(b, HPI - 2)
                for c in range(C):
                    attention_lo(b, 0, c)
                invert(b, HPI - 1)
                if not last:
                    dve.wait_ge(vh_ready.sem, vh_ready.at(b, NH))
                    attention_input(b + 1)
                for c in range(C):
                    normalise_o(b, 1, c)
                    attention_lo(b, 1, c)
                for c in range(C):
                    dve.wait_ge(out_stored[c].sem, out_stored[c].at(b, 0))
                second_residual(b, range(TH))
                ln_m.half_moments(dve, b, 0)
                second_residual(b, (TH, TH + 1, TH + 2))
                expert_input(b, 0)
                second_residual(b, (TH + 3,))
                ln_m.half_moments(dve, b, 1)
                expert_input(b, 1)
                expert_input_lo(b, 0)
                for c in range(C):
                    choose_experts(b, c)
                    weights_out(b, c)
                expert_hidden(b, 0)
                expert_input_lo(b, 1)
                block_rows(b, range(TH))
                ln_o.half_moments(dve, b, 0)
                expert_hidden(b, 1)
                block_output(b, 0)
                block_rows(b, range(TH, T))
                ln_o.half_moments(dve, b, 1)
                if not last:
                    x_transposed_lo(b + 1)
                block_output(b, 1)

            input_moments(0)
            staged.cut_lo(dve, WQK)
            input_rows(0)
            attention_input(0)
            x_transposed_lo(0)
            for n in (WV, WO, W1, W2):
                staged.cut_lo(dve, n)
            staged.wait(dve, W2)
            dve.wait_ge(prepared, 5)
            with dve.Fori(0, B - 1) as b:
                batch(b, False)
            batch(B - 1, True)

        @block.tensor
        def _(pe):
            for sig in (pv_done,):
                pe.sem_inc(sig.sem, sig.credit)

            def max_tile(b, i, head, q, done):
                slot, pair_of = head % HPI, (done - 1) % 2
                if q == 0:
                    pe.wait_ge(stack_loaded[slot].sem, stack_loaded[slot].at(b, 32 * (head // HPI + 1), i * 32))
                if done > 2:
                    pe.wait_ge(max_read.sem, max_read.at(b, done - 2, i * HPI * NM))
                for c in range(C):
                    mm = pe.matmul(banks[:, 2 * pair_of + c, :], q_stack[0:STACK, slot, P * q:P * q + P],
                                   k_stack[0:STACK, slot, HALF * c:HALF * c + HALF], start=True, stop=True)
                mm.then_inc(max_ready.sem, 1)

            def transpose_maxima(b, i, head, done, need):
                pe.wait_ge(max_read.sem, max_read.at(b, need, i * HPI * NM))
                pe.transpose(banks[0:T, 2 * ((done - 1) % 2), 0:P], maxima[:, head % 2, :], ident[:, :])\
                    .then_inc(max_ready.sem, 1)

            def transposed_scores(b, i, j, n):
                kt, c, slot = n // C, n % C, j
                if n == 0:
                    turn = 32 * (j // HPI + 1)
                    pe.wait_ge(shift_loaded[slot].sem, shift_loaded[slot].at(b, turn, i * 32))
                pe.wait_ge(exp_done.sem, exp_done.at(b, NST * j + n - 1, i * HPI * NST))
                rows = STACK + SHIFT_ROWS
                pe.matmul(banks[:, ST + n % 2, :], k_stack[0:rows, slot, P * kt:P * kt + P],
                          q_stack[0:rows, slot, HALF * c:HALF * c + HALF], start=True, stop=True)\
                    .then_inc(st_ready.sem, 1)

            def weigh_values(b, i, j, kt):
                if kt % 2 == 0:
                    pe.wait_ge(exp_done.sem, exp_done.at(b, NST * j + C * (kt + 2), i * HPI * NST))
                if kt == 0:
                    pe.wait_ge(vh_ready.sem, vh_ready.at(b, j + 1, i * HPI))
                    pe.wait_ge(o_copied.sem, o_copied.at(b, j - 1, i * HPI))
                for u in range(4):
                    first = QUARTER * (u % 2)
                    mm = pe.matmul(banks[VW * u:VW * u + VW, PV + j % 2, 0:QUARTER], vh[:, j % 2, kt, :],
                                   probs[:, C * kt + u // 2, first:first + QUARTER], start=kt == 0, stop=kt == T - 1)
                if kt % 2 == 1:
                    mm.then_inc(pv_done.sem, 1)

            def heads(b, i, last):
                for j in range(HPI):
                    base, more = RING_0 + NM * j, not (last and j >= HPI - 2)
                    for kt in range(T):
                        tail = j == HPI - 1 and kt == T - 1
                        transposed_scores(b, i, j, C * kt)
                        if tail:
                            transposed_scores(b, i, j, C * kt + 1)
                        if more:
                            max_tile(b, i, j + 2, kt, base + m_index(kt) + 1)
                        if not tail:
                            transposed_scores(b, i, j, C * kt + 1)
                        if kt >= LAG:
                            weigh_values(b, i, j, kt - LAG)
                        elif j > 0:
                            weigh_values(b, i, j - 1, T + kt - LAG)
                        if kt == 1 and not (last and j == HPI - 1):
                            transpose_maxima(b, i, j + 1, base + (3 if more else 1), base + (1 if more else 0))
                for kt in range(T - LAG, T):
                    weigh_values(b, i, HPI - 1, kt)

            def project_attention(b, c):
                staged.wait(pe, WO)
                for t in range(TH * c, TH * c + TH):
                    q = t % TH
                    if q == 0:
                        pe.wait_ge(oT_lo.sem, oT_lo.at(b, C + c + 1))
                    for k in range(K):
                        mm = three_products(pe, banks[:, (X, Y)[c] + q, 0:D],
                                            [w[:, k, P * t:P * t + P] for w in oT], [m[:, k, :] for m in wo],
                                            k == 0, k == K - 1)
                    mm.then_inc(wo_ready.sem, 1)

            def expert_input(b, c):
                pe.wait_ge(x2_done.sem, x2_done.at(b, TH * (c + 1)))
                pe.wait_ge(m_normed.sem, m_normed.at(b, TH * (c + 1)))
                for k in range(K):
                    for q in range(TH):
                        mm = pe.transpose(banks[:, (X, Y)[c] + k, P * q:P * q + P],
                                          xn[:, TH * c + q, P * k:P * k + P], ident[:, :])
                    mm.then_inc(xfT_ready.sem, 1)

            def gates(b, c):
                pe.wait_ge(xf_done.sem, xf_done.at(b, K * (c + 1)))
                for k in range(K):
                    mm = pe.matmul(banks[0:NE, (X, Y)[c] + 2, :], wg[:, k, :], xf32[:, k, :], start=k == 0,
                                   stop=k == K - 1)
                mm.then_inc(gT_ready.sem, 1)

            def gate_rows(b, c):
                pe.wait_ge(gT_copied.sem, gT_copied.at(b, c + 1))
                if c == 0:
                    pe.wait_ge(x2_done.sem, x2_done.at(b, T))
                else:
                    pe.wait_ge(choose.sem, choose.at(b, 1))
                pe.sem_inc(taken["pe"], 1)
                for q in range(TH):
                    mm = pe.transpose(banks[:, Y + 3, NE * q:NE * q + NE], gT[:, c, P * q:P * q + P],
                                      ident[0:NE, 0:NE])
                mm.then_inc(gate_ready.sem, 1)

            def weight_columns(b, c):
                pe.wait_ge(choose.sem, choose.at(b, STEPS * (c + 1)))
                pe.transpose(banks[0:TH * NE, (X + 2, Y)[c], 0:P],
                             cw[:, c, :, :].rearrange("p e t -> p (e t)"), ident[:, :])\
                    .then_inc(cwT_ready.sem, 1)

            def experts_up(b, c, experts):
                staged.wait(pe, W1)
                pe.wait_ge(consts, 16 * (len(cols) + 1))
                for e in experts:
                    n = NE * c + e
                    if e == 0:
                        pe.wait_ge(xf_lo.sem, xf_lo.at(b, K * (c + 1)))
                    if e == 2 and c == 0:
                        pe.wait_ge(cwT_copied.sem, cwT_copied.at(b, 1))
                    if e >= 4:
                        pe.wait_ge(up_done.sem, up_done.at(b, n - 3))
                    elif c > 0:
                        pe.wait_ge(y_done.sem, y_done.at(b, e + 1))
                    for k in range(K):
                        mm = three_products(pe, banks[:, X + e % 4, :], [w[:, k, EH * e:EH * e + EH] for w in w1],
                                            [m[:, k, :] for m in xfT], k == 0, k == K - 1)
                    mm.then_inc(up_ready.sem, 1)

            def experts_down(b, c):
                staged.wait(pe, W2)
                for t in range(TH * c, TH * c + TH):
                    q = t % TH
                    if c == 0:
                        pe.wait_ge(up_done.sem, up_done.at(b, NE - TH + q + 1))
                    elif q == 0:
                        pe.wait_ge(xf_done.sem, xf_done.at(b, K * C))
                        pe.wait_ge(gT_copied.sem, gT_copied.at(b, C))
                        pe.wait_ge(cwT_copied.sem, cwT_copied.at(b, C))
                    for e in range(NE):
                        if q == 0:
                            pe.wait_ge(up_lo.sem, up_lo.at(b, NE * c + e + 1))
                        mm = three_products(pe, banks[:, (X, Y)[c] + q, 0:D],
                                            [h[:, e, P * q:P * q + P] for h in hidden],
                                            [w[:, e, :] for w in w2], e == 0, e == NE - 1)
                    mm.then_inc(down_ready.sem, 1)

            with pe.Fori(0, B) as b:
                for n in range(2 * K):
                    c, k = divmod(n, K)
                    if n == 0:
                        pe.wait_ge(up_done.sem, up_done.at(b, 0))
                    pe.wait_ge(a_normed.sem, a_normed.at(b, TH * c + TH))
                    for q in range(TH):
                        mm = pe.transpose(banks[:, X + n, P * q:P * q + P],
                                          v[:, TH * c + q, P * k:P * k + P], ident[:, :])
                    mm.then_inc(xT_ready.sem, 1)
                staged.wait(pe, WQK)
                for n in range(NQ):
                    m, which, c = n // (2 * C), n // C % 2, n % C
                    if n == 0:
                        pe.wait_ge(y_done.sem, y_done.at(b, 0))
                    if n < C:
                        pe.wait_ge(f_lo.sem, f_lo.at(b, K * (n + 1)))
                    if n >= 4:
                        pe.wait_ge(rest_done.sem, rest_done.at(b, n - 3))
                    for k in range(K):
                        first = D * which + P * m
                        mm = three_products(pe, banks[:, Y + n % 4, :], [w[:, k, first:first + P] for w in wqk],
                                            [x[:, k, HALF * c:HALF * c + HALF] for x in xT], k == 0, k == K - 1)
                    mm.then_inc(qk_ready.sem, 1)
                for t in range(T):
                    staged.wait(pe, WV)
                    n, u = divmod(t, 2)
                    if u == 0:
                        pe.wait_ge(rest_done.sem, rest_done.at(b, NQ - 4 + n + 1))
                    for k in range(K):
                        mm = three_products(pe, banks[:, Y + n, D * u:D * u + D],
                                            [w[:, k, P * t:P * t + P] for w in xT], [m[:, k, :] for m in wv],
                                            k == 0, k == K - 1)
                    if u == 1:
                        mm.then_inc(v_ready.sem, 1)
                for q in range(T):
                    max_tile(b, 0, 0, q, q + 1)
                transpose_maxima(b, 0, 0, T + 1, T)
                for q in range(T):
                    max_tile(b, 0, 1, q, T + 1 + q + 1)
                pe.wait_ge(prepared, 5)
                pe.wait_ge(v_copied.sem, v_copied.at(b, T // 2))
                pe.sem_inc(taken["pe"], 1)
                with pe.Fori(0, NH // HPI - 1) as i:
                    heads(b, i, False)
                heads(b, NH // HPI - 1, True)
                pe.wait_ge(max_read.sem, max_read.at(b, NMT))
                pe.wait_ge(exp_done.sem, exp_done.at(b, NH * NST))
                pe.wait_ge(o_copied.sem, o_copied.at(b, NH))
                project_attention(b, 0)
                project_attention(b, 1)
                expert_input(b, 0)
                gates(b, 0)
                gate_rows(b, 0)
                expert_input(b, 1)
                experts_up(b, 0, (0,))
                weight_columns(b, 0)
                gates(b, 1)
                experts_up(b, 0, (1,))
                gate_rows(b, 1)
                experts_up(b, 0, (2,))
                weight_columns(b, 1)
                experts_up(b, 0, range(3, NE))
                experts_down(b, 0)
                experts_up(b, 1, range(NE))
                experts_down(b, 1)


def build(nc, a, out):
    x = a["x"]
    x1 = nc.dram_tensor("x1_rows", [B, S, D], F32).ap()
    with ExitStack() as ctx:
        ident = ctx.enter_context(nc.sbuf_tensor("ident", [P, P], F32))
        mhalf = ctx.enter_context(nc.sbuf_tensor("minus_half", [P, 2 * T], F32))

        def rows(w):
            return w.rearrange("(k p) n -> p k n", p=P)

        with nc.cleanup_on_exit():
            cosine_block(nc, ident, mhalf, x, x1, {n: rows(a[n]) for n in ("WqkT", "WvT", "W1T", "W2T", "W3T")},
                         (a["bq"], a["bk"]), a["bv"], a["b1"], a["b2"], a["b3"])
        weights = {n: rows(a[n]) for n in ("Uqk", "Uv", "Uo", "Ug", "U1", "U2")}
        expert_block(nc, ident, mhalf, x1, out, weights, {n: a[f"f{n}"] for n in ("g1", "b1", "g2", "b2")})


def layout(inputs):
    import numpy as np

    a = {n.removeprefix("L0_attn_"): np.asarray(v) for n, v in inputs.items() if n.startswith("L0_attn_")}
    f = {n.removeprefix("L0_ffn_"): np.asarray(v) for n, v in inputs.items() if n.startswith("L0_ffn_")}
    arrays = {"x": a["x"], "WqkT": np.concatenate([a["Wq"].T, a["Wk"].T], axis=1)}
    arrays |= {f"W{n}T": a[f"W{n}"].T for n in "v123"}
    arrays |= {n: a[n].reshape(1, -1) for n in ("bq", "bk", "bv", "b3")}
    arrays |= {n: a[n].reshape(-1, P).T for n in ("b1", "b2")}
    arrays |= {"Uqk": np.concatenate([f["Wq"], f["Wk"]], axis=1), "Uv": f["Wv"], "Uo": f["Wo"], "Ug": f["Wg"]}
    arrays |= {"U1": f["W1"].transpose(1, 0, 2).reshape(D, -1), "U2": f["W2"].reshape(-1, D)}
    arrays |= {f"f{n}": f[n].reshape(-1, P).T for n in ("g1", "b1", "g2", "b2")}
    return {n: np.ascontiguousarray(v) for n, v in arrays.items()}


def kernel(**inputs):
    import concourse.bacc as bacc
    from concourse.bass_utils import run_bass_kernel_spmd

    nc = bacc.Bacc("TRN2", target_bir_lowering=False, num_devices=1)
    arrays = layout(inputs)
    aps = {n: nc.dram_tensor(f"in_{n}", v.shape, F32, kind="ExternalInput").ap() for n, v in arrays.items()}
    out = nc.dram_tensor("out", [B, S, D], F32, kind="ExternalOutput").ap()
    build(nc, aps, out)
    run = run_bass_kernel_spmd(nc, [{f"in_{n}": v for n, v in arrays.items()}], core_ids=[0])
    return run.results[0]["out"]
```
